# Optimizing a Trainium2 kernel written in Bass

```python
import numpy as np
import jax
import jax.numpy as jnp

def _softmax(x, axis=-1):
    return jax.nn.softmax(x, axis=axis)

def _gelu(x):
    return jax.nn.gelu(x, approximate=True)

def _silu(x):
    return jax.nn.silu(x)

def _sigmoid(x):
    return jax.nn.sigmoid(x)

def _layernorm(x, axis=-1, eps=1e-05):
    m = jnp.mean(x, axis=axis, keepdims=True)
    v = jnp.var(x, axis=axis, keepdims=True)
    return (x - m) / jnp.sqrt(v + eps)

def _scatter_add(tgt, idx, src, axis=0):
    return tgt.at[idx].add(src)

def _segment_sum(src, seg, n):
    return jax.ops.segment_sum(src, seg, n)
kernel_name = 'mk_flamingo_gated_d1_seqx_r2_5986d2'

def setup_inputs(seed: int=0):
    np.random.seed(seed)
    _w = jnp.asarray

    def _rec_inputs():
        import jax
        import jax.numpy as jnp
        _rk = jax.random.key(seed)
        x = -0.0002928 + 1 * jax.random.normal(jax.random.fold_in(_rk, 1), (4, 1024, 512), jnp.float32)
        _lenS = 1024 - jax.random.randint(jax.random.fold_in(_rk, 7), (4,), 0, max(1, 1024 // 4) + 1, jnp.int32)
        _lenS2 = 1024 - jax.random.randint(jax.random.fold_in(_rk, 8), (4,), 0, max(1, 1024 // 4) + 1, jnp.int32)
        _ctx_1024P = jax.random.normal(jax.random.fold_in(_rk, 11), (4, 16, 512), jnp.float32)
        _ctx_1024c = jax.random.dirichlet(jax.random.fold_in(_rk, 511), 0.3 * jnp.ones((16,), jnp.float32), (4, 1024))
        _ctx_1024t = jnp.einsum('bsk,bkd->bsd', _ctx_1024c, _ctx_1024P)
        _ctx_1024t = _ctx_1024t * jax.lax.rsqrt(jnp.mean(jnp.square(_ctx_1024t)) + 1e-12) * 0.953939
        ctx_1024 = 2.81802e-05 + 1.00001 * (_ctx_1024t + 0.3 * jax.random.normal(jax.random.fold_in(_rk, 611), (4, 1024, 512), jnp.float32))
        _validS = jnp.arange(1024)[None, :] < _lenS[:, None]
        _validS2 = jnp.arange(1024)[None, :] < _lenS2[:, None]
        _causal = jnp.tril(jnp.ones((1024, 1024), dtype=bool))
        mask_BxS2_bk0 = jnp.logical_not(jnp.broadcast_to(_validS2[:, :], (4, 1024)))
        _g = jax.random.normal(jax.random.fold_in(_rk, 9001), (2, 1), jnp.float32)
        _g = jnp.sign(_g) * jnp.maximum(jnp.abs(_g), 1.0) + (_g == 0) * 1.0
        g_xattn = _g[0]
        g_ffn = _g[1]
        return (x, ctx_1024, mask_BxS2_bk0, g_xattn, g_ffn)
    x, ctx_1024, mask_BxS2_bk0, g_xattn, g_ffn = _rec_inputs()

    def _L0_xattn_setup():
        import jax, jax.numpy as jnp
        import numpy as np
        NUM_HEADS, NUM_KV, HEAD_DIM, WIDTH = (4, 1, 128, 512)
        MASK_FILL = -2.3819763e+38

        def _apply_rope(x, positions, max_wavelength=10000.0):
            d = x.shape[-1]
            freq_exp = 2.0 / d * jnp.arange(d // 2, dtype=jnp.float32)
            timescale = max_wavelength ** freq_exp
            radians = positions[..., None].astype(jnp.float32) / timescale
            radians = radians[..., None, :]
            sin, cos = (jnp.sin(radians), jnp.cos(radians))
            x1, x2 = jnp.split(x, 2, axis=-1)
            out = jnp.concatenate([x1 * cos - x2 * sin, x2 * cos + x1 * sin], axis=-1)
            return out.astype(x.dtype)

        def _rmsnorm(x, scale):
            var = jnp.mean(jnp.square(x.astype(jnp.float32)), axis=-1, keepdims=True)
            normed = x * jax.lax.rsqrt(var + 1e-06)
            return (normed * (1 + scale)).astype(x.dtype)
        key = jax.random.key(seed)
        ks = jax.random.split(key, 7)
        B, T, S = (8, 256, 1024)
        return {'x': jax.random.normal(ks[0], (B, T, WIDTH), jnp.float32), 'mem_seq': jax.random.normal(ks[1], (B, S, WIDTH), jnp.float32), 'mem_mask': jax.random.randint(ks[2], (B, S), 0, 2).astype(bool), 'rms_scale': jax.random.normal(ks[3], (WIDTH,), jnp.float32) * 0.02, 'q_w': jax.random.normal(ks[4], (NUM_HEADS, WIDTH, HEAD_DIM), jnp.float32) / np.sqrt(WIDTH), 'kv_w': jax.random.normal(ks[5], (2, NUM_KV, WIDTH, HEAD_DIM), jnp.float32) / np.sqrt(WIDTH), 'out_w': jax.random.normal(ks[6], (NUM_HEADS, HEAD_DIM, WIDTH), jnp.float32) / np.sqrt(NUM_HEADS * HEAD_DIM)}
    _L0_xattn_all = _L0_xattn_setup()
    _L0_xattn_in = {k: v for k, v in _L0_xattn_all.items() if k in ('rms_scale', 'q_w', 'kv_w', 'out_w')}
    del _L0_xattn_all

    def _L0_ffn_setup():
        import jax, jax.numpy as jnp
        import numpy as np
        B, L, H = (32, 256, 512)
        E, R, TOP_K = (8, 16, 2)

        def _gates(cls, router_w):
            logits = jnp.einsum('bh,eh->be', cls, router_w)
            top_vals, top_idx = jax.lax.top_k(logits, TOP_K)
            mask = jnp.full_like(logits, -jnp.inf)
            rows = jnp.arange(logits.shape[0])[:, None]
            mask = mask.at[rows, top_idx].set(top_vals)
            return jax.nn.softmax(mask, axis=1)
        key = jax.random.key(seed)
        k1, k2, k3, k4 = jax.random.split(key, 4)
        x = jax.random.normal(k1, (B, L, H), dtype=jnp.float32)
        router_w = jax.random.normal(k2, (E, H), dtype=jnp.float32) * 0.02
        lora_down = jax.random.normal(k3, (E, R, H), dtype=jnp.float32) * (1.0 / np.sqrt(H))
        lora_up = jax.random.normal(k4, (E, H, R), dtype=jnp.float32) * (1.0 / np.sqrt(R))
        return {'x': x, 'router_w': router_w, 'lora_down': lora_down, 'lora_up': lora_up}
    _L0_ffn_all = _L0_ffn_setup()
    _L0_ffn_in = {k: v for k, v in _L0_ffn_all.items() if k in ('router_w', 'lora_down', 'lora_up')}
    del _L0_ffn_all
    return {'x': x, 'ctx_1024': ctx_1024, 'mask_BxS2_bk0': mask_BxS2_bk0, 'g_xattn': g_xattn, 'g_ffn': g_ffn, 'L0_xattn_rms_scale': _L0_xattn_in['rms_scale'], 'L0_xattn_q_w': _L0_xattn_in['q_w'], 'L0_xattn_kv_w': _L0_xattn_in['kv_w'], 'L0_xattn_out_w': _L0_xattn_in['out_w'], 'L0_ffn_router_w': _L0_ffn_in['router_w'], 'L0_ffn_lora_down': _L0_ffn_in['lora_down'], 'L0_ffn_lora_up': _L0_ffn_in['lora_up']}

def reference(x, ctx_1024, mask_BxS2_bk0, g_xattn, g_ffn, L0_xattn_rms_scale, L0_xattn_q_w, L0_xattn_kv_w, L0_xattn_out_w, L0_ffn_router_w, L0_ffn_lora_down, L0_ffn_lora_up):
    import jax
    import jax.numpy as jnp

    def _L0_xattn_ref(x, mem_seq, mem_mask, rms_scale, q_w, kv_w, out_w):
        import jax, jax.numpy as jnp
        import numpy as np
        NUM_HEADS, NUM_KV, HEAD_DIM, WIDTH = (4, 1, 128, 512)
        MASK_FILL = -2.3819763e+38

        def _apply_rope(x, positions, max_wavelength=10000.0):
            d = x.shape[-1]
            freq_exp = 2.0 / d * jnp.arange(d // 2, dtype=jnp.float32)
            timescale = max_wavelength ** freq_exp
            radians = positions[..., None].astype(jnp.float32) / timescale
            radians = radians[..., None, :]
            sin, cos = (jnp.sin(radians), jnp.cos(radians))
            x1, x2 = jnp.split(x, 2, axis=-1)
            out = jnp.concatenate([x1 * cos - x2 * sin, x2 * cos + x1 * sin], axis=-1)
            return out.astype(x.dtype)

        def _rmsnorm(x, scale):
            var = jnp.mean(jnp.square(x.astype(jnp.float32)), axis=-1, keepdims=True)
            normed = x * jax.lax.rsqrt(var + 1e-06)
            return (normed * (1 + scale)).astype(x.dtype)
        B, S, _ = mem_seq.shape
        T = x.shape[1]
        G = NUM_HEADS // NUM_KV
        xn = _rmsnorm(x, rms_scale)
        mn = _rmsnorm(mem_seq, rms_scale)
        q = jnp.einsum('BTD,NDH->BTNH', xn, q_w)
        kv = jnp.einsum('BSD,cKDH->cBSKH', mn, kv_w)
        k, v = (kv[0], kv[1])
        q_pos = jnp.broadcast_to(jnp.arange(S, T + S), (B, T))
        k_pos = jnp.broadcast_to(jnp.arange(S), (B, S))
        q = _apply_rope(q, q_pos) * HEAD_DIM ** (-0.5)
        k = _apply_rope(k, k_pos)
        q = q.reshape(B, T, NUM_KV, G, HEAD_DIM)
        logits = jnp.einsum('BTKGH,BSKH->BKGTS', q, k, preferred_element_type=jnp.float32)
        masked = jnp.where(mem_mask[:, None, None, None, :], logits, MASK_FILL)
        probs = jax.nn.softmax(masked, axis=-1).astype(x.dtype)
        enc = jnp.einsum('BKGTS,BSKH->BTKGH', probs, v).reshape(B, T, NUM_HEADS, HEAD_DIM)
        return jnp.einsum('BTNH,NHD->BTD', enc, out_w)

    def _L0_ffn_ref(x, router_w, lora_down, lora_up):
        import jax, jax.numpy as jnp
        import numpy as np
        B, L, H = (32, 256, 512)
        E, R, TOP_K = (8, 16, 2)

        def _gates(cls, router_w):
            logits = jnp.einsum('bh,eh->be', cls, router_w)
            top_vals, top_idx = jax.lax.top_k(logits, TOP_K)
            mask = jnp.full_like(logits, -jnp.inf)
            rows = jnp.arange(logits.shape[0])[:, None]
            mask = mask.at[rows, top_idx].set(top_vals)
            return jax.nn.softmax(mask, axis=1)
        gates = _gates(x[:, 0, :], router_w)
        down = jnp.einsum('blh,erh->bler', x, lora_down)
        weighted = jnp.einsum('bler,ehr,be->blh', down, lora_up, gates)
        return x + weighted
    x = x + jnp.tanh(g_xattn[0]) * _L0_xattn_ref(_layernorm(x, axis=-1), ctx_1024, mask_BxS2_bk0, L0_xattn_rms_scale, L0_xattn_q_w, L0_xattn_kv_w, L0_xattn_out_w)
    x = x + jnp.tanh(g_ffn[0]) * _L0_ffn_ref(_layernorm(x, axis=-1), L0_ffn_router_w, L0_ffn_lora_down, L0_ffn_lora_up)
    return x

_drawn_inputs = setup_inputs


def setup_inputs(seed=0):
    import zlib

    import numpy as np

    out = dict(_drawn_inputs(seed))
    spreads = {}
    factors = {'L0_xattn_rms_scale': 7.249}
    for name, (base, spread) in spreads.items():
        noise = np.random.default_rng([zlib.crc32(name.encode()), seed]).standard_normal(out[name].shape)
        drawn = base * np.exp(spread * noise) if base else spread * noise
        out[name] = jnp.asarray(drawn.astype(out[name].dtype))
    for name, factor in factors.items():
        out[name] = (out[name] * factor).astype(out[name].dtype)
    return out
```

```python
from contextlib import ExitStack

import numpy as np

import concourse.bass as bass
from concourse import mybir

F32 = mybir.dt.float32
F32R = mybir.dt.float32r
U8 = mybir.dt.uint8
I32 = mybir.dt.int32
ALU = mybir.AluOpType
ACT = mybir.ActivationFunctionType
AX = mybir.AxisListType

P = 128
B, S, D = 4, 1024, 512
NH, HD = 4, 128
E, R, TOPK = 8, 16, 2
ER = E * R
KC = D // P
CH = 512
NC = S // CH
T = CH // P
GK = 256
NG = S // GK
FILL = 2.3819763e38
LN_EPS = 1e-5
RMS_EPS = 1e-6


def rope_tables():
    half = HD // 2
    freq = np.float32(2.0 / HD) * np.arange(half, dtype=np.float32)
    timescale = (np.float32(10000.0) ** freq).astype(np.float32)
    pos = np.arange(2 * S, dtype=np.float32)
    rad = (pos[None, :] / timescale[:, None]).astype(np.float32)
    cos = np.cos(rad).astype(np.float32)
    sin = np.sin(rad).astype(np.float32)
    cos = np.concatenate([cos, cos], 0)
    sin = np.concatenate([-sin, sin], 0)
    scale = np.float32(-float(HD) ** -0.5)
    keys = np.stack([cos[:, :S], sin[:, :S]], 1)
    queries = np.stack([cos[:, S:] * scale, sin[:, S:] * scale], 1)
    return np.ascontiguousarray(queries), np.ascontiguousarray(keys)


def gated_block(nc, x, ctx_in, mask, g_xattn, g_ffn, rms_scale, q_w, kv_w, out_w, router_w,
                lora_down, lora_up, q_table, k_table, out):
    stack = ExitStack()
    with stack:
        def sb(name, shape, dt=F32):
            return stack.enter_context(nc.sbuf_tensor(name, shape, dt))

        def sem(name):
            return stack.enter_context(nc.semaphore(name))

        wq = [sb(f"wq_{p}", [P, KC, NH * HD], F32R) for p in "hl"]
        wkv = [sb(f"wkv_{p}", [P, 2, KC, HD], F32R) for p in "hl"]
        wo = [sb(f"wo_{p}", [P, NH, D], F32R) for p in "hl"]
        wdn = [sb(f"wdn_{p}", [P, KC, ER], F32R) for p in "hl"]
        wup = [sb(f"wup_{p}", [P, D], F32R) for p in "hl"]
        wrt = [sb(f"wrt_{p}", [P, KC, E], F32R) for p in "hl"]
        qtab = sb("qtab", [P, 2, S])
        ktab = sb("ktab", [P, 2, CH])
        ident = sb("ident", [P, P])
        own = sb("own", [P, E])
        lower = sb("lower", [P, E, E])
        neg_half = sb("neg_half", [P, T])
        gates_in = sb("gates_in", [P, 2])
        t12 = sb("t12", [P, 2])
        rms1 = sb("rms1", [P, KC])
        xb = [sb(f"x_{i}", [P, T, D]) for i in range(NC)]
        norm = sb("norm", [P, T, D])
        xT = [sb(f"xT_{p}", [P, KC, CH], F32R) for p in "hl"]
        qT = [sb(f"qT_{p}", [P, NH, CH], F32R) for p in "hl"]
        kT = [sb(f"kT_{p}", [P, S], F32R) for p in "hl"]
        v = [sb(f"v_{p}", [P, S // P, HD], F32R) for p in "hl"]
        q_swap = sb("q_swap", [P, CH])
        q_sin = sb("q_sin", [P, CH])
        q_rot = sb("q_rot", [P, CH])
        probs = sb("probs", [P, 4 * S])
        pT = [sb(f"pT_{p}", [P, 4, CH], F32R) for p in "hl"]
        eT = [sb(f"eT_{p}", [P, KC, CH], F32R) for p in "hl"]
        dT = [sb(f"dT_{p}", [P, CH], F32R) for p in "hl"]
        x2 = sb("x2", [P, T, D])
        bias = sb("bias", [P, S])
        mask_u8 = sb("mask_u8", [P, S], U8)
        st6 = sb("st6", [P, 3, T, 6])
        mv1 = sb("mv1", [P, T, 2])
        var1 = sb("var1", [P, T])
        rs1 = sb("rs1", [P, T])
        nm1 = sb("nm1", [P, T])
        mv2 = sb("mv2", [P, T, 2])
        small2 = sb("small2", [P, T, 5])
        mvc = sb("mvc", [P, 8, 2])
        smallc = sb("smallc", [P, 8, 3])
        lmin = sb("lmin", [P, NH * T])
        lsum = sb("lsum", [P, NH * T])
        lrec = sb("lrec", [P, NH * T])
        rt = sb("rt", [P, 16, E])
        cmp = sb("cmp", [P, 3, E, E])
        gate = sb("gate", [P, 1])
        flag_f = sb("flag_f", [1, 3 * B * NG])
        flags = sb("flags", [1, 2 * B], I32)

        bank = [stack.enter_context(nc.psum_tensor(f"bank{i}", [P, 512], F32)) for i in range(3)]
        lg = stack.enter_context(nc.psum_tensor("lg", [P, 1024], F32))
        tp = [stack.enter_context(nc.psum_tensor(f"tp{i}", [P, 512], F32)) for i in range(2)]
        enc = stack.enter_context(nc.psum_tensor("enc", [P, 512], F32))
        tbank, qbank = bank[0:2], bank[2]

        raw_q = probs[:, 0:2048].rearrange("p (h k n) -> p h k n", h=NH, k=KC)
        raw_o = norm[:, :, :]
        raw_kv = x2[:, 0:2, :].rearrange("p c (k n) -> p c k n", k=KC)
        raw_dn = x2[:, 2, :]
        raw_up = x2[:, 3, :].rearrange("p (k n) -> p k n", k=KC)
        raw_router = q_swap[0:E, :]
        raw_rms = q_sin[0:KC, 0:P]
        ctxT = [p.rearrange("p s n -> p (s n)") for p in (pT[0][:, :, :], pT[1][:, :, :])]

        def ctx_part(p, path):
            n = path.bt * P
            return ctxT[p][:, 0:KC * n].rearrange("p (k n) -> p k n", k=KC)

        ctx_raw = probs[:, 2048:4096].rearrange("p (t d) -> p t d", t=4)
        mask_row = bias[0:1, :].bitcast(U8)

        names = """passed g_in raw_w raw_kv_in raw_dn_in raw_up_in raw_aux_in tab_in mask_in ident_ok const_ok tanh_ok
            aux_full rms_ok rt_ok dn_w_full dn_w_hi dn_w_ok up_w_full up_w_hi up_w_ok wq_hi wq_ok wo_hi wo_ok
            wkv_hi wkv_ok flags_ok flag_step const_step
            x_in0 x_in1 ln1_bn ln1_stats ln1_scales xn_ready tx_full tx_hi tx_done ty_full ty_hi ty_done
            q_full q_swapped q_sin_ok q_cos_ok q_sum q_hi q_done
            lg_full lg_min ex_done rec_done nrm_done tp_full tp_hi tp_done pv_full pv_hi pv_done
            op_full res_done ln2_bn ln2_stats ln2_var ln2_scales y_ready aff_ready up_full fin_done stored
            rt_full rt_read rt_neg gate_step rt_exp gate_ok dn_full dn_hi dn_done
            ctx_in_s ktab_in mask_b_in bias_ok ctx_bn ctx_stats ctx_rms ctx_inv ctx_normed tc_full tc_hi tc_done
            k_full k_swapped k_sin k_cos k_sum k_hi k_done v_full v_hi v_done"""
        s = {n: sem("s_" + n) for n in names.split()}
        block = stack.enter_context(nc.Block())

        def rotation(h):
            proj = (qbank[:, :], qbank[:, :], lg[:, 0:512], lg[:, 512:1024])[h]
            if h == 2:
                return proj, probs[:, 0:512], probs[:, 1024:1536], probs[:, 1536:2048]
            return proj, q_swap[:, :], q_sin[:, :], q_rot[:, :]

        def hold(eng, name, value):
            eng.wait_ge(s[name], value)
            eng.sem_inc(s["passed"], 1)

        def load_flags(eng, b):
            long_path = eng.value_load(flags[0:1, bass.ds(2 * b, 1)], min_val=0, max_val=1)
            group = eng.value_load(flags[0:1, bass.ds(2 * b + 1, 1)], min_val=0, max_val=NG - 1)
            return long_path, group

        def either(eng, long_path, body):
            with eng.If(long_path == 0):
                body(SHORT)
            with eng.Else():
                body(LONG)

        class SHORT:
            nk = GK // P
            unit = 4
            blocks = 1
            bt = GK // P
            ahead = True

        class LONG:
            nk = S // P
            unit = 1
            blocks = 2
            bt = 4
            ahead = False

        def pipeline(eng, step):
            step(0, 0, first=True)
            with eng.Fori(0, B - 1) as b:
                step(b, 1)
                step(b + 1, 0)
            step(B - 1, 1, last=True)

        @block.sync
        def _(sp):
            def rows(t, b, cc):
                start = (b * NC + cc) * T
                return t.rearrange("(c p) d -> p c d", p=P)[:, bass.ds(start, T), :]

            x_rows = x.rearrange("b s d -> (b s) d")
            out_rows = out.rearrange("b s d -> (b s) d")
            x_in = [s["x_in0"], s["x_in1"]]

            def load_x(b, cc):
                sp.dma_start(xb[cc][:, :, :], rows(x_rows, b, cc)).then_inc(x_in[cc], 16)

            def load_ctx(b, long_path, group):
                def body(path):
                    n = path.nk * P
                    first = group * GK if path is SHORT else 0
                    sp.dma_start(mask_u8[:, 0:n], mask[bass.ds(b, 1), bass.ds(first, n)].to_broadcast([P, n]))\
                        .then_inc(s["mask_b_in"], 16)
                    n = path.bt * P
                    for k in range(path.blocks):
                        first = group * GK if path is SHORT else k * n
                        if k:
                            sp.wait_ge(s["tc_full"], b * 8 + 4)
                            sp.wait_ge(s["k_sum"], b * 2 + 1)
                        sp.dma_start(ctx_raw[:, 0:path.bt, :],
                                     ctx_in[bass.ds(b, 1), bass.ds(first, n), :]
                                     .rearrange("o (t p) d -> p (o t) d", p=P)).then_inc(s["ctx_in_s"], 16 * (2 // path.blocks))
                        sp.dma_start(ktab[:, :, 0:n], k_table[:, :, bass.ds(first, n)]).then_inc(s["ktab_in"], 16 * (2 // path.blocks))
                either(sp, long_path, body)

            sp.dma_start(mask_row, mask.rearrange("b s -> (b s)").rearrange("(o n) -> o n", o=1)).then_inc(s["mask_in"], 16)
            load_x(0, 0)
            sp.dma_start(raw_router, router_w).then_inc(s["raw_aux_in"], 16)
            sp.dma_start(raw_rms, rms_scale.rearrange("(k p) -> k p", p=P)).then_inc(s["raw_aux_in"], 16)
            sp.dma_start(raw_q.rearrange("p h k n -> p (h k) n"),
                         q_w.rearrange("h (k p) n -> p (h k) n", p=P)).then_inc(s["raw_w"], 16)
            sp.dma_start(raw_kv.rearrange("p c k n -> p (c k) n"),
                         kv_w.rearrange("c o (k p) n -> p (c o k) n", p=P)).then_inc(s["raw_kv_in"], 16)
            sp.dma_start(qtab[:, :, :], q_table).then_inc(s["tab_in"], 16)
            sp.wait_ge(s["flags_ok"], 1)
            lp, g = load_flags(sp, 0)
            load_ctx(0, lp, g)
            load_x(0, 1)
            sp.dma_start(raw_dn, lora_down.rearrange("e r d -> (e r) d")).then_inc(s["raw_dn_in"], 16)
            for k in range(KC):
                sp.dma_start(raw_up[:, k, :].rearrange("p (e r) -> p e r", e=E),
                             lora_up[:, k * P:(k + 1) * P, :].rearrange("e p r -> p e r")).then_inc(s["raw_up_in"], 16)
            sp.wait_ge(s["tx_full"], T)
            sp.dma_start(raw_o, out_w.rearrange("h p n -> p h n")).then_inc(s["raw_w"], 16)

            def store(c):
                sp.wait_ge(s["fin_done"], (c + 1) * T + T)
                sp.dma_start(out_rows.rearrange("(c p) d -> p c d", p=P)[:, bass.ds(c * T, T), :], x2[:, :, :])\
                    .then_inc(s["stored"], 16)

            def step(b, cc, first=False, last=False):
                c = b * NC + cc
                if not (first or last):
                    sp.wait_ge(s["res_done"], c * T)
                    load_x(b + cc, 1 - cc)
                if not first:
                    store(c - 1)
                if cc == NC - 1 and not last:
                    lp_now, _ = load_flags(sp, b)
                    lp_next, g_next = load_flags(sp, b + 1)
                    hold(sp, "k_done", (b + 1) * 2)
                    with sp.If(lp_now == 0):
                        hold(sp, "bias_ok", b + 1)
                    with sp.Else():
                        hold(sp, "tp_full", (c + 1) * NH * 8)
                    load_ctx(b + 1, lp_next, g_next)

            pipeline(sp, step)
            store(B * NC - 1)
            sp.wait_ge(s["stored"], 16 * B * NC)

        @block.gpsimd
        def _(pool):
            pool.dma_start(gates_in[:, 0:1], g_xattn.rearrange("(o n) -> o n", o=1).to_broadcast([P, 1])).then_inc(s["g_in"], 16)
            pool.dma_start(gates_in[:, 1:2], g_ffn.rearrange("(o n) -> o n", o=1).to_broadcast([P, 1])).then_inc(s["g_in"], 16)
            pool.memset(ident[:, :], 0.0).then_inc(s["const_step"], 1)
            pool.memset(neg_half[:, :], -0.5).then_inc(s["const_step"], 1)
            pool.memset(own[:, :], 1.0).then_inc(s["const_step"], 1)
            pool.memset(lower[:, :, :], 1.0).then_inc(s["const_step"], 1)
            pool.wait_ge(s["const_step"], 4)
            pool.affine_select(out=ident[:, :], in_=ident[:, :], compare_op=ALU.not_equal, fill=1.0, base=0,
                               pattern=[[-1, P]], channel_multiplier=1).then_inc(s["ident_ok"], 1)
            pool.affine_select(out=own[:, :], in_=own[:, :], compare_op=ALU.is_ge, fill=0.0, base=0,
                               pattern=[[-R, E]], channel_multiplier=1).then_inc(s["const_step"], 1)
            pool.wait_ge(s["const_step"], 5)
            pool.affine_select(out=own[:, :], in_=own[:, :], compare_op=ALU.is_ge, fill=0.0, base=R - 1,
                               pattern=[[R, E]], channel_multiplier=-1).then_inc(s["const_step"], 1)
            pool.affine_select(out=lower[:, :, :], in_=lower[:, :, :], compare_op=ALU.is_ge, fill=0.0, base=-1,
                               pattern=[[1, E], [-1, E]], channel_multiplier=0).then_inc(s["const_step"], 1)
            pool.wait_ge(s["const_step"], 7)
            pool.drain().then_inc(s["const_ok"], 1)
            def ln1(c):
                hold(pool, "ln1_stats", (c + 1) * T)
                pool.tensor_scalar(var1[:, :], mv1[:, :, 1], 1.0 + RMS_EPS, LN_EPS * RMS_EPS, ALU.mult, ALU.add)\
                    .then_inc(s["ln1_scales"], 1)
                pool.tensor_scalar(nm1[:, :], mv1[:, :, 0], -1.0, 0.0, ALU.mult, ALU.add).then_inc(s["ln1_scales"], 1)
                pool.wait_ge(s["ln1_scales"], c * 3 + 2)
                pool.tensor_tensor(rs1[:, :], var1[:, :], neg_half[:, :], ALU.pow).then_inc(s["ln1_scales"], 1)

            def xn(c, cc):
                hold(pool, "ln1_scales", c * 3 + 3)
                for t in range(T):
                    pool.tensor_scalar(norm[:, t, :], xb[cc][:, t, :], nm1[:, t:t + 1], rs1[:, t:t + 1],
                                       ALU.add, ALU.mult).then_inc(s["xn_ready"], 1)

            def ctx_norm(b, path, k):
                w = 2 // path.blocks
                t0 = k * path.bt
                at = b * 6 + k * 3
                m, var = mvc[:, t0:t0 + path.bt, 0], mvc[:, t0:t0 + path.bt, 1]
                square, total, inv = (smallc[:, t0:t0 + path.bt, i] for i in range(3))
                pool.wait_ge(s["ctx_stats"], b * 8 + (t0 + path.bt) * path.unit)
                pool.tensor_tensor(square, m, m, ALU.mult).then_inc(s["ctx_rms"], w)
                pool.wait_ge(s["ctx_rms"], at + w)
                pool.tensor_tensor(total, square, var, ALU.add).then_inc(s["ctx_rms"], w)
                hold(pool, "ctx_rms", at + 2 * w)
                pool.tensor_scalar(total, total, RMS_EPS, 1.0, ALU.add, ALU.mult).then_inc(s["ctx_rms"], w)
                pool.wait_ge(s["ctx_rms"], at + 3 * w)
                pool.tensor_tensor(inv, total, neg_half[:, 0:path.bt], ALU.pow).then_inc(s["ctx_inv"], w)
                hold(pool, "ctx_inv", b * 2 + (k + 1) * w)
                for j in range(path.bt):
                    pool.tensor_scalar(ctx_raw[:, j, :], ctx_raw[:, j, :], smallc[:, t0 + j, 2:3], 1.0,
                                       ALU.mult, ALU.mult).then_inc(s["ctx_normed"], path.unit)

            def k_sines(b, path, k):
                n = path.bt * P
                w = 2 // path.blocks
                pool.wait_ge(s["k_swapped"], b * 4 + (k + 1) * w * 2)
                pool.wait_ge(s["ktab_in"], 16 * (b * 2 + (k + 1) * w))
                pool.tensor_tensor(q_sin[:, 0:n], q_swap[:, 0:n], ktab[:, 1, 0:n], ALU.mult).then_inc(s["k_sin"], w)

            def q_sine(c, cc, h):
                pool.wait_ge(s["q_swapped"], (c * NH + h + 1) * 2)
                _, swapped, sines, _ = rotation(h)
                pool.tensor_tensor(sines, swapped, qtab[:, 1, cc * CH:(cc + 1) * CH], ALU.mult)\
                    .then_inc(s["q_sin_ok"], 1)

            def ln2(c, t):
                m = small2[:, t, :]
                at = (c * T + t) * 3
                hold(pool, "ln2_stats", c * T + t + 1)
                pool.tensor_scalar(m[:, 0:1], mv2[:, t, 1:2], LN_EPS, 1.0, ALU.add, ALU.mult).then_inc(s["ln2_var"], 1)
                pool.wait_ge(s["ln2_var"], at + 1)
                pool.tensor_tensor(m[:, 1:2], m[:, 0:1], neg_half[:, 0:1], ALU.pow).then_inc(s["ln2_var"], 1)
                hold(pool, "ln2_var", at + 2)
                pool.tensor_scalar(m[:, 2:3], mv2[:, t, 0:1], -1.0, m[:, 1:2], ALU.mult, ALU.mult).then_inc(s["ln2_var"], 1)
                pool.tensor_scalar(m[:, 3:4], m[:, 1:2], t12[:, 1:2], 1.0, ALU.mult, ALU.add).then_inc(s["ln2_scales"], 1)
                hold(pool, "ln2_var", at + 3)
                pool.tensor_scalar(m[:, 4:5], m[:, 2:3], t12[:, 1:2], 1.0, ALU.mult, ALU.mult).then_inc(s["ln2_scales"], 1)

            def affine(c, t):
                hold(pool, "y_ready", c * T + t + 1)
                pool.tensor_scalar(x2[:, t, :], x2[:, t, :], small2[:, t, 3:4], small2[:, t, 4:5],
                                   ALU.mult, ALU.add).then_inc(s["aff_ready"], 1)

            def prologue():
                pool.wait_ge(s["tanh_ok"], 1)
                pool.wait_ge(s["tab_in"], 16)
                ln1(0)
                xn(0, 0)
                for h in range(NH):
                    q_sine(0, 0, h)
                pool.wait_ge(s["flags_ok"], 1)
                lp, _ = load_flags(pool, 0)

                def first_keys(path):
                    for k in range(path.blocks):
                        ctx_norm(0, path, k)
                        k_sines(0, path, k)
                either(pool, lp, first_keys)

            def step(b, cc, first=False, last=False):
                c = b * NC + cc
                if not last:
                    ln1(c + 1)
                    if first:
                        pool.wait_ge(s["wo_ok"], NH)
                    else:
                        pool.wait_ge(s["ty_full"], c * T)
                    xn(c + 1, 1 - cc)
                    q_sine(c + 1, 1 - cc, 0)
                    q_sine(c + 1, 1 - cc, 1)
                if cc == NC - 1 and not last:
                    lp, _ = load_flags(pool, b + 1)
                    either(pool, lp, lambda path: outputs(c, 1 - cc, b + 1, path, last))
                else:
                    outputs(c, 1 - cc, None, None, last)

            def outputs(c, ncc, new_batch, path, last):
                if path:
                    ctx_norm(new_batch, path, 0)
                if not last:
                    q_sine(c + 1, ncc, 2)
                ln2(c, 0)
                if path:
                    k_sines(new_batch, path, 0)
                if not last:
                    q_sine(c + 1, ncc, 3)
                if path and path.blocks == 2:
                    ctx_norm(new_batch, path, 1)
                    k_sines(new_batch, path, 1)
                for t in range(1, T):
                    ln2(c, t)
                for t in range(T):
                    affine(c, t)

            prologue()
            pipeline(pool, step)

        @block.scalar
        def _(act):
            act.wait_ge(s["g_in"], 32)
            act.activation(t12[:, :], gates_in[:, :], ACT.Tanh).then_inc(s["tanh_ok"], 1)

            def hi(dst, src, wait, at, done, inc=1):
                act.wait_ge(s[wait], at)
                act.activation(dst, src, ACT.Copy).then_inc(s[done], inc)

            def tx_hi(n, tiles=range(T)):
                for t in tiles:
                    hi(xT[0][:, :, t * P:(t + 1) * P], tbank[t % 2][:, :].rearrange("p (k n) -> p k n", k=KC),
                       "tx_full", n * T + t + 1, "tx_hi")

            def ty_hi(c, tiles=range(T)):
                for t in tiles:
                    hi(xT[0][:, :, t * P:(t + 1) * P], tbank[t % 2][:, :].rearrange("p (k n) -> p k n", k=KC),
                       "ty_full", c * T + t + 1, "ty_hi")

            def q_swap_halves(n, h):
                act.wait_ge(s["q_full"], n * NH + h + 1)
                proj, swapped, _, _ = rotation(h)
                act.activation(swapped[0:64, :], proj[64:128, :], ACT.Copy).then_inc(s["q_swapped"], 1)
                act.activation(swapped[64:128, :], proj[0:64, :], ACT.Copy).then_inc(s["q_swapped"], 1)

            def q_high(n, h):
                act.wait_ge(s["q_sum"], n * NH + h + 1)
                act.activation(qT[0][:, h, :], rotation(h)[3], ACT.Copy).then_inc(s["q_hi"], 1)

            def exps(path, c, h):
                w = path.nk * P
                o = (h % 2) * 1024 if path.ahead else 0
                for qt in range(T):
                    i = h * T + qt
                    act.wait_ge(s["lg_min"], c * 16 + i + 1)
                    p = probs[:, o + qt * w:o + (qt + 1) * w]
                    act.activation(p, p, ACT.Exp, bias=lmin[:, i:i + 1], scale=-1.0,
                                   accum_out=lsum[:, i:i + 1]).then_inc(s["ex_done"], 1)

            def tp_high(path, c, h, kt):
                slot = (h % 2) * 2 + kt if path.ahead else kt % 4
                hi(pT[0][:, slot, :], tp[kt % 2][:, :], "tp_full", (c * NH + h) * 8 + (kt + 1) * path.unit, "tp_hi", path.unit)

            def pv_high(c, h):
                hi(eT[0][:, h, :], enc[:, :], "pv_full", c * NH + h + 1, "pv_hi")

            def y(c, t):
                act.wait_ge(s["ln2_scales"], (c * T + t) * 2 + 2)
                act.activation(norm[:, t, :], x2[:, t, :], ACT.Identity, bias=small2[:, t, 2:3],
                               scale=small2[:, t, 1:2]).then_inc(s["y_ready"], 1)

            def ctx_high(b, path, k):
                for j in range(path.bt):
                    kt = k * path.bt + j
                    hi(ctx_part(0, path)[:, :, j * P:(j + 1) * P], tbank[kt % 2][:, :].rearrange("p (k n) -> p k n", k=KC),
                       "tc_full", b * 8 + (kt + 1) * path.unit, "tc_hi", path.unit)

            def k_swap_halves(b, path, k):
                w = 2 // path.blocks
                n = path.bt * P
                act.wait_ge(s["k_full"], b * 2 + (k + 1) * w)
                act.activation(q_swap[0:64, 0:n], qbank[64:128, 0:n], ACT.Copy).then_inc(s["k_swapped"], w)
                act.activation(q_swap[64:128, 0:n], qbank[0:64, 0:n], ACT.Copy).then_inc(s["k_swapped"], w)

            def k_high(b, path, k):
                w = 2 // path.blocks
                n = path.bt * P
                at = b * 2 + (k + 1) * w
                act.wait_ge(s["k_sum"], at)
                act.activation(kT[0][:, k * n:(k + 1) * n], q_rot[:, 0:n], ACT.Copy).then_inc(s["k_hi"], w)

            def v_high(b, path, k):
                w = 2 // path.blocks
                n = path.bt * P
                hi(v[0][:, k * path.bt:(k + 1) * path.bt, :], enc[:, 0:n].rearrange("p (t n) -> p t n", n=HD),
                   "v_full", b * 2 + (k + 1) * w, "v_hi", w)

            def prologue():
                act.wait_ge(s["rms_ok"], 1)
                act.wait_ge(s["raw_w"], 16)
                for k in range(KC):
                    act.activation(wq[0][:, k, :].rearrange("p (h n) -> p h n", h=NH), raw_q[:, :, k, :], ACT.Copy,
                                   scale=rms1[:, k:k + 1]).then_inc(s["wq_hi"], 1)
                act.wait_ge(s["raw_kv_in"], 16)
                for k in range(KC):
                    act.activation(wkv[0][:, :, k, :], raw_kv[:, :, k, :], ACT.Copy,
                                   scale=rms1[:, k:k + 1]).then_inc(s["wkv_hi"], 1)
                tx_hi(0)
                for h in range(NH):
                    q_swap_halves(0, h)
                    q_high(0, h)
                act.wait_ge(s["flags_ok"], 1)
                lp, _ = load_flags(act, 0)

                def first_keys(path):
                    for k in range(path.blocks):
                        ctx_high(0, path, k)
                        k_swap_halves(0, path, k)
                        k_high(0, path, k)
                        v_high(0, path, k)
                    exps(path, 0, 0)
                either(act, lp, first_keys)
                hi(wdn[0][:, :, :], tbank[0][:, :].rearrange("p (k n) -> p k n", k=KC), "dn_w_full", 1, "dn_w_hi")
                hi(wup[0][:, :], tbank[1][:, :], "up_w_full", 1, "up_w_hi")
                act.wait_ge(s["raw_w"], 32)
                for h in range(NH):
                    act.activation(wo[0][:, h, :], raw_o[:, h, :], ACT.Copy, scale=t12[:, 0:1]).then_inc(s["wo_hi"], 1)

            def router_exp(b):
                act.wait_ge(s["rt_neg"], b + 1)
                act.activation(rt[:, 3, :], rt[:, 0, :], ACT.Exp, bias=rt[:, 2, 0:1]).then_inc(s["rt_exp"], 1)

            def down_high(c):
                act.wait_ge(s["dn_full"], c + 1)
                act.activation(dT[0][:, :], tbank[1][:, :], ACT.Copy, scale=gate[:, 0:1]).then_inc(s["dn_hi"], 1)

            def attention(path, b, cc, first, last):
                c = b * NC + cc
                n = c + 1

                def exps_ahead(h):
                    if path.ahead:
                        exps(path, c, h)

                def weighted(h):
                    if not path.ahead:
                        for kt in range(path.nk):
                            tp_high(path, c, h, kt)
                    pv_high(c, h)
                    if not path.ahead and h < NH - 1:
                        exps(path, c, h + 1)

                def turned(h):
                    if path.ahead:
                        for kt in range(path.nk):
                            tp_high(path, c, h, kt)

                turned(0)
                if not first:
                    ty_hi(c - 1, (0, 1))
                exps_ahead(1)
                if not first:
                    ty_hi(c - 1, (2, 3))
                weighted(0)
                if cc and not first:
                    router_exp(b)
                turned(1)
                exps_ahead(2)
                if not first:
                    act.wait_ge(s["gate_ok"], b + cc)
                    down_high(c - 1)
                if not last:
                    tx_hi(n)
                weighted(1)
                turned(2)
                exps_ahead(3)
                for h in (0, 1):
                    if h:
                        turned(3)
                    if not last:
                        q_swap_halves(n, h)
                        q_high(n, h)
                    weighted(2 + h)

            def outputs(c, new_batch, path, last):
                keys = path.blocks if new_batch is not None else 0
                if not last:
                    q_swap_halves(c + 1, 2)
                    q_high(c + 1, 2)
                if keys:
                    ctx_high(new_batch, path, 0)
                    k_swap_halves(new_batch, path, 0)
                y(c, 0)
                if keys:
                    k_high(new_batch, path, 0)
                if not last:
                    q_swap_halves(c + 1, 3)
                if keys:
                    v_high(new_batch, path, 0)
                if not last:
                    q_high(c + 1, 3)
                if keys == 2:
                    ctx_high(new_batch, path, 1)
                    k_swap_halves(new_batch, path, 1)
                    k_high(new_batch, path, 1)
                    v_high(new_batch, path, 1)
                y(c, 1)
                if not last:
                    exps(path, c + 1, 0)
                y(c, 2)
                y(c, 3)

            def step(b, cc, first=False, last=False):
                c = b * NC + cc
                lp, _ = load_flags(act, b)

                def same_batch(path):
                    attention(path, b, cc, first, last)
                    if cc == 0 or last:
                        outputs(c, None, path, last)
                either(act, lp, same_batch)
                if cc and not last:
                    lp2, _ = load_flags(act, b + 1)
                    either(act, lp2, lambda path: outputs(c, b + 1, path, last))

            prologue()
            pipeline(act, step)
            ty_hi(B * NC - 1)
            down_high(B * NC - 1)

        @block.vector
        def _(dve):
            dve.sem_inc(s["fin_done"], T)

            def lo(dst, src, high, wait, at, done, inc=1):
                dve.wait_ge(s[wait], at)
                dve.tensor_tensor(dst, src, high.bitcast(F32), ALU.subtract).then_inc(s[done], inc)

            def ln1(b, cc):
                c = b * NC + cc
                dve.wait_ge(s[f"x_in{cc}"], b * 16 + 16)
                for t in range(T):
                    dve.bn_stats(st6[:, 0, t, :], xb[cc][:, t, :]).then_inc(s["ln1_bn"], 1)
                for t in range(T):
                    hold(dve, "ln1_bn", c * T + t + 1)
                    dve.bn_aggr(mv1[:, t, :], st6[:, 0, t, :]).then_inc(s["ln1_stats"], 1)

            def tx_lo(n):
                for t in range(T):
                    lo(xT[1][:, :, t * P:(t + 1) * P], tbank[t % 2][:, :].rearrange("p (k n) -> p k n", k=KC),
                       xT[0][:, :, t * P:(t + 1) * P], "tx_hi", n * T + t + 1, "tx_done")

            def ty_lo(c, tiles=range(T)):
                for t in tiles:
                    lo(xT[1][:, :, t * P:(t + 1) * P], tbank[t % 2][:, :].rearrange("p (k n) -> p k n", k=KC),
                       xT[0][:, :, t * P:(t + 1) * P], "ty_hi", c * T + t + 1, "ty_done")

            def q_cos(n, ncc, h):
                i = n * NH + h
                if not (isinstance(i, int) and i == 0):
                    dve.wait_ge(s["q_done"], i)
                dve.wait_ge(s["q_swapped"], (i + 1) * 2)
                proj, _, _, rotated = rotation(h)
                dve.tensor_tensor(rotated, proj, qtab[:, 0, ncc * CH:(ncc + 1) * CH], ALU.mult)\
                    .then_inc(s["q_cos_ok"], 1)

            def q_sum(n, h):
                i = n * NH + h
                dve.wait_ge(s["q_cos_ok"], i + 1)
                dve.wait_ge(s["q_sin_ok"], i + 1)
                _, _, sines, rotated = rotation(h)
                dve.tensor_tensor(rotated, rotated, sines, ALU.add).then_inc(s["q_sum"], 1)

            def q_low(n, h):
                i = n * NH + h
                dve.wait_ge(s["q_hi"], i + 1)
                dve.tensor_tensor(qT[1][:, h, :], rotation(h)[3], qT[0][:, h, :].bitcast(F32), ALU.subtract)\
                    .then_inc(s["q_done"], 1)

            def minima(path, c, h):
                w = path.nk * P
                o = (h % 2) * 1024 if path.ahead else 0
                for qt in range(T):
                    i = h * T + qt
                    src = lg[:, qt * w:(qt + 1) * w] if path.ahead else lg[:, :]
                    hold(dve, "lg_full", c * 16 + (i | 1 if path.ahead else i) + 1)
                    dve.tensor_tensor_reduce(probs[:, o + qt * w:o + (qt + 1) * w], src, bias[:, 0:w], 1.0, 3.4e38,
                                             ALU.add, ALU.min, lmin[:, i:i + 1]).then_inc(s["lg_min"], 1)

            def normalize(path, c, h):
                w = path.nk * P
                o = (h % 2) * 1024 if path.ahead else 0
                dve.wait_ge(s["ex_done"], c * 16 + (h + 1) * T)
                dve.reciprocal(lrec[:, h * T:(h + 1) * T], lsum[:, h * T:(h + 1) * T]).then_inc(s["rec_done"], 1)
                dve.wait_ge(s["rec_done"], c * NH + h + 1)
                for qt in range(T):
                    p = probs[:, o + qt * w:o + (qt + 1) * w]
                    dve.tensor_scalar(p, p, lrec[:, h * T + qt:h * T + qt + 1], None, ALU.mult).then_inc(s["nrm_done"], 1)

            def tp_low(path, c, h, kt):
                slot = (h % 2) * 2 + kt if path.ahead else kt % 4
                lo(pT[1][:, slot, :], tp[kt % 2][:, :], pT[0][:, slot, :], "tp_hi",
                   (c * NH + h) * 8 + (kt + 1) * path.unit, "tp_done", path.unit)

            def pv_low(c, h):
                lo(eT[1][:, h, :], enc[:, :], eT[0][:, h, :], "pv_hi", c * NH + h + 1, "pv_done")

            def residual(c, cc, t, first):
                if not first:
                    dve.wait_ge(s["stored"], c * 16)
                dve.wait_ge(s["op_full"], c * T + t + 1)
                dve.tensor_tensor(x2[:, t, :], tp[t % 2][:, :], xb[cc][:, t, :], ALU.add)\
                    .then_inc(s["res_done"], 1)

            def ln2_stats(c, t):
                dve.wait_ge(s["res_done"], c * T + t + 1)
                dve.bn_stats(st6[:, 1, t, :], x2[:, t, :]).then_inc(s["ln2_bn"], 1)
                hold(dve, "ln2_bn", c * T + t + 1)
                dve.bn_aggr(mv2[:, t, :], st6[:, 1, t, :]).then_inc(s["ln2_stats"], 1)

            def ctx_stats(b, path, k):
                w = 2 // path.blocks
                dve.wait_ge(s["ctx_in_s"], 16 * (b * 2 + (k + 1) * w))
                for j in range(path.bt):
                    kt = k * path.bt + j
                    dve.bn_stats(st6[:, 2, j, :], ctx_raw[:, j, :]).then_inc(s["ctx_bn"], path.unit)
                    hold(dve, "ctx_bn", b * 8 + (kt + 1) * path.unit)
                    dve.bn_aggr(mvc[:, kt, :], st6[:, 2, j, :]).then_inc(s["ctx_stats"], path.unit)

            def mask_bias(b, path):
                m = path.nk * P
                dve.wait_ge(s["mask_b_in"], (b + 1) * 16)
                dve.tensor_scalar(bias[:, 0:m], mask_u8[:, 0:m], -FILL, FILL, ALU.mult, ALU.add)\
                    .then_inc(s["bias_ok"], 1)

            def ctx_low(b, path, k):
                for j in range(path.bt):
                    kt = k * path.bt + j
                    lo(ctx_part(1, path)[:, :, j * P:(j + 1) * P], tbank[kt % 2][:, :].rearrange("p (k n) -> p k n", k=KC),
                       ctx_part(0, path)[:, :, j * P:(j + 1) * P], "tc_hi", b * 8 + (kt + 1) * path.unit, "tc_done", path.unit)

            def k_cos(b, path, k, rotations):
                w = 2 // path.blocks
                n = path.bt * P
                at = b * 2 + (k + 1) * w
                if k:
                    dve.wait_ge(s["k_done"], at - w)
                dve.wait_ge(s["q_done"], rotations)
                dve.wait_ge(s["k_swapped"], at * 2)
                dve.wait_ge(s["ktab_in"], 16 * at)
                dve.tensor_tensor(q_rot[:, 0:n], qbank[:, 0:n], ktab[:, 0, 0:n], ALU.mult).then_inc(s["k_cos"], w)

            def k_low(b, path, k):
                w = 2 // path.blocks
                n = path.bt * P
                at = b * 2 + (k + 1) * w
                dve.wait_ge(s["k_cos"], at)
                dve.wait_ge(s["k_sin"], at)
                dve.tensor_tensor(q_rot[:, 0:n], q_rot[:, 0:n], q_sin[:, 0:n], ALU.add).then_inc(s["k_sum"], w)
                dve.wait_ge(s["k_hi"], at)
                dve.tensor_tensor(kT[1][:, k * n:(k + 1) * n], q_rot[:, 0:n],
                                  kT[0][:, k * n:(k + 1) * n].bitcast(F32), ALU.subtract).then_inc(s["k_done"], w)

            def v_low(b, path, k):
                w = 2 // path.blocks
                n = path.bt * P
                lo(v[1][:, k * path.bt:(k + 1) * path.bt, :], enc[:, 0:n].rearrange("p (t n) -> p t n", n=HD),
                   v[0][:, k * path.bt:(k + 1) * path.bt, :], "v_hi", b * 2 + (k + 1) * w, "v_done", w)

            def router(b):
                n = [0]

                def link(ins):
                    n[0] += 1
                    ins.then_inc(s["gate_step"], 1)
                    hold(dve, "gate_step", b * LINKS + n[0])

                LINKS = 12
                l = rt[:, 0, :]
                dve.wait_ge(s["rt_full"], b + 1)
                dve.tensor_copy(l, tbank[0][:, 0:E]).then_inc(s["rt_read"], 1)
                hold(dve, "rt_read", b + 1)
                link(dve.max(rt[:, 1, :], l))
                dve.tensor_scalar(rt[:, 2, 0:1], rt[:, 1, 0:1], -1.0, None, ALU.mult).then_inc(s["rt_neg"], 1)
                mine = l.rearrange("p (e o) -> p e o", o=1).to_broadcast([P, E, E])
                other = l.rearrange("p (o e) -> p o e", o=1).to_broadcast([P, E, E])
                link(dve.tensor_tensor(cmp[:, 0], other, mine, ALU.is_gt))
                link(dve.tensor_tensor(cmp[:, 1], other, mine, ALU.is_equal))
                link(dve.tensor_tensor(cmp[:, 2], cmp[:, 1], lower[:, :, :], ALU.mult))
                link(dve.tensor_tensor(cmp[:, 1], cmp[:, 0], cmp[:, 2], ALU.add))
                link(dve.tensor_reduce(rt[:, 4, :], cmp[:, 1], AX.X, ALU.add))
                link(dve.tensor_scalar(rt[:, 5, :], rt[:, 4, :], TOPK - 0.5, None, ALU.is_lt))
                dve.wait_ge(s["rt_exp"], b + 1)
                link(dve.tensor_tensor(rt[:, 6, :], rt[:, 3, :], rt[:, 5, :], ALU.mult))
                link(dve.tensor_reduce(rt[:, 7, 0:1], rt[:, 6, :], AX.X, ALU.add))
                link(dve.tensor_tensor(rt[:, 8, :], rt[:, 6, :], own[:, :], ALU.mult))
                link(dve.tensor_reduce(rt[:, 7, 1:2], rt[:, 8, :], AX.X, ALU.add))
                link(dve.reciprocal(rt[:, 7, 2:3], rt[:, 7, 0:1]))
                assert n[0] == LINKS
                dve.scalar_tensor_tensor(out=gate[:, 0:1], in0=rt[:, 7, 1:2], scalar=rt[:, 7, 2:3],
                                         in1=t12[:, 1:2], op0=ALU.mult, op1=ALU.mult).then_inc(s["gate_ok"], 1)

            def down_low(gates, c):
                dve.wait_ge(s["gate_ok"], gates)
                dve.wait_ge(s["dn_hi"], c + 1)
                dve.scalar_tensor_tensor(out=dT[1][:, :], in0=tbank[1][:, :], scalar=gate[:, 0:1], in1=dT[0][:, :].bitcast(F32),
                                         op0=ALU.mult, op1=ALU.subtract).then_inc(s["dn_done"], 1)

            def final(c, t):
                dve.wait_ge(s["up_full"], c * T + t + 1)
                dve.wait_ge(s["aff_ready"], c * T + t + 1)
                dve.tensor_tensor(x2[:, t, :], tbank[t % 2][:, :], x2[:, t, :], ALU.add)\
                    .then_inc(s["fin_done"], 1)

            def split_scaled(raw, dst, high, scale, wait, at, done):
                dve.wait_ge(s[wait], at)
                dve.scalar_tensor_tensor(out=dst, in0=raw, scalar=scale, in1=high.bitcast(F32),
                                         op0=ALU.mult, op1=ALU.subtract).then_inc(s[done], 1)

            def path_flags():
                f = flag_f[:, :].rearrange("o (a b g) -> o a b g", a=3, b=B)
                count = [0]

                def link(ins):
                    count[0] += 1
                    ins.then_inc(s["flag_step"], 1)
                    dve.wait_ge(s["flag_step"], count[0])

                dve.wait_ge(s["mask_in"], 16)
                link(dve.tensor_reduce(f[:, 0], mask_row.rearrange("o (b g k) -> o b g k", b=B, g=NG), AX.X, ALU.max))
                for g in range(NG):
                    link(dve.tensor_scalar(f[:, 1, :, g], f[:, 0, :, g], float(g), None, ALU.mult))
                link(dve.tensor_reduce(f[:, 2, :, 0], f[:, 0], AX.X, ALU.add))
                link(dve.tensor_reduce(f[:, 2, :, 1], f[:, 1], AX.X, ALU.add))
                link(dve.tensor_scalar(f[:, 2, :, 2], f[:, 2, :, 1], float(NG - 1), None, ALU.min))
                o = flags[:, :].rearrange("o (b a) -> o b a", a=2)
                link(dve.tensor_scalar(o[:, :, 0], f[:, 2, :, 0], 1.0, None, ALU.not_equal))
                dve.tensor_copy(o[:, :, 1], f[:, 2, :, 2]).then_inc(s["flags_ok"], 1)

            def prologue():
                path_flags()
                ln1(0, 0)
                dve.wait_ge(s["aux_full"], 1)
                aux = tbank[0][:, 0:KC * E].rearrange("p (k n) -> p k n", k=KC)
                dve.tensor_scalar(rms1[:, :], tbank[1][:, 0:KC], 1.0, None, ALU.add).then_inc(s["rms_ok"], 1)
                dve.tensor_copy(wrt[0][:, :, :], aux).then_inc(s["rt_ok"], 1)
                dve.wait_ge(s["rt_ok"], 1)
                dve.tensor_tensor(wrt[1][:, :, :], aux, wrt[0][:, :, :].bitcast(F32), ALU.subtract)\
                    .then_inc(s["rt_ok"], 1)
                dve.wait_ge(s["rms_ok"], 1)
                for k in range(KC):
                    split_scaled(raw_q[:, :, k, :], wq[1][:, k, :].rearrange("p (h n) -> p h n", h=NH),
                                 wq[0][:, k, :].rearrange("p (h n) -> p h n", h=NH), rms1[:, k:k + 1], "wq_hi", k + 1, "wq_ok")
                tx_lo(0)
                for k in range(KC):
                    split_scaled(raw_kv[:, :, k, :], wkv[1][:, :, k, :], wkv[0][:, :, k, :], rms1[:, k:k + 1],
                                 "wkv_hi", k + 1, "wkv_ok")
                dve.wait_ge(s["tab_in"], 16)
                for h in range(NH):
                    q_cos(0, 0, h)
                    q_sum(0, h)
                    q_low(0, h)
                lp, _ = load_flags(dve, 0)

                def first_keys(path):
                    for k in range(path.blocks):
                        ctx_stats(0, path, k)
                        ctx_low(0, path, k)
                        k_cos(0, path, k, NH)
                        k_low(0, path, k)
                        v_low(0, path, k)
                    dve.wait_ge(s["const_ok"], 1)
                    mask_bias(0, path)
                    minima(path, 0, 0)
                    normalize(path, 0, 0)
                either(dve, lp, first_keys)
                lo(wdn[1][:, :, :], tbank[0][:, :].rearrange("p (k n) -> p k n", k=KC), wdn[0][:, :, :], "dn_w_hi", 1, "dn_w_ok")
                lo(wup[1][:, :], tbank[1][:, :], wup[0][:, :], "up_w_hi", 1, "up_w_ok")
                for h in range(NH):
                    split_scaled(raw_o[:, h, :], wo[1][:, h, :], wo[0][:, h, :], t12[:, 0:1], "wo_hi", h + 1, "wo_ok")

            def attention(path, b, cc, first, last):
                c = b * NC + cc
                n = c + 1
                ncc = 1 - cc

                def turned(h):
                    if path.ahead:
                        for kt in range(path.nk):
                            tp_low(path, c, h, kt)

                def minima_ahead(h):
                    if path.ahead:
                        minima(path, c, h)

                def normalize_ahead(h):
                    if path.ahead:
                        normalize(path, c, h)

                def weighted(h):
                    if not path.ahead:
                        for kt in range(path.nk):
                            tp_low(path, c, h, kt)
                    pv_low(c, h)
                    if not path.ahead and h < NH - 1:
                        minima(path, c, h + 1)
                        normalize(path, c, h + 1)

                turned(0)
                if not first:
                    ty_lo(c - 1, (0, 1))
                minima_ahead(1)
                if not last:
                    ln1(b + cc, ncc)
                if not first:
                    ty_lo(c - 1, (2, 3))
                normalize_ahead(1)
                weighted(0)
                if cc:
                    router(b)
                turned(1)
                minima_ahead(2)
                normalize_ahead(2)
                if not first:
                    down_low(b + cc, c - 1)
                if not last:
                    tx_lo(n)
                weighted(1)
                turned(2)
                minima_ahead(3)
                if not first:
                    final(c - 1, 0)
                    final(c - 1, 1)
                normalize_ahead(3)
                if not last:
                    q_cos(n, ncc, 0)
                if not first:
                    final(c - 1, 2)
                    final(c - 1, 3)
                if not last:
                    q_sum(n, 0)
                    q_low(n, 0)
                weighted(2)
                turned(3)
                if not last:
                    q_cos(n, ncc, 1)
                    q_sum(n, 1)
                    q_low(n, 1)
                weighted(3)

            def outputs(c, cc, new_batch, path, first, last):
                n = c + 1
                keys = path.blocks if new_batch is not None else 0

                def residual_stats(t):
                    residual(c, cc, t, first)
                    ln2_stats(c, t)

                if keys:
                    ctx_stats(new_batch, path, 0)
                    mask_bias(new_batch, path)
                if not last:
                    q_cos(n, 1 - cc, 2)
                    q_sum(n, 2)
                residual_stats(0)
                if not last:
                    q_low(n, 2)
                if keys:
                    ctx_low(new_batch, path, 0)
                    k_cos(new_batch, path, 0, n * NH + 3)
                    k_low(new_batch, path, 0)
                if not last:
                    if keys:
                        dve.wait_ge(s["k_done"], new_batch * 2 + 2 // keys)
                    q_cos(n, 1 - cc, 3)
                    q_sum(n, 3)
                if keys:
                    v_low(new_batch, path, 0)
                if not last:
                    q_low(n, 3)
                if keys == 2:
                    ctx_stats(new_batch, path, 1)
                    ctx_low(new_batch, path, 1)
                    k_cos(new_batch, path, 1, (n + 1) * NH)
                    k_low(new_batch, path, 1)
                    v_low(new_batch, path, 1)
                residual_stats(1)
                if not last:
                    minima(path, n, 0)
                residual_stats(2)
                if not last:
                    normalize(path, n, 0)
                residual_stats(3)

            def step(b, cc, first=False, last=False):
                c = b * NC + cc
                lp, _ = load_flags(dve, b)

                def same_batch(path):
                    attention(path, b, cc, first, last)
                    if cc == 0 or last:
                        outputs(c, cc, None, path, first, last)
                either(dve, lp, same_batch)
                if cc and not last:
                    lp2, _ = load_flags(dve, b + 1)
                    either(dve, lp2, lambda path: outputs(c, cc, b + 1, path, first, last))

            prologue()
            pipeline(dve, step)
            ty_lo(B * NC - 1)
            down_low(B, B * NC - 1)
            for t in range(T):
                final(B * NC - 1, t)

        @block.tensor
        def _(pe):
            def product(dst, a, b, steps):
                last = None
                for i in range(steps):
                    for j, (p, q) in enumerate(((0, 0), (0, 1), (1, 0))):
                        last = pe.matmul(dst, a(p, i), b(q, i), start=(i == 0 and j == 0),
                                         stop=(i == steps - 1 and j == 2), skip_group_check=True)
                return last

            def turn(dst, src, n=P):
                return pe.transpose(dst, src, ident[0:n, 0:n])

            def turn_norm(t, full):
                for k in range(KC):
                    last = turn(tbank[t % 2][:, k * P:(k + 1) * P], norm[:, t, k * P:(k + 1) * P])
                last.then_inc(s[full], 1)

            def tx(n, waits):
                for t in range(T):
                    if t < 2:
                        waits(t)
                    else:
                        pe.wait_ge(s["tx_done"], n * T + t - 1)
                    pe.wait_ge(s["xn_ready"], n * T + t + 1)
                    turn_norm(t, "tx_full")

            def ty(c):
                for t in range(T):
                    if t < 2:
                        pe.wait_ge(s["fin_done"], c * T + T)
                    else:
                        pe.wait_ge(s["ty_done"], c * T + t - 1)
                    pe.wait_ge(s["y_ready"], c * T + t + 1)
                    turn_norm(t, "ty_full")

            def router(b, c):
                pe.wait_ge(s["ty_done"], c * T + 3)
                product(tbank[0][:, 0:E], lambda p, k: xT[p][:, k, 0:1].to_broadcast([P, P]),
                        lambda q, k: wrt[q][:, k, :], KC).then_inc(s["rt_full"], 1)

            def down(c):
                pe.wait_ge(s["ty_done"], (c + 1) * T)
                product(tbank[1][:, :], lambda p, k: wdn[p][:, k, :], lambda q, k: xT[q][:, k, :], KC)\
                    .then_inc(s["dn_full"], 1)

            def up(c, tiles=range(T)):
                for t in tiles:
                    if t < 2:
                        pe.wait_ge(s["dn_done"], c + 1)
                    else:
                        pe.wait_ge(s["fin_done"], T + c * T + t - 1)
                    product(tbank[t % 2][:, :], lambda p, _: dT[p][:, t * P:(t + 1) * P],
                            lambda q, _: wup[q][:, :], 1).then_inc(s["up_full"], 1)

            def q_proj(n, h):
                pe.wait_ge(s["tx_done"], (n + 1) * T)
                start = isinstance(n, int) and n == 0
                if h < 2 and not (start and h == 0):
                    pe.wait_ge(s["q_swapped"], (n * NH + h) * 2)
                    pe.wait_ge(s["q_cos_ok"], n * NH + h)
                elif h >= 2 and not start:
                    pe.wait_ge(s["lg_min"], n * 16)
                product(rotation(h)[0], lambda p, k: wq[p][:, k, h * HD:(h + 1) * HD],
                        lambda q, k: xT[q][:, k, :], KC).then_inc(s["q_full"], 1)

            def first_logits(path, n):
                pe.wait_ge(s["q_swapped"], (n + 1) * NH * 2)
                pe.wait_ge(s["q_cos_ok"], (n + 1) * NH)
                pe.wait_ge(s["q_done"], n * NH + 3)
                logits(path, n, 0)

            def logits(path, c, h):
                w = path.nk * P
                pe.wait_ge(s["q_done"], c * NH + h + 1)
                for qt in range(T):
                    i = c * 16 + h * T + qt
                    if h or qt:
                        if path.ahead and h and qt % 2 == 0:
                            pe.wait_ge(s["lg_min"], i - T + 2)
                        elif not path.ahead:
                            pe.wait_ge(s["lg_min"], i)
                    for half in range(max(1, w // 512)):
                        n = min(w, 512)
                        dst = lg[:, qt * w:(qt + 1) * w] if path.ahead else lg[:, half * n:(half + 1) * n]
                        last = product(dst, lambda p, _: qT[p][:, h, qt * P:(qt + 1) * P],
                                       lambda q, _: kT[q][:, half * n:(half + 1) * n], 1)
                    last.then_inc(s["lg_full"], 1)

            def turn_probs(path, c, h, kt, first):
                w = path.nk * P
                o = (h % 2) * 1024 if path.ahead else 0
                at = (c * NH + h) * 8
                if path.ahead and h:
                    pe.wait_ge(s["tp_done"], at - 4 + 4 * kt)
                elif not path.ahead and kt >= 2:
                    pe.wait_ge(s["tp_done"], at + kt - 1)
                elif not path.ahead and h:
                    pe.wait_ge(s["tp_done"], at)
                elif not first:
                    pe.wait_ge(s["res_done"], c * T)
                for qt in range(T):
                    pe.wait_ge(s["nrm_done"], c * 16 + h * T + qt + 1)
                    last = turn(tp[kt % 2][:, qt * P:(qt + 1) * P], probs[:, o + qt * w + kt * P:o + qt * w + (kt + 1) * P])
                last.then_inc(s["tp_full"], path.unit)

            def weigh_values(path, c, h, kt):
                slot = (h % 2) * 2 + kt if path.ahead else kt % 4
                pe.wait_ge(s["tp_done"], (c * NH + h) * 8 + (kt + 1) * path.unit)
                if kt == 0:
                    if not (isinstance(c, int) and c * NH + h == 0):
                        pe.wait_ge(s["pv_done"], c * NH + h)
                for j, (p, q) in enumerate(((0, 0), (0, 1), (1, 0))):
                    last = pe.matmul(enc[:, :], v[p][:, kt, :], pT[q][:, slot, :], start=(kt == 0 and j == 0),
                                     stop=(kt == path.nk - 1 and j == 2), skip_group_check=True)
                if kt == path.nk - 1:
                    last.then_inc(s["pv_full"], 1)

            def attention(path, b, cc, first, last):
                c = b * NC + cc
                n = c + 1

                def others(h):
                    if h == 0 and not first:
                        ty(c - 1)
                        if cc:
                            router(b, c - 1)
                    if h == 1:
                        def waits(t):
                            if t == 0 and cc:
                                pe.wait_ge(s["rt_read"], b + 1)
                            elif t == 1 and not first:
                                pe.wait_ge(s["dn_done"], c)
                        if not first:
                            down(c - 1)
                        if not last:
                            tx(n, waits)
                    if h == 2:
                        if not first:
                            if not last:
                                pe.wait_ge(s["tx_done"], (n + 1) * T)
                            up(c - 1, (0, 1))
                        if not last:
                            q_proj(n, 0)
                        if not first:
                            up(c - 1, (2, 3))
                    if h == 3 and not last:
                        q_proj(n, 1)

                for h in range(NH):
                    if path.ahead:
                        if h < NH - 1:
                            logits(path, c, h + 1)
                        for kt in range(path.nk):
                            turn_probs(path, c, h, kt, first)
                        others(h)
                        for kt in range(path.nk):
                            weigh_values(path, c, h, kt)
                    else:
                        others(h)
                        turn_probs(path, c, h, 0, first)
                        for kt in range(1, path.nk):
                            turn_probs(path, c, h, kt, first)
                            weigh_values(path, c, h, kt - 1)
                        weigh_values(path, c, h, path.nk - 1)
                        if h < NH - 1:
                            logits(path, c, h + 1)

            def out_proj(c, t):
                if t < 2:
                    pe.wait_ge(s["wo_ok"], NH)
                    pe.wait_ge(s["tp_done"], (c + 1) * NH * 8)
                    pe.wait_ge(s["pv_done"], (c + 1) * NH)
                else:
                    pe.wait_ge(s["res_done"], c * T + t - 1)
                product(tp[t % 2][:, :], lambda p, h: eT[p][:, h, t * P:(t + 1) * P],
                        lambda q, h: wo[q][:, h, :], NH).then_inc(s["op_full"], 1)

            def turn_ctx(b, path, k):
                for j in range(path.bt):
                    kt = k * path.bt + j
                    pe.wait_ge(s["ctx_normed"], b * 8 + (kt + 1) * path.unit)
                    if kt >= 2:
                        pe.wait_ge(s["tc_done"], b * 8 + (kt - 1) * path.unit)
                    for kk in range(KC):
                        last = turn(tbank[kt % 2][:, kk * P:(kk + 1) * P], ctx_raw[:, j, kk * P:(kk + 1) * P])
                    last.then_inc(s["tc_full"], path.unit)

            def k_proj(b, path, k, rotations):
                w = 2 // path.blocks
                n = path.bt * P
                pe.wait_ge(s["tc_done"], b * 8 + (k + 1) * path.bt * path.unit)
                if k:
                    pe.wait_ge(s["k_cos"], b * 2 + k)
                else:
                    pe.wait_ge(s["q_cos_ok"], rotations)
                product(qbank[:, 0:n], lambda p, kk: wkv[p][:, 0, kk, :], lambda q, kk: ctx_part(q, path)[:, kk, :], KC)\
                    .then_inc(s["k_full"], w)

            def v_proj(b, path, k):
                w = 2 // path.blocks
                if k:
                    pe.wait_ge(s["v_done"], b * 2 + k)
                for j in range(path.bt):
                    last = product(enc[:, j * P:(j + 1) * P], lambda p, kk: ctx_part(p, path)[:, kk, j * P:(j + 1) * P],
                                   lambda q, kk: wkv[q][:, 1, kk, :], KC)
                last.then_inc(s["v_full"], w)

            def keys_there(b):
                pe.wait_ge(s["k_done"], (b + 1) * 2)
                pe.wait_ge(s["v_done"], (b + 1) * 2)
                pe.wait_ge(s["bias_ok"], b + 1)

            def outputs(c, new_batch, path, last):
                n = c + 1
                keys = path.blocks if new_batch is not None else 0
                if not last:
                    q_proj(n, 2)
                out_proj(c, 0)
                if keys:
                    pe.wait_ge(s["fin_done"], n * T)
                    turn_ctx(new_batch, path, 0)
                    k_proj(new_batch, path, 0, n * NH + 2)
                if not last:
                    q_proj(n, 3)
                if keys:
                    v_proj(new_batch, path, 0)
                if keys == 2:
                    turn_ctx(new_batch, path, 1)
                    k_proj(new_batch, path, 1, None)
                    v_proj(new_batch, path, 1)
                out_proj(c, 1)
                if keys:
                    keys_there(new_batch)
                if not last:
                    first_logits(path, n)
                out_proj(c, 2)
                out_proj(c, 3)

            def step(b, cc, first=False, last=False):
                c = b * NC + cc
                lp, _ = load_flags(pe, b)

                def same_batch(path):
                    attention(path, b, cc, first, last)
                    if cc == 0 or last:
                        outputs(c, None, path, last)
                either(pe, lp, same_batch)
                if cc and not last:
                    lp2, _ = load_flags(pe, b + 1)
                    either(pe, lp2, lambda path: outputs(c, b + 1, path, last))

            pe.wait_ge(s["ident_ok"], 1)
            pe.wait_ge(s["raw_aux_in"], 32)
            for k in range(KC):
                pe.transpose(tbank[0][:, k * E:(k + 1) * E], raw_router[:, k * P:(k + 1) * P], ident[0:E, 0:E])
            pe.transpose(tbank[1][:, 0:KC], raw_rms, ident[0:KC, 0:KC]).then_inc(s["aux_full"], 1)
            pe.wait_ge(s["rt_ok"], 2)
            pe.wait_ge(s["rms_ok"], 1)
            tx(0, lambda t: None)
            pe.wait_ge(s["wq_ok"], KC)
            for h in range(NH):
                q_proj(0, h)
            pe.wait_ge(s["wkv_ok"], KC)
            pe.wait_ge(s["flags_ok"], 1)
            lp, _ = load_flags(pe, 0)

            def first_keys(path):
                for k in range(path.blocks):
                    turn_ctx(0, path, k)
                    k_proj(0, path, k, 2)
                    v_proj(0, path, k)
                keys_there(0)
                first_logits(path, 0)
            either(pe, lp, first_keys)
            pe.wait_ge(s["raw_dn_in"], 16)
            pe.wait_ge(s["raw_up_in"], 16 * KC)
            for k in range(KC):
                last = turn(tbank[0][:, k * P:(k + 1) * P], raw_dn[:, k * P:(k + 1) * P])
            last.then_inc(s["dn_w_full"], 1)
            for k in range(KC):
                last = turn(tbank[1][:, k * P:(k + 1) * P], raw_up[:, k, :])
            last.then_inc(s["up_w_full"], 1)
            pe.wait_ge(s["dn_w_ok"], 1)
            pe.wait_ge(s["up_w_ok"], 1)

            pipeline(pe, step)
            ty(B * NC - 1)
            down(B * NC - 1)
            up(B * NC - 1)


_INS = ["x", "ctx_1024", "mask_BxS2_bk0", "g_xattn", "g_ffn", "L0_xattn_rms_scale", "L0_xattn_q_w",
        "L0_xattn_kv_w", "L0_xattn_out_w", "L0_ffn_router_w", "L0_ffn_lora_down", "L0_ffn_lora_up"]
_OUT = ((B, S, D), "float32")


def kernel(**inputs):
    import numpy as _np
    import concourse.bacc as _bacc
    from concourse import mybir as _mybir
    from concourse.bass_utils import run_bass_kernel_spmd as _run

    nc = _bacc.Bacc("TRN2", target_bir_lowering=False, num_devices=1)
    arrays, args = {}, []

    def give(name, a):
        arrays[name] = a
        args.append(nc.dram_tensor(name, a.shape, _mybir.dt.from_np(a.dtype), kind="ExternalInput").ap())

    for name in _INS:
        a = _np.ascontiguousarray(inputs[name])
        give(f"in_{name}_dram", a)
    for name, a in zip(("q_table", "k_table"), rope_tables()):
        give(f"in_{name}_dram", a)
    shape, dtype = _OUT
    args.append(nc.dram_tensor("out_dram", shape, _mybir.dt.from_np(_np.dtype(dtype)), kind="ExternalOutput").ap())
    gated_block(nc, *args)
    r = _run(nc, [arrays], core_ids=[0])
    return r.results[0]["out_dram"]
```

```python
from contextlib import ExitStack

import numpy as np

import concourse.bass as bass
from concourse import mybir

F32 = mybir.dt.float32
F32R = mybir.dt.float32r
U8 = mybir.dt.uint8
I32 = mybir.dt.int32
ALU = mybir.AluOpType
ACT = mybir.ActivationFunctionType
AX = mybir.AxisListType

P = 128
B, S, D = 4, 1024, 512
NH, HD = 4, 128
E, R, TOPK = 8, 16, 2
ER = E * R
KC = D // P
CH = 512
NC = S // CH
T = CH // P
GK = 256
NG = S // GK
FILL = 2.3819763e38
LN_EPS = 1e-5
RMS_EPS = 1e-6


def rope_tables():
    half = HD // 2
    freq = np.float32(2.0 / HD) * np.arange(half, dtype=np.float32)
    timescale = (np.float32(10000.0) ** freq).astype(np.float32)
    pos = np.arange(2 * S, dtype=np.float32)
    rad = (pos[None, :] / timescale[:, None]).astype(np.float32)
    cos = np.cos(rad).astype(np.float32)
    sin = np.sin(rad).astype(np.float32)
    cos = np.concatenate([cos, cos], 0)
    sin = np.concatenate([-sin, sin], 0)
    scale = np.float32(-float(HD) ** -0.5)
    keys = np.stack([cos[:, :S], sin[:, :S]], 1)
    queries = np.stack([cos[:, S:] * scale, sin[:, S:] * scale], 1)
    return np.ascontiguousarray(queries), np.ascontiguousarray(keys)


def gated_block(nc, x, ctx_in, mask, g_xattn, g_ffn, rms_scale, q_w, kv_w, out_w, router_w,
                lora_down, lora_up, q_table, k_table, out):
    stack = ExitStack()
    with stack:
        def sb(name, shape, dt=F32):
            return stack.enter_context(nc.sbuf_tensor(name, shape, dt))

        def sem(name):
            return stack.enter_context(nc.semaphore(name))

        wq = [sb(f"wq_{p}", [P, KC, NH * HD], F32R) for p in "hl"]
        wkv = [sb(f"wkv_{p}", [P, 2, KC, HD], F32R) for p in "hl"]
        wo = [sb(f"wo_{p}", [P, NH, D], F32R) for p in "hl"]
        wdn = [sb(f"wdn_{p}", [P, KC, ER], F32R) for p in "hl"]
        wup = [sb(f"wup_{p}", [P, D], F32R) for p in "hl"]
        wrt = [sb(f"wrt_{p}", [P, KC, E], F32R) for p in "hl"]
        qtab = sb("qtab", [P, 2, S])
        ktab = sb("ktab", [P, 2, CH])
        ident = sb("ident", [P, P])
        own = sb("own", [P, E])
        lower = sb("lower", [P, E, E])
        neg_half = sb("neg_half", [P, T])
        gates_in = sb("gates_in", [P, 2])
        t12 = sb("t12", [P, 2])
        rms1 = sb("rms1", [P, KC])
        xb = [sb(f"x_{i}", [P, T, D]) for i in range(NC)]
        norm = sb("norm", [P, T, D])
        xT = [sb(f"xT_{p}", [P, KC, CH], F32R) for p in "hl"]
        qT = [sb(f"qT_{p}", [P, NH, CH], F32R) for p in "hl"]
        kT = [sb(f"kT_{p}", [P, S], F32R) for p in "hl"]
        v = [sb(f"v_{p}", [P, S // P, HD], F32R) for p in "hl"]
        q_swap = sb("q_swap", [P, CH])
        q_sin = sb("q_sin", [P, CH])
        q_rot = sb("q_rot", [P, CH])
        probs = sb("probs", [P, 4 * S])
        pT = [sb(f"pT_{p}", [P, 4, CH], F32R) for p in "hl"]
        eT = [sb(f"eT_{p}", [P, KC, CH], F32R) for p in "hl"]
        dT = [sb(f"dT_{p}", [P, CH], F32R) for p in "hl"]
        x2 = sb("x2", [P, T, D])
        bias = sb("bias", [P, S])
        mask_u8 = sb("mask_u8", [P, S], U8)
        st6 = sb("st6", [P, 3, T, 6])
        mv1 = sb("mv1", [P, T, 2])
        var1 = sb("var1", [P, T])
        rs1 = sb("rs1", [P, T])
        nm1 = sb("nm1", [P, T])
        mv2 = sb("mv2", [P, T, 2])
        small2 = sb("small2", [P, T, 5])
        mvc = sb("mvc", [P, 8, 2])
        smallc = sb("smallc", [P, 8, 3])
        lmin = sb("lmin", [P, NH * T])
        lsum = sb("lsum", [P, NH * T])
        lrec = sb("lrec", [P, NH * T])
        rt = sb("rt", [P, 16, E])
        cmp = sb("cmp", [P, 3, E, E])
        gate = sb("gate", [P, 1])
        flag_f = sb("flag_f", [1, 3 * B * NG])
        flags = sb("flags", [1, 2 * B], I32)

        bank = [stack.enter_context(nc.psum_tensor(f"bank{i}", [P, 512], F32)) for i in range(3)]
        lg = stack.enter_context(nc.psum_tensor("lg", [P, 1024], F32))
        tp = [stack.enter_context(nc.psum_tensor(f"tp{i}", [P, 512], F32)) for i in range(2)]
        enc = stack.enter_context(nc.psum_tensor("enc", [P, 512], F32))
        tbank, qbank = bank[0:2], bank[2]

        raw_q = probs[:, 0:2048].rearrange("p (h k n) -> p h k n", h=NH, k=KC)
        raw_o = norm[:, :, :]
        raw_kv = x2[:, 0:2, :].rearrange("p c (k n) -> p c k n", k=KC)
        raw_dn = x2[:, 2, :]
        raw_up = x2[:, 3, :].rearrange("p (k n) -> p k n", k=KC)
        raw_router = q_swap[0:E, :]
        raw_rms = q_sin[0:KC, 0:P]
        ctxT = [p.rearrange("p s n -> p (s n)") for p in (pT[0][:, :, :], pT[1][:, :, :])]

        def ctx_part(p, path):
            n = path.bt * P
            return ctxT[p][:, 0:KC * n].rearrange("p (k n) -> p k n", k=KC)

        ctx_raw = probs[:, 2048:4096].rearrange("p (t d) -> p t d", t=4)
        mask_row = bias[0:1, :].bitcast(U8)

        names = """passed g_in raw_w raw_kv_in raw_dn_in raw_up_in raw_aux_in tab_in mask_in ident_ok const_ok tanh_ok
            aux_full rms_ok rt_ok dn_w_full dn_w_hi dn_w_ok up_w_full up_w_hi up_w_ok wq_hi wq_ok wo_hi wo_ok
            wkv_hi wkv_ok flags_ok flag_step const_step
            x_in0a x_in0b x_in1a x_in1b ln1_bn ln1_stats ln1_scales xn_ready tx_full tx_hi tx_done ty_full ty_hi ty_done
            q_full q_swapped q_sin_ok q_cos_ok q_sum q_hi q_done
            lg_full lg_min ex_done rec_done nrm_done tp_full tp_hi tp_done pv_full pv_hi pv_done
            op_full res_done ln2_bn ln2_stats ln2_var ln2_scales y_ready aff_ready up_full fin_done stored
            rt_full rt_read rt_neg gate_step rt_exp gate_ok dn_full dn_hi dn_done
            ctx_in_s ktab_in mask_b_in bias_ok ctx_bn ctx_stats ctx_rms ctx_inv ctx_normed tc_full tc_hi tc_done
            k_full k_swapped k_sin k_cos k_sum k_hi k_done v_full v_hi v_done"""
        s = {n: sem("s_" + n) for n in names.split()}
        block = stack.enter_context(nc.Block())

        def rotation(h):
            proj = (qbank[:, :], qbank[:, :], lg[:, 0:512], lg[:, 512:1024])[h]
            if h == 2:
                return proj, probs[:, 0:512], probs[:, 1024:1536], probs[:, 1536:2048]
            return proj, q_swap[:, :], q_sin[:, :], q_rot[:, :]

        def hold(eng, name, value):
            eng.wait_ge(s[name], value)
            eng.sem_inc(s["passed"], 1)

        def load_flags(eng, b):
            long_path = eng.value_load(flags[0:1, bass.ds(2 * b, 1)], min_val=0, max_val=1)
            group = eng.value_load(flags[0:1, bass.ds(2 * b + 1, 1)], min_val=0, max_val=NG - 1)
            return long_path, group

        def either(eng, long_path, body):
            with eng.If(long_path == 0):
                body(SHORT)
            with eng.Else():
                body(LONG)

        class SHORT:
            nk = GK // P
            unit = 4
            blocks = 1
            bt = GK // P
            ahead = True

        class LONG:
            nk = S // P
            unit = 1
            blocks = 2
            bt = 4
            ahead = False

        def pipeline(eng, start, attention, outputs):
            def batch(path, b, first, last):
                if first:
                    start(path)
                else:
                    outputs(path, b - 1, NC - 1, True, False, False)
                attention(path, b, 0, first, False)
                outputs(path, b, 0, False, first, False)
                attention(path, b, 1, False, last)
                if last:
                    outputs(path, b, 1, False, False, True)

            lp, _ = load_flags(eng, 0)
            either(eng, lp, lambda path: batch(path, 0, True, False))
            with eng.Fori(1, B - 1) as b:
                lp, _ = load_flags(eng, b)
                either(eng, lp, lambda path: batch(path, b, False, False))
            lp, _ = load_flags(eng, B - 1)
            either(eng, lp, lambda path: batch(path, B - 1, False, True))

        @block.sync
        def _(sp):
            def rows(t, b, cc, first, n):
                start = (b * NC + cc) * T + first
                return t.rearrange("(c p) d -> p c d", p=P)[:, bass.ds(start, n), :]

            x_rows = x.rearrange("b s d -> (b s) d")
            out_rows = out.rearrange("b s d -> (b s) d")
            x_in = [[s[f"x_in{cc}{half}"] for half in "ab"] for cc in range(NC)]

            def load_x(b, cc, half):
                tiles = slice(half * T // 2, (half + 1) * T // 2)
                sp.dma_start(xb[cc][:, tiles, :], rows(x_rows, b, cc, half * T // 2, T // 2)).then_inc(x_in[cc][half], 16)

            def load_ctx(b, long_path, group):
                def body(path):
                    n = path.nk * P
                    first = group * GK if path is SHORT else 0
                    sp.dma_start(mask_u8[:, 0:n], mask[bass.ds(b, 1), bass.ds(first, n)].to_broadcast([P, n]))\
                        .then_inc(s["mask_b_in"], 16)
                    n = path.bt * P
                    for k in range(path.blocks):
                        first = group * GK if path is SHORT else k * n
                        if k:
                            sp.wait_ge(s["tc_full"], b * 8 + 4)
                            sp.wait_ge(s["k_sum"], b * 2 + 1)
                        sp.dma_start(ctx_raw[:, 0:path.bt, :],
                                     ctx_in[bass.ds(b, 1), bass.ds(first, n), :]
                                     .rearrange("o (t p) d -> p (o t) d", p=P)).then_inc(s["ctx_in_s"], 16 * (2 // path.blocks))
                        sp.dma_start(ktab[:, :, 0:n], k_table[:, :, bass.ds(first, n)]).then_inc(s["ktab_in"], 16 * (2 // path.blocks))
                either(sp, long_path, body)

            sp.dma_start(mask_row, mask.rearrange("b s -> (b s)").rearrange("(o n) -> o n", o=1)).then_inc(s["mask_in"], 16)
            load_x(0, 0, 0)
            load_x(0, 0, 1)
            sp.dma_start(raw_router, router_w).then_inc(s["raw_aux_in"], 16)
            sp.dma_start(raw_rms, rms_scale.rearrange("(k p) -> k p", p=P)).then_inc(s["raw_aux_in"], 16)
            sp.dma_start(raw_q.rearrange("p h k n -> p (h k) n"),
                         q_w.rearrange("h (k p) n -> p (h k) n", p=P)).then_inc(s["raw_w"], 16)
            sp.dma_start(raw_kv.rearrange("p c k n -> p (c k) n"),
                         kv_w.rearrange("c o (k p) n -> p (c o k) n", p=P)).then_inc(s["raw_kv_in"], 16)
            sp.dma_start(qtab[:, :, :], q_table).then_inc(s["tab_in"], 16)
            sp.wait_ge(s["flags_ok"], 1)
            lp, g = load_flags(sp, 0)
            load_ctx(0, lp, g)
            load_x(0, 1, 0)
            load_x(0, 1, 1)
            sp.dma_start(raw_dn, lora_down.rearrange("e r d -> (e r) d")).then_inc(s["raw_dn_in"], 16)
            for k in range(KC):
                sp.dma_start(raw_up[:, k, :].rearrange("p (e r) -> p e r", e=E),
                             lora_up[:, k * P:(k + 1) * P, :].rearrange("e p r -> p e r")).then_inc(s["raw_up_in"], 16)
            sp.wait_ge(s["tx_full"], T)
            sp.dma_start(raw_o, out_w.rearrange("h p n -> p h n")).then_inc(s["raw_w"], 16)

            def store(c):
                sp.wait_ge(s["fin_done"], (c + 1) * T + T)
                sp.dma_start(out_rows.rearrange("(c p) d -> p c d", p=P)[:, bass.ds(c * T, T), :], x2[:, :, :])\
                    .then_inc(s["stored"], 16)

            def step(b, cc, first=False, last=False):
                c = b * NC + cc
                if not (first or last):
                    for half in (0, 1):
                        sp.wait_ge(s["res_done"], (c - 1) * T + (half + 1) * T // 2)
                        load_x(b + cc, 1 - cc, half)
                if not first:
                    store(c - 1)
                if cc == NC - 1 and not last:
                    lp_now, _ = load_flags(sp, b)
                    lp_next, g_next = load_flags(sp, b + 1)
                    hold(sp, "k_done", (b + 1) * 2)
                    with sp.If(lp_now == 0):
                        hold(sp, "bias_ok", b + 1)
                    with sp.Else():
                        hold(sp, "tp_full", (c + 1) * NH * 8)
                    load_ctx(b + 1, lp_next, g_next)

            step(0, 0, first=True)
            with sp.Fori(0, B - 1) as b:
                step(b, 1)
                step(b + 1, 0)
            step(B - 1, 1, last=True)
            store(B * NC - 1)
            sp.wait_ge(s["stored"], 16 * B * NC)

        @block.gpsimd
        def _(pool):
            pool.dma_start(gates_in[:, 0:1], g_xattn.rearrange("(o n) -> o n", o=1).to_broadcast([P, 1])).then_inc(s["g_in"], 16)
            pool.dma_start(gates_in[:, 1:2], g_ffn.rearrange("(o n) -> o n", o=1).to_broadcast([P, 1])).then_inc(s["g_in"], 16)
            pool.memset(ident[:, :], 0.0).then_inc(s["const_step"], 1)
            pool.memset(neg_half[:, :], -0.5).then_inc(s["const_step"], 1)
            pool.memset(own[:, :], 1.0).then_inc(s["const_step"], 1)
            pool.memset(lower[:, :, :], 1.0).then_inc(s["const_step"], 1)
            pool.wait_ge(s["const_step"], 4)
            pool.affine_select(out=ident[:, :], in_=ident[:, :], compare_op=ALU.not_equal, fill=1.0, base=0,
                               pattern=[[-1, P]], channel_multiplier=1).then_inc(s["ident_ok"], 1)
            pool.affine_select(out=own[:, :], in_=own[:, :], compare_op=ALU.is_ge, fill=0.0, base=0,
                               pattern=[[-R, E]], channel_multiplier=1).then_inc(s["const_step"], 1)
            pool.wait_ge(s["const_step"], 5)
            pool.affine_select(out=own[:, :], in_=own[:, :], compare_op=ALU.is_ge, fill=0.0, base=R - 1,
                               pattern=[[R, E]], channel_multiplier=-1).then_inc(s["const_step"], 1)
            pool.affine_select(out=lower[:, :, :], in_=lower[:, :, :], compare_op=ALU.is_ge, fill=0.0, base=-1,
                               pattern=[[1, E], [-1, E]], channel_multiplier=0).then_inc(s["const_step"], 1)
            pool.wait_ge(s["const_step"], 7)
            pool.drain().then_inc(s["const_ok"], 1)
            def ln1(c, half):
                two = slice(half * T // 2, (half + 1) * T // 2)
                at = c * 6 + half * 3
                hold(pool, "ln1_stats", c * T + (half + 1) * T // 2)
                pool.tensor_scalar(var1[:, two], mv1[:, two, 1], 1.0 + RMS_EPS, LN_EPS * RMS_EPS, ALU.mult, ALU.add)\
                    .then_inc(s["ln1_scales"], 1)
                pool.tensor_scalar(nm1[:, two], mv1[:, two, 0], -1.0, 0.0, ALU.mult, ALU.add).then_inc(s["ln1_scales"], 1)
                pool.wait_ge(s["ln1_scales"], at + 2)
                pool.tensor_tensor(rs1[:, two], var1[:, two], neg_half[:, two], ALU.pow).then_inc(s["ln1_scales"], 1)

            def xn(c, cc, half, reuse):
                hold(pool, "ln1_scales", c * 6 + half * 3 + 3)
                for t in range(half * T // 2, (half + 1) * T // 2):
                    if reuse:
                        hold(pool, "ty_full", (c - 2) * T + t + 1)
                    pool.tensor_scalar(norm[:, t, :], xb[cc][:, t, :], nm1[:, t:t + 1], rs1[:, t:t + 1],
                                       ALU.add, ALU.mult).then_inc(s["xn_ready"], 1)

            def normalize(path, c, h):
                w = path.nk * P
                o = (h % 2) * 1024 if path.ahead else 0
                hold(pool, "rec_done", c * NH + h + 1)
                for qt in range(T):
                    p = probs[:, o + qt * w:o + (qt + 1) * w]
                    pool.tensor_scalar(p, p, lrec[:, h * T + qt:h * T + qt + 1], 1.0, ALU.mult, ALU.mult)\
                        .then_inc(s["nrm_done"], 1)

            def ctx_norm(b, path, k):
                w = 2 // path.blocks
                t0 = k * path.bt
                at = b * 6 + k * 3
                m, var = mvc[:, t0:t0 + path.bt, 0], mvc[:, t0:t0 + path.bt, 1]
                square, total, inv = (smallc[:, t0:t0 + path.bt, i] for i in range(3))
                pool.wait_ge(s["ctx_stats"], b * 8 + (t0 + path.bt) * path.unit)
                pool.tensor_tensor(square, m, m, ALU.mult).then_inc(s["ctx_rms"], w)
                pool.wait_ge(s["ctx_rms"], at + w)
                pool.tensor_tensor(total, square, var, ALU.add).then_inc(s["ctx_rms"], w)
                hold(pool, "ctx_rms", at + 2 * w)
                pool.tensor_scalar(total, total, RMS_EPS, 1.0, ALU.add, ALU.mult).then_inc(s["ctx_rms"], w)
                pool.wait_ge(s["ctx_rms"], at + 3 * w)
                pool.tensor_tensor(inv, total, neg_half[:, 0:path.bt], ALU.pow).then_inc(s["ctx_inv"], w)
                hold(pool, "ctx_inv", b * 2 + (k + 1) * w)
                for j in range(path.bt):
                    pool.tensor_scalar(ctx_raw[:, j, :], ctx_raw[:, j, :], smallc[:, t0 + j, 2:3], 1.0,
                                       ALU.mult, ALU.mult).then_inc(s["ctx_normed"], path.unit)

            def k_sines(b, path, k):
                n = path.bt * P
                w = 2 // path.blocks
                pool.wait_ge(s["k_swapped"], b * 4 + (k + 1) * w * 2)
                pool.wait_ge(s["ktab_in"], 16 * (b * 2 + (k + 1) * w))
                pool.tensor_tensor(q_sin[:, 0:n], q_swap[:, 0:n], ktab[:, 1, 0:n], ALU.mult).then_inc(s["k_sin"], w)

            def q_sine(c, cc, h):
                pool.wait_ge(s["q_swapped"], (c * NH + h + 1) * 2)
                _, swapped, sines, _ = rotation(h)
                pool.tensor_tensor(sines, swapped, qtab[:, 1, cc * CH:(cc + 1) * CH], ALU.mult)\
                    .then_inc(s["q_sin_ok"], 1)

            def ln2(c, t):
                m = small2[:, t, :]
                at = (c * T + t) * 3
                hold(pool, "ln2_stats", c * T + t + 1)
                pool.tensor_scalar(m[:, 0:1], mv2[:, t, 1:2], LN_EPS, 1.0, ALU.add, ALU.mult).then_inc(s["ln2_var"], 1)
                pool.wait_ge(s["ln2_var"], at + 1)
                pool.tensor_tensor(m[:, 1:2], m[:, 0:1], neg_half[:, 0:1], ALU.pow).then_inc(s["ln2_var"], 1)
                hold(pool, "ln2_var", at + 2)
                pool.tensor_scalar(m[:, 2:3], mv2[:, t, 0:1], -1.0, m[:, 1:2], ALU.mult, ALU.mult).then_inc(s["ln2_var"], 1)
                pool.tensor_scalar(m[:, 3:4], m[:, 1:2], t12[:, 1:2], 1.0, ALU.mult, ALU.add).then_inc(s["ln2_scales"], 1)
                hold(pool, "ln2_var", at + 3)
                pool.tensor_scalar(m[:, 4:5], m[:, 2:3], t12[:, 1:2], 1.0, ALU.mult, ALU.mult).then_inc(s["ln2_scales"], 1)

            def affine(c, t):
                hold(pool, "y_ready", c * T + t + 1)
                pool.tensor_scalar(x2[:, t, :], x2[:, t, :], small2[:, t, 3:4], small2[:, t, 4:5],
                                   ALU.mult, ALU.add).then_inc(s["aff_ready"], 1)

            def prologue():
                pool.wait_ge(s["tanh_ok"], 1)
                pool.wait_ge(s["tab_in"], 16)
                for half in (0, 1):
                    ln1(0, half)
                    xn(0, 0, half, False)
                for h in range(NH):
                    q_sine(0, 0, h)
                pool.wait_ge(s["flags_ok"], 1)

            def start(path):
                for k in range(path.blocks):
                    ctx_norm(0, path, k)
                    k_sines(0, path, k)
                normalize(path, 0, 0)

            def attention(path, b, cc, first, last):
                c = b * NC + cc
                if first:
                    pool.wait_ge(s["wo_ok"], NH)
                if not last:
                    ln1(c + 1, 0)
                    xn(c + 1, 1 - cc, 0, not first)
                if path.ahead:
                    normalize(path, c, 1)
                if not first:
                    affine(c - 1, T - 2)
                    affine(c - 1, T - 1)
                if not last:
                    ln1(c + 1, 1)
                    xn(c + 1, 1 - cc, 1, not first)
                if not path.ahead:
                    normalize(path, c, 1)
                normalize(path, c, 2)
                if path.ahead:
                    normalize(path, c, 3)
                if not last:
                    q_sine(c + 1, 1 - cc, 0)
                if not path.ahead:
                    normalize(path, c, 3)
                if not last:
                    q_sine(c + 1, 1 - cc, 1)

            def outputs(path, b, cc, new_keys, first, last):
                c, ncc = b * NC + cc, 1 - cc
                if not last:
                    q_sine(c + 1, ncc, 2)
                if new_keys:
                    ctx_norm(b + 1, path, 0)
                ln2(c, 0)
                if not last:
                    q_sine(c + 1, ncc, 3)
                if new_keys:
                    k_sines(b + 1, path, 0)
                    if path.blocks == 2:
                        ctx_norm(b + 1, path, 1)
                        k_sines(b + 1, path, 1)
                ln2(c, 1)
                if not last:
                    normalize(path, c + 1, 0)
                ln2(c, 2)
                ln2(c, 3)
                for t in range(T - 2):
                    affine(c, t)

            prologue()
            pipeline(pool, start, attention, outputs)
            affine(B * NC - 1, T - 2)
            affine(B * NC - 1, T - 1)

        @block.scalar
        def _(act):
            act.wait_ge(s["g_in"], 32)
            act.activation(t12[:, :], gates_in[:, :], ACT.Tanh).then_inc(s["tanh_ok"], 1)

            def hi(dst, src, wait, at, done, inc=1):
                act.wait_ge(s[wait], at)
                act.activation(dst, src, ACT.Copy).then_inc(s[done], inc)

            def tx_hi(n, tiles=range(T)):
                for t in tiles:
                    hi(xT[0][:, :, t * P:(t + 1) * P], tbank[t % 2][:, :].rearrange("p (k n) -> p k n", k=KC),
                       "tx_full", n * T + t + 1, "tx_hi")

            def ty_hi(c, tiles=range(T)):
                for t in tiles:
                    hi(xT[0][:, :, t * P:(t + 1) * P], tbank[t % 2][:, :].rearrange("p (k n) -> p k n", k=KC),
                       "ty_full", c * T + t + 1, "ty_hi")

            def q_swap_halves(n, h):
                act.wait_ge(s["q_full"], n * NH + h + 1)
                proj, swapped, _, _ = rotation(h)
                act.activation(swapped[0:64, :], proj[64:128, :], ACT.Copy).then_inc(s["q_swapped"], 1)
                act.activation(swapped[64:128, :], proj[0:64, :], ACT.Copy).then_inc(s["q_swapped"], 1)

            def q_high(n, h):
                act.wait_ge(s["q_sum"], n * NH + h + 1)
                act.activation(qT[0][:, h, :], rotation(h)[3], ACT.Copy).then_inc(s["q_hi"], 1)

            def exps(path, c, h):
                w = path.nk * P
                o = (h % 2) * 1024 if path.ahead else 0
                for qt in range(T):
                    i = h * T + qt
                    act.wait_ge(s["lg_min"], c * 16 + i + 1)
                    p = probs[:, o + qt * w:o + (qt + 1) * w]
                    act.activation(p, p, ACT.Exp, bias=lmin[:, i:i + 1], scale=-1.0,
                                   accum_out=lsum[:, i:i + 1]).then_inc(s["ex_done"], 1)

            def tp_high(path, c, h, kt):
                slot = (h % 2) * 2 + kt if path.ahead else kt % 4
                hi(pT[0][:, slot, :], tp[kt % 2][:, :], "tp_full", (c * NH + h) * 8 + (kt + 1) * path.unit, "tp_hi", path.unit)

            def pv_high(c, h):
                hi(eT[0][:, h, :], enc[:, :], "pv_full", c * NH + h + 1, "pv_hi")

            def y(c, t):
                act.wait_ge(s["ln2_scales"], (c * T + t) * 2 + 2)
                act.activation(norm[:, t, :], x2[:, t, :], ACT.Identity, bias=small2[:, t, 2:3],
                               scale=small2[:, t, 1:2]).then_inc(s["y_ready"], 1)

            def ctx_high(b, path, k):
                for j in range(path.bt):
                    kt = k * path.bt + j
                    hi(ctx_part(0, path)[:, :, j * P:(j + 1) * P], tbank[kt % 2][:, :].rearrange("p (k n) -> p k n", k=KC),
                       "tc_full", b * 8 + (kt + 1) * path.unit, "tc_hi", path.unit)

            def k_swap_halves(b, path, k):
                w = 2 // path.blocks
                n = path.bt * P
                act.wait_ge(s["k_full"], b * 2 + (k + 1) * w)
                act.activation(q_swap[0:64, 0:n], qbank[64:128, 0:n], ACT.Copy).then_inc(s["k_swapped"], w)
                act.activation(q_swap[64:128, 0:n], qbank[0:64, 0:n], ACT.Copy).then_inc(s["k_swapped"], w)

            def k_high(b, path, k):
                w = 2 // path.blocks
                n = path.bt * P
                at = b * 2 + (k + 1) * w
                act.wait_ge(s["k_sum"], at)
                act.activation(kT[0][:, k * n:(k + 1) * n], q_rot[:, 0:n], ACT.Copy).then_inc(s["k_hi"], w)

            def v_high(b, path, k):
                w = 2 // path.blocks
                n = path.bt * P
                hi(v[0][:, k * path.bt:(k + 1) * path.bt, :], enc[:, 0:n].rearrange("p (t n) -> p t n", n=HD),
                   "v_full", b * 2 + (k + 1) * w, "v_hi", w)

            def prologue():
                act.wait_ge(s["rms_ok"], 1)
                act.wait_ge(s["raw_w"], 16)
                for k in range(KC):
                    act.activation(wq[0][:, k, :].rearrange("p (h n) -> p h n", h=NH), raw_q[:, :, k, :], ACT.Copy,
                                   scale=rms1[:, k:k + 1]).then_inc(s["wq_hi"], 1)
                act.wait_ge(s["raw_kv_in"], 16)
                for k in range(KC):
                    act.activation(wkv[0][:, :, k, :], raw_kv[:, :, k, :], ACT.Copy,
                                   scale=rms1[:, k:k + 1]).then_inc(s["wkv_hi"], 1)
                tx_hi(0)
                for h in range(NH):
                    q_swap_halves(0, h)
                    q_high(0, h)
                act.wait_ge(s["flags_ok"], 1)

            def start(path):
                for k in range(path.blocks):
                    ctx_high(0, path, k)
                    k_swap_halves(0, path, k)
                    k_high(0, path, k)
                    v_high(0, path, k)
                exps(path, 0, 0)
                hi(wdn[0][:, :, :], tbank[0][:, :].rearrange("p (k n) -> p k n", k=KC), "dn_w_full", 1, "dn_w_hi")
                hi(wup[0][:, :], tbank[1][:, :], "up_w_full", 1, "up_w_hi")
                act.wait_ge(s["raw_w"], 32)
                for h in range(NH):
                    act.activation(wo[0][:, h, :], raw_o[:, h, :], ACT.Copy, scale=t12[:, 0:1]).then_inc(s["wo_hi"], 1)

            def router_exp(b):
                act.wait_ge(s["rt_neg"], b + 1)
                act.activation(rt[:, 3, :], rt[:, 0, :], ACT.Exp, bias=rt[:, 2, 0:1]).then_inc(s["rt_exp"], 1)

            def down_high(c):
                act.wait_ge(s["dn_full"], c + 1)
                act.activation(dT[0][:, :], qbank[:, :], ACT.Copy, scale=gate[:, 0:1]).then_inc(s["dn_hi"], 1)

            def attention(path, b, cc, first, last):
                c = b * NC + cc
                n = c + 1

                def exps_ahead(h):
                    if path.ahead:
                        exps(path, c, h)

                def weighted(h):
                    if not path.ahead:
                        for kt in range(path.nk):
                            tp_high(path, c, h, kt)
                    pv_high(c, h)
                    if not path.ahead and h < NH - 1:
                        exps(path, c, h + 1)

                def turned(h):
                    if path.ahead:
                        for kt in range(path.nk):
                            tp_high(path, c, h, kt)

                exps_ahead(1)
                turned(0)
                if not first:
                    ty_hi(c - 1, (0,))
                    y(c - 1, T - 2)
                    ty_hi(c - 1, (1,))
                    y(c - 1, T - 1)
                    ty_hi(c - 1, (2, 3))
                if cc:
                    router_exp(b)
                weighted(0)
                exps_ahead(2)
                turned(1)
                if not last:
                    tx_hi(n, (0, 1))
                if not first:
                    act.wait_ge(s["gate_ok"], b + cc)
                    down_high(c - 1)
                if not last:
                    tx_hi(n, (2, 3))
                weighted(1)
                exps_ahead(3)
                turned(2)
                for h in (0, 1):
                    if h:
                        turned(3)
                    if not last:
                        q_swap_halves(n, h)
                    if path.ahead:
                        weighted(2 + h)
                    if not last:
                        q_high(n, h)
                    if not path.ahead:
                        weighted(2 + h)

            def outputs(path, b, cc, new_keys, first, last):
                c = b * NC + cc
                if not last:
                    q_swap_halves(c + 1, 2)
                    if not new_keys:
                        q_high(c + 1, 2)
                    q_swap_halves(c + 1, 3)
                if new_keys:
                    ctx_high(b + 1, path, 0)
                    q_high(c + 1, 2)
                y(c, 0)
                if not last:
                    q_high(c + 1, 3)
                if new_keys:
                    k_swap_halves(b + 1, path, 0)
                    k_high(b + 1, path, 0)
                    v_high(b + 1, path, 0)
                    if path.blocks == 2:
                        ctx_high(b + 1, path, 1)
                        k_swap_halves(b + 1, path, 1)
                        k_high(b + 1, path, 1)
                        v_high(b + 1, path, 1)
                    y(c, 1)
                if not last:
                    exps(path, c + 1, 0)
                if not new_keys:
                    y(c, 1)

            prologue()
            pipeline(act, start, attention, outputs)
            y(B * NC - 1, T - 2)
            y(B * NC - 1, T - 1)
            ty_hi(B * NC - 1)
            down_high(B * NC - 1)

        @block.vector
        def _(dve):
            dve.sem_inc(s["fin_done"], T)

            def lo(dst, src, high, wait, at, done, inc=1):
                dve.wait_ge(s[wait], at)
                dve.tensor_tensor(dst, src, high.bitcast(F32), ALU.subtract).then_inc(s[done], inc)

            def ln1(b, cc, half):
                c = b * NC + cc
                tiles = range(half * T // 2, (half + 1) * T // 2)
                dve.wait_ge(s[f"x_in{cc}{'ab'[half]}"], b * 16 + 16)
                for t in tiles:
                    dve.bn_stats(st6[:, 0, t, :], xb[cc][:, t, :]).then_inc(s["ln1_bn"], 1)
                for t in tiles:
                    hold(dve, "ln1_bn", c * T + t + 1)
                    dve.bn_aggr(mv1[:, t, :], st6[:, 0, t, :]).then_inc(s["ln1_stats"], 1)

            def tx_lo(n, tiles=range(T)):
                for t in tiles:
                    lo(xT[1][:, :, t * P:(t + 1) * P], tbank[t % 2][:, :].rearrange("p (k n) -> p k n", k=KC),
                       xT[0][:, :, t * P:(t + 1) * P], "tx_hi", n * T + t + 1, "tx_done")

            def ty_lo(c, tiles=range(T)):
                for t in tiles:
                    lo(xT[1][:, :, t * P:(t + 1) * P], tbank[t % 2][:, :].rearrange("p (k n) -> p k n", k=KC),
                       xT[0][:, :, t * P:(t + 1) * P], "ty_hi", c * T + t + 1, "ty_done")

            def q_cos(n, ncc, h):
                i = n * NH + h
                if h == 3:
                    dve.wait_ge(s["q_done"], i - 1)
                elif not (isinstance(i, int) and i == 0):
                    dve.wait_ge(s["q_done"], i)
                dve.wait_ge(s["q_swapped"], (i + 1) * 2)
                proj, _, _, rotated = rotation(h)
                dve.tensor_tensor(rotated, proj, qtab[:, 0, ncc * CH:(ncc + 1) * CH], ALU.mult)\
                    .then_inc(s["q_cos_ok"], 1)

            def q_sum(n, h):
                i = n * NH + h
                dve.wait_ge(s["q_cos_ok"], i + 1)
                dve.wait_ge(s["q_sin_ok"], i + 1)
                _, _, sines, rotated = rotation(h)
                dve.tensor_tensor(rotated, rotated, sines, ALU.add).then_inc(s["q_sum"], 1)

            def q_low(n, h):
                i = n * NH + h
                dve.wait_ge(s["q_hi"], i + 1)
                dve.tensor_tensor(qT[1][:, h, :], rotation(h)[3], qT[0][:, h, :].bitcast(F32), ALU.subtract)\
                    .then_inc(s["q_done"], 1)

            def minima(path, c, h):
                w = path.nk * P
                o = (h % 2) * 1024 if path.ahead else 0
                for qt in range(T):
                    i = h * T + qt
                    src = lg[:, qt * w:(qt + 1) * w] if path.ahead else lg[:, :]
                    hold(dve, "lg_full", c * 16 + (i | 1 if path.ahead else i) + 1)
                    dve.tensor_tensor_reduce(probs[:, o + qt * w:o + (qt + 1) * w], src, bias[:, 0:w], 1.0, 3.4e38,
                                             ALU.add, ALU.min, lmin[:, i:i + 1]).then_inc(s["lg_min"], 1)

            def inverses(c, h):
                dve.wait_ge(s["ex_done"], c * 16 + (h + 1) * T)
                dve.reciprocal(lrec[:, h * T:(h + 1) * T], lsum[:, h * T:(h + 1) * T]).then_inc(s["rec_done"], 1)

            def tp_low(path, c, h, kt):
                slot = (h % 2) * 2 + kt if path.ahead else kt % 4
                lo(pT[1][:, slot, :], tp[kt % 2][:, :], pT[0][:, slot, :], "tp_hi",
                   (c * NH + h) * 8 + (kt + 1) * path.unit, "tp_done", path.unit)

            def pv_low(c, h):
                lo(eT[1][:, h, :], enc[:, :], eT[0][:, h, :], "pv_hi", c * NH + h + 1, "pv_done")

            def residual(c, cc, t, first):
                if not first:
                    dve.wait_ge(s["stored"], c * 16)
                dve.wait_ge(s["op_full"], c * T + t + 1)
                dve.tensor_tensor(x2[:, t, :], tp[t % 2][:, :], xb[cc][:, t, :], ALU.add)\
                    .then_inc(s["res_done"], 1)

            def ln2_stats(c, t):
                dve.wait_ge(s["res_done"], c * T + t + 1)
                dve.bn_stats(st6[:, 1, t, :], x2[:, t, :]).then_inc(s["ln2_bn"], 1)
                hold(dve, "ln2_bn", c * T + t + 1)
                dve.bn_aggr(mv2[:, t, :], st6[:, 1, t, :]).then_inc(s["ln2_stats"], 1)

            def ctx_stats(b, path, k):
                w = 2 // path.blocks
                dve.wait_ge(s["ctx_in_s"], 16 * (b * 2 + (k + 1) * w))
                for j in range(path.bt):
                    kt = k * path.bt + j
                    dve.bn_stats(st6[:, 2, j, :], ctx_raw[:, j, :]).then_inc(s["ctx_bn"], path.unit)
                    hold(dve, "ctx_bn", b * 8 + (kt + 1) * path.unit)
                    dve.bn_aggr(mvc[:, kt, :], st6[:, 2, j, :]).then_inc(s["ctx_stats"], path.unit)

            def mask_bias(b, path):
                m = path.nk * P
                dve.wait_ge(s["mask_b_in"], (b + 1) * 16)
                dve.tensor_scalar(bias[:, 0:m], mask_u8[:, 0:m], -FILL, FILL, ALU.mult, ALU.add)\
                    .then_inc(s["bias_ok"], 1)

            def ctx_low(b, path, k):
                for j in range(path.bt):
                    kt = k * path.bt + j
                    lo(ctx_part(1, path)[:, :, j * P:(j + 1) * P], tbank[kt % 2][:, :].rearrange("p (k n) -> p k n", k=KC),
                       ctx_part(0, path)[:, :, j * P:(j + 1) * P], "tc_hi", b * 8 + (kt + 1) * path.unit, "tc_done", path.unit)

            def k_cos(b, path, k, rotations):
                w = 2 // path.blocks
                n = path.bt * P
                at = b * 2 + (k + 1) * w
                if k:
                    dve.wait_ge(s["k_done"], at - w)
                dve.wait_ge(s["q_done"], rotations)
                dve.wait_ge(s["k_swapped"], at * 2)
                dve.wait_ge(s["ktab_in"], 16 * at)
                dve.tensor_tensor(q_rot[:, 0:n], qbank[:, 0:n], ktab[:, 0, 0:n], ALU.mult).then_inc(s["k_cos"], w)

            def k_low(b, path, k):
                w = 2 // path.blocks
                n = path.bt * P
                at = b * 2 + (k + 1) * w
                dve.wait_ge(s["k_cos"], at)
                dve.wait_ge(s["k_sin"], at)
                dve.tensor_tensor(q_rot[:, 0:n], q_rot[:, 0:n], q_sin[:, 0:n], ALU.add).then_inc(s["k_sum"], w)
                dve.wait_ge(s["k_hi"], at)
                dve.tensor_tensor(kT[1][:, k * n:(k + 1) * n], q_rot[:, 0:n],
                                  kT[0][:, k * n:(k + 1) * n].bitcast(F32), ALU.subtract).then_inc(s["k_done"], w)

            def v_low(b, path, k):
                w = 2 // path.blocks
                n = path.bt * P
                lo(v[1][:, k * path.bt:(k + 1) * path.bt, :], enc[:, 0:n].rearrange("p (t n) -> p t n", n=HD),
                   v[0][:, k * path.bt:(k + 1) * path.bt, :], "v_hi", b * 2 + (k + 1) * w, "v_done", w)

            LINKS = (1, 6, 5)

            def chain(b, part):
                n = [sum(LINKS[:part])]

                def link(ins):
                    n[0] += 1
                    ins.then_inc(s["gate_step"], 1)
                    hold(dve, "gate_step", b * sum(LINKS) + n[0])
                return link

            def router_max(b):
                link = chain(b, 0)
                l = rt[:, 0, :]
                dve.wait_ge(s["rt_full"], b + 1)
                dve.tensor_copy(l, qbank[:, 0:E]).then_inc(s["rt_read"], 1)
                hold(dve, "rt_read", b + 1)
                link(dve.max(rt[:, 1, :], l))
                dve.tensor_scalar(rt[:, 2, 0:1], rt[:, 1, 0:1], -1.0, None, ALU.mult).then_inc(s["rt_neg"], 1)

            def router_rank(b):
                link = chain(b, 1)
                l = rt[:, 0, :]
                mine = l.rearrange("p (e o) -> p e o", o=1).to_broadcast([P, E, E])
                other = l.rearrange("p (o e) -> p o e", o=1).to_broadcast([P, E, E])
                link(dve.tensor_tensor(cmp[:, 0], other, mine, ALU.is_gt))
                link(dve.tensor_tensor(cmp[:, 1], other, mine, ALU.is_equal))
                link(dve.tensor_tensor(cmp[:, 2], cmp[:, 1], lower[:, :, :], ALU.mult))
                link(dve.tensor_tensor(cmp[:, 1], cmp[:, 0], cmp[:, 2], ALU.add))
                link(dve.tensor_reduce(rt[:, 4, :], cmp[:, 1], AX.X, ALU.add))
                link(dve.tensor_scalar(rt[:, 5, :], rt[:, 4, :], TOPK - 0.5, None, ALU.is_lt))

            def router_gate(b):
                link = chain(b, 2)
                dve.wait_ge(s["rt_exp"], b + 1)
                link(dve.tensor_tensor(rt[:, 6, :], rt[:, 3, :], rt[:, 5, :], ALU.mult))
                link(dve.tensor_reduce(rt[:, 7, 0:1], rt[:, 6, :], AX.X, ALU.add))
                link(dve.tensor_tensor(rt[:, 8, :], rt[:, 6, :], own[:, :], ALU.mult))
                link(dve.tensor_reduce(rt[:, 7, 1:2], rt[:, 8, :], AX.X, ALU.add))
                link(dve.reciprocal(rt[:, 7, 2:3], rt[:, 7, 0:1]))
                dve.scalar_tensor_tensor(out=gate[:, 0:1], in0=rt[:, 7, 1:2], scalar=rt[:, 7, 2:3],
                                         in1=t12[:, 1:2], op0=ALU.mult, op1=ALU.mult).then_inc(s["gate_ok"], 1)

            def down_low(gates, c):
                dve.wait_ge(s["gate_ok"], gates)
                dve.wait_ge(s["dn_hi"], c + 1)
                dve.scalar_tensor_tensor(out=dT[1][:, :], in0=qbank[:, :], scalar=gate[:, 0:1], in1=dT[0][:, :].bitcast(F32),
                                         op0=ALU.mult, op1=ALU.subtract).then_inc(s["dn_done"], 1)

            def final(c, t):
                dve.wait_ge(s["up_full"], c * T + t + 1)
                dve.wait_ge(s["aff_ready"], c * T + t + 1)
                dve.tensor_tensor(x2[:, t, :], tbank[t % 2][:, :], x2[:, t, :], ALU.add)\
                    .then_inc(s["fin_done"], 1)

            def split_scaled(raw, dst, high, scale, wait, at, done):
                dve.wait_ge(s[wait], at)
                dve.scalar_tensor_tensor(out=dst, in0=raw, scalar=scale, in1=high.bitcast(F32),
                                         op0=ALU.mult, op1=ALU.subtract).then_inc(s[done], 1)

            def path_flags():
                f = flag_f[:, :].rearrange("o (a b g) -> o a b g", a=3, b=B)
                count = [0]

                def link(ins):
                    count[0] += 1
                    ins.then_inc(s["flag_step"], 1)
                    dve.wait_ge(s["flag_step"], count[0])

                dve.wait_ge(s["mask_in"], 16)
                link(dve.tensor_reduce(f[:, 0], mask_row.rearrange("o (b g k) -> o b g k", b=B, g=NG), AX.X, ALU.max))
                for g in range(NG):
                    link(dve.tensor_scalar(f[:, 1, :, g], f[:, 0, :, g], float(g), None, ALU.mult))
                link(dve.tensor_reduce(f[:, 2, :, 0], f[:, 0], AX.X, ALU.add))
                link(dve.tensor_reduce(f[:, 2, :, 1], f[:, 1], AX.X, ALU.add))
                link(dve.tensor_scalar(f[:, 2, :, 2], f[:, 2, :, 1], float(NG - 1), None, ALU.min))
                o = flags[:, :].rearrange("o (b a) -> o b a", a=2)
                link(dve.tensor_scalar(o[:, :, 0], f[:, 2, :, 0], 1.0, None, ALU.not_equal))
                dve.tensor_copy(o[:, :, 1], f[:, 2, :, 2]).then_inc(s["flags_ok"], 1)

            def prologue():
                path_flags()
                ln1(0, 0, 0)
                ln1(0, 0, 1)
                dve.wait_ge(s["aux_full"], 1)
                aux = tbank[0][:, 0:KC * E].rearrange("p (k n) -> p k n", k=KC)
                dve.tensor_scalar(rms1[:, :], tbank[1][:, 0:KC], 1.0, None, ALU.add).then_inc(s["rms_ok"], 1)
                dve.tensor_copy(wrt[0][:, :, :], aux).then_inc(s["rt_ok"], 1)
                dve.wait_ge(s["rt_ok"], 1)
                dve.tensor_tensor(wrt[1][:, :, :], aux, wrt[0][:, :, :].bitcast(F32), ALU.subtract)\
                    .then_inc(s["rt_ok"], 1)
                dve.wait_ge(s["rms_ok"], 1)
                for k in range(KC):
                    split_scaled(raw_q[:, :, k, :], wq[1][:, k, :].rearrange("p (h n) -> p h n", h=NH),
                                 wq[0][:, k, :].rearrange("p (h n) -> p h n", h=NH), rms1[:, k:k + 1], "wq_hi", k + 1, "wq_ok")
                tx_lo(0)
                for k in range(KC):
                    split_scaled(raw_kv[:, :, k, :], wkv[1][:, :, k, :], wkv[0][:, :, k, :], rms1[:, k:k + 1],
                                 "wkv_hi", k + 1, "wkv_ok")
                dve.wait_ge(s["tab_in"], 16)
                for h in range(NH):
                    q_cos(0, 0, h)
                    q_sum(0, h)
                    q_low(0, h)

            def start(path):
                for k in range(path.blocks):
                    ctx_stats(0, path, k)
                    ctx_low(0, path, k)
                    k_cos(0, path, k, NH)
                    k_low(0, path, k)
                    v_low(0, path, k)
                dve.wait_ge(s["const_ok"], 1)
                mask_bias(0, path)
                minima(path, 0, 0)
                inverses(0, 0)
                lo(wdn[1][:, :, :], tbank[0][:, :].rearrange("p (k n) -> p k n", k=KC), wdn[0][:, :, :], "dn_w_hi", 1, "dn_w_ok")
                lo(wup[1][:, :], tbank[1][:, :], wup[0][:, :], "up_w_hi", 1, "up_w_ok")
                for h in range(NH):
                    split_scaled(raw_o[:, h, :], wo[1][:, h, :], wo[0][:, h, :], t12[:, 0:1], "wo_hi", h + 1, "wo_ok")

            def attention(path, b, cc, first, last):
                c = b * NC + cc
                n = c + 1
                ncc = 1 - cc

                def turned(h):
                    if path.ahead:
                        for kt in range(path.nk):
                            tp_low(path, c, h, kt)

                def minima_ahead(h):
                    if path.ahead:
                        minima(path, c, h)

                def inverses_ahead(h):
                    if path.ahead:
                        inverses(c, h)

                def weighted(h):
                    if not path.ahead:
                        for kt in range(path.nk):
                            tp_low(path, c, h, kt)
                    pv_low(c, h)
                    if not path.ahead and h < NH - 1:
                        minima(path, c, h + 1)
                        inverses(c, h + 1)

                minima_ahead(1)
                turned(0)
                inverses_ahead(1)
                if not first:
                    ty_lo(c - 1, (0, 1))
                if not last:
                    ln1(b + cc, ncc, 0)
                if not first:
                    ty_lo(c - 1, (2, 3))
                if cc:
                    router_max(b)
                if not last:
                    ln1(b + cc, ncc, 1)
                weighted(0)
                minima_ahead(2)
                turned(1)
                if cc:
                    router_rank(b)
                inverses_ahead(2)
                if not last:
                    tx_lo(n, (0, 1))
                if cc:
                    router_gate(b)
                if not first:
                    down_low(b + cc, c - 1)
                if not last:
                    tx_lo(n, (2, 3))
                weighted(1)
                minima_ahead(3)
                turned(2)
                if not first:
                    final(c - 1, 0)
                    final(c - 1, 1)
                inverses_ahead(3)
                if not last:
                    q_cos(n, ncc, 0)
                if not first:
                    final(c - 1, 2)
                    final(c - 1, 3)
                for h in (0, 1):
                    if h:
                        turned(3)
                        if not last:
                            q_cos(n, ncc, 1)
                    if path.ahead:
                        if not last and h == 0:
                            q_sum(n, 0)
                        weighted(2 + h)
                        if not last and h == 1:
                            q_sum(n, 1)
                    elif not last:
                        q_sum(n, h)
                    if not last:
                        q_low(n, h)
                    if not path.ahead:
                        weighted(2 + h)

            def outputs(path, b, cc, new_keys, first, last):
                c, n = b * NC + cc, b * NC + cc + 1

                def residual_stats(t):
                    residual(c, cc, t, first)
                    ln2_stats(c, t)

                if new_keys:
                    ctx_stats(b + 1, path, 0)
                if not last:
                    q_cos(n, 1 - cc, 2)
                if new_keys:
                    mask_bias(b + 1, path)
                residual_stats(0)
                if not last:
                    q_sum(n, 2)
                    if not new_keys:
                        q_low(n, 2)
                    q_cos(n, 1 - cc, 3)
                if new_keys:
                    ctx_low(b + 1, path, 0)
                    q_low(n, 2)
                if not last:
                    q_sum(n, 3)
                    q_low(n, 3)
                if new_keys:
                    residual_stats(1)
                    k_cos(b + 1, path, 0, (n + 1) * NH)
                    k_low(b + 1, path, 0)
                    v_low(b + 1, path, 0)
                    if path.blocks == 2:
                        ctx_stats(b + 1, path, 1)
                        ctx_low(b + 1, path, 1)
                        k_cos(b + 1, path, 1, (n + 1) * NH)
                        k_low(b + 1, path, 1)
                        v_low(b + 1, path, 1)
                    residual_stats(2)
                    minima(path, n, 0)
                else:
                    residual_stats(1)
                    if not last:
                        minima(path, n, 0)
                    residual_stats(2)
                if not last:
                    inverses(n, 0)
                residual_stats(3)

            prologue()
            pipeline(dve, start, attention, outputs)
            ty_lo(B * NC - 1)
            down_low(B, B * NC - 1)
            for t in range(T):
                final(B * NC - 1, t)

        @block.tensor
        def _(pe):
            def product(dst, a, b, steps):
                last = None
                for i in range(steps):
                    for j, (p, q) in enumerate(((0, 0), (0, 1), (1, 0))):
                        last = pe.matmul(dst, a(p, i), b(q, i), start=(i == 0 and j == 0),
                                         stop=(i == steps - 1 and j == 2), skip_group_check=True)
                return last

            def turn(dst, src, n=P):
                return pe.transpose(dst, src, ident[0:n, 0:n])

            def turn_norm(t, full):
                for k in range(KC):
                    last = turn(tbank[t % 2][:, k * P:(k + 1) * P], norm[:, t, k * P:(k + 1) * P])
                last.then_inc(s[full], 1)

            def tx(n):
                for t in range(T):
                    if t >= 2:
                        pe.wait_ge(s["tx_done"], n * T + t - 1)
                    pe.wait_ge(s["xn_ready"], n * T + t + 1)
                    turn_norm(t, "tx_full")

            def ty(c):
                for t in range(T):
                    if t < 2:
                        pe.wait_ge(s["fin_done"], c * T + T)
                    else:
                        pe.wait_ge(s["ty_done"], c * T + t - 1)
                    pe.wait_ge(s["y_ready"], c * T + t + 1)
                    turn_norm(t, "ty_full")

            def router(b, c):
                pe.wait_ge(s["ty_done"], c * T + 1)
                product(qbank[:, 0:E], lambda p, k: xT[p][:, k, 0:1].to_broadcast([P, P]),
                        lambda q, k: wrt[q][:, k, :], KC).then_inc(s["rt_full"], 1)

            def down(c, batch=None):
                pe.wait_ge(s["ty_done"], (c + 1) * T)
                if batch is not None:
                    pe.wait_ge(s["rt_read"], batch + 1)
                product(qbank[:, :], lambda p, k: wdn[p][:, k, :], lambda q, k: xT[q][:, k, :], KC)\
                    .then_inc(s["dn_full"], 1)

            def up(c, tiles=range(T)):
                for t in tiles:
                    if t < 2:
                        pe.wait_ge(s["dn_done"], c + 1)
                    else:
                        pe.wait_ge(s["fin_done"], T + c * T + t - 1)
                    product(tbank[t % 2][:, :], lambda p, _: dT[p][:, t * P:(t + 1) * P],
                            lambda q, _: wup[q][:, :], 1).then_inc(s["up_full"], 1)

            def q_proj(n, h):
                pe.wait_ge(s["tx_done"], (n + 1) * T)
                start = isinstance(n, int) and n == 0
                if h < 2 and not (start and h == 0):
                    pe.wait_ge(s["q_swapped"], (n * NH + h) * 2)
                    pe.wait_ge(s["q_cos_ok"], n * NH + h)
                elif h >= 2 and not start:
                    pe.wait_ge(s["lg_min"], n * 16)
                product(rotation(h)[0], lambda p, k: wq[p][:, k, h * HD:(h + 1) * HD],
                        lambda q, k: xT[q][:, k, :], KC).then_inc(s["q_full"], 1)

            def first_logits(path, n):
                pe.wait_ge(s["q_swapped"], (n + 1) * NH * 2)
                pe.wait_ge(s["q_cos_ok"], (n + 1) * NH)
                pe.wait_ge(s["q_done"], n * NH + 3)
                logits(path, n, 0)

            def logits(path, c, h):
                w = path.nk * P
                pe.wait_ge(s["q_done"], c * NH + h + 1)
                for qt in range(T):
                    i = c * 16 + h * T + qt
                    if h or qt:
                        if path.ahead and h and qt % 2 == 0:
                            pe.wait_ge(s["lg_min"], i - T + 2)
                        elif not path.ahead:
                            pe.wait_ge(s["lg_min"], i)
                    for half in range(max(1, w // 512)):
                        n = min(w, 512)
                        dst = lg[:, qt * w:(qt + 1) * w] if path.ahead else lg[:, half * n:(half + 1) * n]
                        last = product(dst, lambda p, _: qT[p][:, h, qt * P:(qt + 1) * P],
                                       lambda q, _: kT[q][:, half * n:(half + 1) * n], 1)
                    last.then_inc(s["lg_full"], 1)

            def turn_probs(path, c, h, kt, first):
                w = path.nk * P
                o = (h % 2) * 1024 if path.ahead else 0
                at = (c * NH + h) * 8
                if path.ahead and h:
                    pe.wait_ge(s["tp_done"], at - 4 + 4 * kt)
                elif not path.ahead and kt >= 2:
                    pe.wait_ge(s["tp_done"], at + kt - 1)
                elif not path.ahead and h:
                    pe.wait_ge(s["tp_done"], at)
                elif not first:
                    pe.wait_ge(s["res_done"], c * T)
                for qt in range(T):
                    pe.wait_ge(s["nrm_done"], c * 16 + h * T + qt + 1)
                    last = turn(tp[kt % 2][:, qt * P:(qt + 1) * P], probs[:, o + qt * w + kt * P:o + qt * w + (kt + 1) * P])
                last.then_inc(s["tp_full"], path.unit)

            def weigh_values(path, c, h, kt):
                slot = (h % 2) * 2 + kt if path.ahead else kt % 4
                pe.wait_ge(s["tp_done"], (c * NH + h) * 8 + (kt + 1) * path.unit)
                if kt == 0:
                    if not (isinstance(c, int) and c * NH + h == 0):
                        pe.wait_ge(s["pv_done"], c * NH + h)
                for j, (p, q) in enumerate(((0, 0), (0, 1), (1, 0))):
                    last = pe.matmul(enc[:, :], v[p][:, kt, :], pT[q][:, slot, :], start=(kt == 0 and j == 0),
                                     stop=(kt == path.nk - 1 and j == 2), skip_group_check=True)
                if kt == path.nk - 1:
                    last.then_inc(s["pv_full"], 1)

            def attention(path, b, cc, first, last):
                c = b * NC + cc
                n = c + 1

                def others(h):
                    if h == 0 and not first:
                        ty(c - 1)
                        if cc:
                            router(b, c - 1)
                    if h == 1:
                        if not first:
                            down(c - 1, b if cc else None)
                        if not last:
                            tx(n)
                    if h == 2:
                        if not first:
                            if not last:
                                pe.wait_ge(s["tx_done"], (n + 1) * T)
                            up(c - 1, (0, 1))
                        if not last:
                            q_proj(n, 0)
                        if not first:
                            up(c - 1, (2, 3))
                    if h == 3 and not last:
                        q_proj(n, 1)

                for h in range(NH):
                    if path.ahead:
                        if h < NH - 1:
                            logits(path, c, h + 1)
                        for kt in range(path.nk):
                            turn_probs(path, c, h, kt, first)
                        others(h)
                        for kt in range(path.nk):
                            weigh_values(path, c, h, kt)
                    else:
                        others(h)
                        turn_probs(path, c, h, 0, first)
                        for kt in range(1, path.nk):
                            turn_probs(path, c, h, kt, first)
                            weigh_values(path, c, h, kt - 1)
                        weigh_values(path, c, h, path.nk - 1)
                        if h < NH - 1:
                            logits(path, c, h + 1)

            def out_proj(c, t):
                if t < 2:
                    pe.wait_ge(s["wo_ok"], NH)
                    pe.wait_ge(s["tp_done"], (c + 1) * NH * 8)
                    pe.wait_ge(s["pv_done"], (c + 1) * NH)
                else:
                    pe.wait_ge(s["res_done"], c * T + t - 1)
                product(tp[t % 2][:, :], lambda p, h: eT[p][:, h, t * P:(t + 1) * P],
                        lambda q, h: wo[q][:, h, :], NH).then_inc(s["op_full"], 1)

            def turn_ctx(b, path, k):
                for j in range(path.bt):
                    kt = k * path.bt + j
                    pe.wait_ge(s["ctx_normed"], b * 8 + (kt + 1) * path.unit)
                    if kt >= 2:
                        pe.wait_ge(s["tc_done"], b * 8 + (kt - 1) * path.unit)
                    for kk in range(KC):
                        last = turn(tbank[kt % 2][:, kk * P:(kk + 1) * P], ctx_raw[:, j, kk * P:(kk + 1) * P])
                    last.then_inc(s["tc_full"], path.unit)

            def k_proj(b, path, k, rotations):
                w = 2 // path.blocks
                n = path.bt * P
                pe.wait_ge(s["tc_done"], b * 8 + (k + 1) * path.bt * path.unit)
                if k:
                    pe.wait_ge(s["k_cos"], b * 2 + k)
                else:
                    pe.wait_ge(s["q_cos_ok"], rotations)
                product(qbank[:, 0:n], lambda p, kk: wkv[p][:, 0, kk, :], lambda q, kk: ctx_part(q, path)[:, kk, :], KC)\
                    .then_inc(s["k_full"], w)

            def v_proj(b, path, k):
                w = 2 // path.blocks
                if k:
                    pe.wait_ge(s["v_done"], b * 2 + k)
                for j in range(path.bt):
                    last = product(enc[:, j * P:(j + 1) * P], lambda p, kk: ctx_part(p, path)[:, kk, j * P:(j + 1) * P],
                                   lambda q, kk: wkv[q][:, 1, kk, :], KC)
                last.then_inc(s["v_full"], w)

            def keys_there(b):
                pe.wait_ge(s["k_done"], (b + 1) * 2)
                pe.wait_ge(s["v_done"], (b + 1) * 2)
                pe.wait_ge(s["bias_ok"], b + 1)

            def outputs(path, b, cc, new_keys, first, last):
                c, n = b * NC + cc, b * NC + cc + 1
                if not last:
                    q_proj(n, 2)
                out_proj(c, 0)
                if not last:
                    q_proj(n, 3)
                if new_keys:
                    pe.wait_ge(s["fin_done"], n * T)
                    turn_ctx(b + 1, path, 0)
                out_proj(c, 1)
                if new_keys:
                    k_proj(b + 1, path, 0, n * NH + 2)
                    v_proj(b + 1, path, 0)
                    if path.blocks == 2:
                        turn_ctx(b + 1, path, 1)
                        k_proj(b + 1, path, 1, None)
                        v_proj(b + 1, path, 1)
                    out_proj(c, 2)
                    keys_there(b + 1)
                    first_logits(path, n)
                else:
                    if not last:
                        first_logits(path, n)
                    out_proj(c, 2)
                out_proj(c, 3)

            pe.wait_ge(s["ident_ok"], 1)
            pe.wait_ge(s["raw_aux_in"], 32)
            for k in range(KC):
                pe.transpose(tbank[0][:, k * E:(k + 1) * E], raw_router[:, k * P:(k + 1) * P], ident[0:E, 0:E])
            pe.transpose(tbank[1][:, 0:KC], raw_rms, ident[0:KC, 0:KC]).then_inc(s["aux_full"], 1)
            pe.wait_ge(s["rt_ok"], 2)
            pe.wait_ge(s["rms_ok"], 1)
            tx(0)
            pe.wait_ge(s["wq_ok"], KC)
            for h in range(NH):
                q_proj(0, h)
            pe.wait_ge(s["wkv_ok"], KC)
            pe.wait_ge(s["flags_ok"], 1)

            def start(path):
                for k in range(path.blocks):
                    turn_ctx(0, path, k)
                    k_proj(0, path, k, 2)
                    v_proj(0, path, k)
                keys_there(0)
                first_logits(path, 0)
                pe.wait_ge(s["raw_dn_in"], 16)
                pe.wait_ge(s["raw_up_in"], 16 * KC)
                for k in range(KC):
                    last = turn(tbank[0][:, k * P:(k + 1) * P], raw_dn[:, k * P:(k + 1) * P])
                last.then_inc(s["dn_w_full"], 1)
                for k in range(KC):
                    last = turn(tbank[1][:, k * P:(k + 1) * P], raw_up[:, k, :])
                last.then_inc(s["up_w_full"], 1)
                pe.wait_ge(s["dn_w_ok"], 1)
                pe.wait_ge(s["up_w_ok"], 1)

            pipeline(pe, start, attention, outputs)
            ty(B * NC - 1)
            down(B * NC - 1)
            up(B * NC - 1)


_INS = ["x", "ctx_1024", "mask_BxS2_bk0", "g_xattn", "g_ffn", "L0_xattn_rms_scale", "L0_xattn_q_w",
        "L0_xattn_kv_w", "L0_xattn_out_w", "L0_ffn_router_w", "L0_ffn_lora_down", "L0_ffn_lora_up"]
_OUT = ((B, S, D), "float32")


def kernel(**inputs):
    import numpy as _np
    import concourse.bacc as _bacc
    from concourse import mybir as _mybir
    from concourse.bass_utils import run_bass_kernel_spmd as _run

    nc = _bacc.Bacc("TRN2", target_bir_lowering=False, num_devices=1)
    arrays, args = {}, []

    def give(name, a):
        arrays[name] = a
        args.append(nc.dram_tensor(name, a.shape, _mybir.dt.from_np(a.dtype), kind="ExternalInput").ap())

    for name in _INS:
        a = _np.ascontiguousarray(inputs[name])
        give(f"in_{name}_dram", a)
    for name, a in zip(("q_table", "k_table"), rope_tables()):
        give(f"in_{name}_dram", a)
    shape, dtype = _OUT
    args.append(nc.dram_tensor("out_dram", shape, _mybir.dt.from_np(_np.dtype(dtype)), kind="ExternalOutput").ap())
    gated_block(nc, *args)
    r = _run(nc, [arrays], core_ids=[0])
    return r.results[0]["out_dram"]
```

```python
from contextlib import ExitStack

import numpy as np

import concourse.bass as bass
from concourse import mybir

F32 = mybir.dt.float32
F32R = mybir.dt.float32r
U8 = mybir.dt.uint8
I32 = mybir.dt.int32
ALU = mybir.AluOpType
ACT = mybir.ActivationFunctionType
AX = mybir.AxisListType

P = 128
B, S, D = 4, 1024, 512
NH, HD = 4, 128
E, R, TOPK = 8, 16, 2
ER = E * R
KC = D // P
CH = 512
NC = S // CH
T = CH // P
GK = 256
NG = S // GK
FILL = 2.3819763e38
LN_EPS = 1e-5
RMS_EPS = 1e-6


def rope_tables():
    half = HD // 2
    freq = np.float32(2.0 / HD) * np.arange(half, dtype=np.float32)
    timescale = (np.float32(10000.0) ** freq).astype(np.float32)
    pos = np.arange(2 * S, dtype=np.float32)
    rad = (pos[None, :] / timescale[:, None]).astype(np.float32)
    cos = np.cos(rad).astype(np.float32)
    sin = np.sin(rad).astype(np.float32)
    cos = np.concatenate([cos, cos], 0)
    sin = np.concatenate([-sin, sin], 0)
    scale = np.float32(-float(HD) ** -0.5)
    keys = np.stack([cos[:, :S], sin[:, :S]], 1)
    queries = np.stack([cos[:, S:] * scale, sin[:, S:] * scale], 1)
    return np.ascontiguousarray(queries), np.ascontiguousarray(keys)


def gated_block(nc, x, ctx_in, mask, g_xattn, g_ffn, rms_scale, q_w, kv_w, out_w, router_w,
                lora_down, lora_up, q_table, k_table, out):
    stack = ExitStack()
    with stack:
        def sb(name, shape, dt=F32):
            return stack.enter_context(nc.sbuf_tensor(name, shape, dt))

        def sem(name):
            return stack.enter_context(nc.semaphore(name))

        wq = [sb(f"wq_{p}", [P, KC, NH * HD], F32R) for p in "hl"]
        wkv = [sb(f"wkv_{p}", [P, 2, KC, HD], F32R) for p in "hl"]
        wo = [sb(f"wo_{p}", [P, NH, D], F32R) for p in "hl"]
        wdn = [sb(f"wdn_{p}", [P, KC, ER], F32R) for p in "hl"]
        wup = [sb(f"wup_{p}", [P, D], F32R) for p in "hl"]
        wrt = [sb(f"wrt_{p}", [P, KC, E], F32R) for p in "hl"]
        qtab = sb("qtab", [P, 2, S])
        ktab = sb("ktab", [P, 2, CH])
        ident = sb("ident", [P, P])
        own = sb("own", [P, E])
        lower = sb("lower", [P, E, E])
        neg_half = sb("neg_half", [P, T])
        gates_in = sb("gates_in", [P, 2])
        t12 = sb("t12", [P, 2])
        rms1 = sb("rms1", [P, KC])
        xb = [sb(f"x_{i}", [P, T, D]) for i in range(NC)]
        norm = sb("norm", [P, T, D])
        xT = [sb(f"xT_{p}", [P, KC, CH], F32R) for p in "hl"]
        qT = [sb(f"qT_{p}", [P, NH, CH], F32R) for p in "hl"]
        kT = [sb(f"kT_{p}", [P, S], F32R) for p in "hl"]
        v = [sb(f"v_{p}", [P, S // P, HD], F32R) for p in "hl"]
        q_swap = sb("q_swap", [P, CH])
        q_sin = sb("q_sin", [P, CH])
        q_rot = sb("q_rot", [P, CH])
        probs = sb("probs", [P, 4 * S])
        pT = [sb(f"pT_{p}", [P, 4, CH], F32R) for p in "hl"]
        eT = [sb(f"eT_{p}", [P, KC, CH], F32R) for p in "hl"]
        dT = [sb(f"dT_{p}", [P, CH], F32R) for p in "hl"]
        x2 = sb("x2", [P, T, D])
        bias = sb("bias", [P, S])
        mask_u8 = sb("mask_u8", [P, S], U8)
        st6 = sb("st6", [P, 3, T, 6])
        mv1 = sb("mv1", [P, T, 2])
        var1 = sb("var1", [P, T])
        rs1 = sb("rs1", [P, T])
        nm1 = sb("nm1", [P, T])
        mv2 = sb("mv2", [P, T, 2])
        small2 = sb("small2", [P, T, 5])
        mvc = sb("mvc", [P, 8, 2])
        smallc = sb("smallc", [P, 8, 3])
        lmin = sb("lmin", [P, NH * T])
        lsum = sb("lsum", [P, NH * T])
        lrec = sb("lrec", [P, NH * T])
        rt = sb("rt", [P, 16, E])
        cmp = sb("cmp", [P, 3, E, E])
        gate = sb("gate", [P, 1])
        flag_f = sb("flag_f", [B, 2, NG + 2])
        flags_b = sb("flags_b", [B, 2], I32)
        flags = sb("flags", [1, 2 * B], I32)

        bank = [stack.enter_context(nc.psum_tensor(f"bank{i}", [P, 512], F32)) for i in range(3)]
        lg = stack.enter_context(nc.psum_tensor("lg", [P, 1024], F32))
        tp = [stack.enter_context(nc.psum_tensor(f"tp{i}", [P, 512], F32)) for i in range(2)]
        enc = stack.enter_context(nc.psum_tensor("enc", [P, 512], F32))
        tbank, qbank = bank[0:2], bank[2]

        raw_q = probs[:, 0:2048].rearrange("p (h k n) -> p h k n", h=NH, k=KC)
        raw_o = norm[:, :, :]
        raw_kv = x2[:, 0:2, :].rearrange("p c (k n) -> p c k n", k=KC)
        raw_dn = x2[:, 2, :]
        raw_up = x2[:, 3, :].rearrange("p (k n) -> p k n", k=KC)
        raw_router = q_swap[0:E, :]
        raw_rms = q_sin[0:KC, 0:P]
        ctxT = [p.rearrange("p s n -> p (s n)") for p in (pT[0][:, :, :], pT[1][:, :, :])]

        def keys_bank(b):
            return tbank[0] if is_start(b) else qbank

        def ctx_part(p, path):
            n = path.bt * P
            return ctxT[p][:, 0:KC * n].rearrange("p (k n) -> p k n", k=KC)

        ctx_raw = probs[:, 2048:4096].rearrange("p (t d) -> p t d", t=4)
        mask_rows = bias[0:B, 0:S // 4].bitcast(U8)

        names = """passed g_in raw_w raw_kv_in raw_dn_in raw_up_in raw_aux_in tab_in mask_in ident_ok const_ok tanh_ok
            aux_full rms_ok rt_ok dn_w_full dn_w_hi dn_w_ok up_w_full up_w_hi up_w_ok wq_hi wq_ok wo_hi wo_ok
            wkv_hi wkv_ok flags_ok flag_step const_step
            x_in0a x_in0b x_in1a x_in1b ln1_bn ln1_stats ln1_scales xn_ready tx_full tx_hi tx_done ty_full ty_hi ty_done
            q_full q_swapped q_sin_ok q_cos_ok q_sum q_hi q_done
            lg_full lg_min ex_done rec_done nrm_done tp_full tp_hi tp_done pv_full pv_hi pv_done
            op_full res_done ln2_bn ln2_stats ln2_var ln2_scales y_ready aff_ready up_full fin_done stored
            rt_full rt_read rt_neg gate_step compared rank_step rank_ok rt_exp gate_ok dn_full dn_hi dn_done
            ctx_in_s ktab_in mask_b_in bias_ok ctx_bn ctx_stats ctx_rms ctx_inv ctx_normed tc_full tc_hi tc_done
            k_full k_swapped k_sin k_cos k_sum k_hi k_done v_full v_hi v_done"""
        s = {n: sem("s_" + n) for n in names.split()}
        block = stack.enter_context(nc.Block())

        FLAG_STEPS = NG + 5

        def is_start(n):
            return isinstance(n, int) and n == 0

        def rotation(n, h):
            if is_start(n):
                return (qbank, tp[0], tp[1], qbank)[h][:, :], q_swap[:, :], q_sin[:, :], q_rot[:, :]
            proj = (qbank[:, :], qbank[:, :], lg[:, 0:512], lg[:, 512:1024])[h]
            if h == 2:
                return proj, probs[:, 0:512], probs[:, 1024:1536], probs[:, 1536:2048]
            return proj, q_swap[:, :], q_sin[:, :], q_rot[:, :]

        def hold(eng, name, value):
            eng.wait_ge(s[name], value)
            eng.sem_inc(s["passed"], 1)

        def load_path(eng, b):
            return eng.value_load(flags[0:1, bass.ds(2 * b, 1)], min_val=0, max_val=1)

        def load_group(eng, b):
            return eng.value_load(flags[0:1, bass.ds(2 * b + 1, 1)], min_val=0, max_val=NG - 1)

        def either(eng, long_path, body):
            with eng.If(long_path == 0):
                body(SHORT)
            with eng.Else():
                body(LONG)

        class SHORT:
            nk = GK // P
            unit = 4
            blocks = 1
            bt = GK // P
            ahead = True

        class LONG:
            nk = S // P
            unit = 1
            blocks = 2
            bt = 4
            ahead = False

        def pipeline(eng, start, attention, outputs):
            def batch(path, b, first, last):
                if first:
                    start(path)
                else:
                    outputs(path, b - 1, NC - 1, True, False, False)
                attention(path, b, 0, first, False)
                outputs(path, b, 0, False, first, False)
                attention(path, b, 1, False, last)
                if last:
                    outputs(path, b, 1, False, False, True)

            lp = load_path(eng, 0)
            either(eng, lp, lambda path: batch(path, 0, True, False))
            with eng.Fori(1, B - 1) as b:
                lp = load_path(eng, b)
                either(eng, lp, lambda path: batch(path, b, False, False))
            lp = load_path(eng, B - 1)
            either(eng, lp, lambda path: batch(path, B - 1, False, True))

        @block.sync
        def _(sp):
            def rows(t, b, cc, first, n):
                start = (b * NC + cc) * T + first
                return t.rearrange("(c p) d -> p c d", p=P)[:, bass.ds(start, n), :]

            x_rows = x.rearrange("b s d -> (b s) d")
            out_rows = out.rearrange("b s d -> (b s) d")
            x_in = [[s[f"x_in{cc}{half}"] for half in "ab"] for cc in range(NC)]

            def load_x(b, cc, half):
                tiles = slice(half * T // 2, (half + 1) * T // 2)
                sp.dma_start(xb[cc][:, tiles, :], rows(x_rows, b, cc, half * T // 2, T // 2)).then_inc(x_in[cc][half], 16)

            def load_ctx(b, long_path, group):
                def body(path):
                    n = path.nk * P
                    first = group * GK if path is SHORT else 0
                    sp.dma_start(mask_u8[:, 0:n], mask[bass.ds(b, 1), bass.ds(first, n)].to_broadcast([P, n]))\
                        .then_inc(s["mask_b_in"], 16)
                    n = path.bt * P
                    for k in range(path.blocks):
                        first = group * GK if path is SHORT else k * n
                        if k:
                            sp.wait_ge(s["tc_full"], b * 8 + 4)
                            sp.wait_ge(s["k_sum"], b * 2 + 1)
                        sp.dma_start(ctx_raw[:, 0:path.bt, :],
                                     ctx_in[bass.ds(b, 1), bass.ds(first, n), :]
                                     .rearrange("o (t p) d -> p (o t) d", p=P)).then_inc(s["ctx_in_s"], 16 * (2 // path.blocks))
                        sp.dma_start(ktab[:, :, 0:n], k_table[:, :, bass.ds(first, n)]).then_inc(s["ktab_in"], 16 * (2 // path.blocks))
                either(sp, long_path, body)

            sp.dma_start(mask_rows, mask).then_inc(s["mask_in"], 16)
            load_x(0, 0, 0)
            load_x(0, 0, 1)
            sp.dma_start(raw_router, router_w).then_inc(s["raw_aux_in"], 16)
            sp.dma_start(raw_rms, rms_scale.rearrange("(k p) -> k p", p=P)).then_inc(s["raw_aux_in"], 16)
            sp.dma_start(raw_q.rearrange("p h k n -> p (h k) n"),
                         q_w.rearrange("h (k p) n -> p (h k) n", p=P)).then_inc(s["raw_w"], 16)
            sp.dma_start(raw_kv.rearrange("p c k n -> p (c k) n"),
                         kv_w.rearrange("c o (k p) n -> p (c o k) n", p=P)).then_inc(s["raw_kv_in"], 16)
            sp.dma_start(qtab[:, :, :], q_table).then_inc(s["tab_in"], 16)
            sp.wait_ge(s["flag_step"], FLAG_STEPS)
            for b in range(B):
                sp.dma_start(flags[:, 2 * b:2 * b + 2], flags_b[b:b + 1, :]).then_inc(s["flags_ok"], 16)
            sp.wait_ge(s["flags_ok"], 16 * B)
            load_ctx(0, load_path(sp, 0), load_group(sp, 0))
            load_x(0, 1, 0)
            load_x(0, 1, 1)
            sp.dma_start(raw_dn, lora_down.rearrange("e r d -> (e r) d")).then_inc(s["raw_dn_in"], 16)
            for k in range(KC):
                sp.dma_start(raw_up[:, k, :].rearrange("p (e r) -> p e r", e=E),
                             lora_up[:, k * P:(k + 1) * P, :].rearrange("e p r -> p e r")).then_inc(s["raw_up_in"], 16)
            sp.wait_ge(s["tx_full"], T)
            sp.dma_start(raw_o, out_w.rearrange("h p n -> p h n")).then_inc(s["raw_w"], 16)

            def store(c):
                sp.wait_ge(s["fin_done"], (c + 1) * T + T)
                sp.dma_start(out_rows.rearrange("(c p) d -> p c d", p=P)[:, bass.ds(c * T, T), :], x2[:, :, :])\
                    .then_inc(s["stored"], 16)

            def step(b, cc, first=False, last=False):
                c = b * NC + cc
                if not (first or last):
                    for half in (0, 1):
                        sp.wait_ge(s["res_done"], (c - 1) * T + (half + 1) * T // 2)
                        load_x(b + cc, 1 - cc, half)
                if not first:
                    store(c - 1)
                if cc == NC - 1 and not last:
                    lp_now = load_path(sp, b)
                    lp_next, g_next = load_path(sp, b + 1), load_group(sp, b + 1)
                    hold(sp, "k_done", (b + 1) * 2)
                    with sp.If(lp_now == 0):
                        hold(sp, "bias_ok", b + 1)
                    with sp.Else():
                        hold(sp, "tp_full", (c + 1) * NH * 8)
                    load_ctx(b + 1, lp_next, g_next)

            step(0, 0, first=True)
            with sp.Fori(0, B - 1) as b:
                step(b, 1)
                step(b + 1, 0)
            step(B - 1, 1, last=True)
            store(B * NC - 1)
            sp.wait_ge(s["stored"], 16 * B * NC)

        @block.gpsimd
        def _(pool):
            pool.dma_start(gates_in[:, 0:1], g_xattn.rearrange("(o n) -> o n", o=1).to_broadcast([P, 1])).then_inc(s["g_in"], 16)
            pool.dma_start(gates_in[:, 1:2], g_ffn.rearrange("(o n) -> o n", o=1).to_broadcast([P, 1])).then_inc(s["g_in"], 16)
            pool.memset(ident[:, :], 0.0).then_inc(s["const_step"], 1)
            pool.memset(neg_half[:, :], -0.5).then_inc(s["const_step"], 1)
            pool.memset(own[:, :], 1.0).then_inc(s["const_step"], 1)
            pool.memset(lower[:, :, :], 1.0).then_inc(s["const_step"], 1)
            pool.wait_ge(s["const_step"], 4)
            pool.affine_select(out=ident[:, :], in_=ident[:, :], compare_op=ALU.not_equal, fill=1.0, base=0,
                               pattern=[[-1, P]], channel_multiplier=1).then_inc(s["ident_ok"], 1)
            pool.affine_select(out=own[:, :], in_=own[:, :], compare_op=ALU.is_ge, fill=0.0, base=0,
                               pattern=[[-R, E]], channel_multiplier=1).then_inc(s["const_step"], 1)
            pool.wait_ge(s["const_step"], 5)
            pool.affine_select(out=own[:, :], in_=own[:, :], compare_op=ALU.is_ge, fill=0.0, base=R - 1,
                               pattern=[[R, E]], channel_multiplier=-1).then_inc(s["const_step"], 1)
            pool.affine_select(out=lower[:, :, :], in_=lower[:, :, :], compare_op=ALU.is_ge, fill=0.0, base=-1,
                               pattern=[[1, E], [-1, E]], channel_multiplier=0).then_inc(s["const_step"], 1)
            pool.wait_ge(s["const_step"], 7)
            pool.drain().then_inc(s["const_ok"], 1)
            def ln1(c, half):
                two = slice(half * T // 2, (half + 1) * T // 2)
                at = c * 6 + half * 3
                hold(pool, "ln1_stats", c * T + (half + 1) * T // 2)
                pool.tensor_scalar(var1[:, two], mv1[:, two, 1], 1.0 + RMS_EPS, LN_EPS * RMS_EPS, ALU.mult, ALU.add)\
                    .then_inc(s["ln1_scales"], 1)
                pool.tensor_scalar(nm1[:, two], mv1[:, two, 0], -1.0, 0.0, ALU.mult, ALU.add).then_inc(s["ln1_scales"], 1)
                pool.wait_ge(s["ln1_scales"], at + 2)
                pool.tensor_tensor(rs1[:, two], var1[:, two], neg_half[:, two], ALU.pow).then_inc(s["ln1_scales"], 1)

            def xn(c, cc, half, reuse):
                hold(pool, "ln1_scales", c * 6 + half * 3 + 3)
                for t in range(half * T // 2, (half + 1) * T // 2):
                    if reuse:
                        hold(pool, "ty_full", (c - 2) * T + t + 1)
                    pool.tensor_scalar(norm[:, t, :], xb[cc][:, t, :], nm1[:, t:t + 1], rs1[:, t:t + 1],
                                       ALU.add, ALU.mult).then_inc(s["xn_ready"], 1)

            def normalize(path, c, h):
                w = path.nk * P
                o = (h % 2) * 1024 if path.ahead else 0
                hold(pool, "rec_done", c * NH + h + 1)
                for qt in range(T):
                    p = probs[:, o + qt * w:o + (qt + 1) * w]
                    pool.tensor_scalar(p, p, lrec[:, h * T + qt:h * T + qt + 1], 1.0, ALU.mult, ALU.mult)\
                        .then_inc(s["nrm_done"], 1)

            def ctx_norm(b, path, k):
                w = 2 // path.blocks
                t0 = k * path.bt
                at = b * 6 + k * 3
                m, var = mvc[:, t0:t0 + path.bt, 0], mvc[:, t0:t0 + path.bt, 1]
                square, total, inv = (smallc[:, t0:t0 + path.bt, i] for i in range(3))
                pool.wait_ge(s["ctx_stats"], b * 8 + (t0 + path.bt) * path.unit)
                pool.tensor_tensor(square, m, m, ALU.mult).then_inc(s["ctx_rms"], w)
                pool.wait_ge(s["ctx_rms"], at + w)
                pool.tensor_tensor(total, square, var, ALU.add).then_inc(s["ctx_rms"], w)
                hold(pool, "ctx_rms", at + 2 * w)
                pool.tensor_scalar(total, total, RMS_EPS, 1.0, ALU.add, ALU.mult).then_inc(s["ctx_rms"], w)
                pool.wait_ge(s["ctx_rms"], at + 3 * w)
                pool.tensor_tensor(inv, total, neg_half[:, 0:path.bt], ALU.pow).then_inc(s["ctx_inv"], w)
                hold(pool, "ctx_inv", b * 2 + (k + 1) * w)
                for j in range(path.bt):
                    pool.tensor_scalar(ctx_raw[:, j, :], ctx_raw[:, j, :], smallc[:, t0 + j, 2:3], 1.0,
                                       ALU.mult, ALU.mult).then_inc(s["ctx_normed"], path.unit)

            def k_sines(b, path, k):
                n = path.bt * P
                w = 2 // path.blocks
                pool.wait_ge(s["k_swapped"], b * 4 + (k + 1) * w * 2)
                pool.wait_ge(s["ktab_in"], 16 * (b * 2 + (k + 1) * w))
                pool.tensor_tensor(q_sin[:, 0:n], q_swap[:, 0:n], ktab[:, 1, 0:n], ALU.mult).then_inc(s["k_sin"], w)

            def router_rank(b):
                n = [0]

                def link(ins):
                    n[0] += 1
                    ins.then_inc(s["rank_step"], 1)
                    pool.wait_ge(s["rank_step"], b * 4 + n[0])

                pool.wait_ge(s["compared"], 2 * (b + 1))
                link(pool.tensor_tensor(cmp[:, 2], cmp[:, 1], lower[:, :, :], ALU.mult))
                link(pool.tensor_tensor(cmp[:, 1], cmp[:, 0], cmp[:, 2], ALU.add))
                link(pool.tensor_tensor(cmp[:, 0, :, 0:4], cmp[:, 1, :, 0:4], cmp[:, 1, :, 4:8], ALU.add))
                link(pool.tensor_tensor(cmp[:, 0, :, 4:6], cmp[:, 0, :, 0:2], cmp[:, 0, :, 2:4], ALU.add))
                pool.tensor_tensor(rt[:, 4, :].rearrange("p (e o) -> p e o", o=1), cmp[:, 0, :, 4:5], cmp[:, 0, :, 5:6],
                                   ALU.add).then_inc(s["rank_ok"], 1)

            def q_sine(n, ncc, h):
                pool.wait_ge(s["q_swapped"], (n * NH + h + 1) * 2)
                _, swapped, sines, _ = rotation(n, h)
                pool.tensor_tensor(sines, swapped, qtab[:, 1, ncc * CH:(ncc + 1) * CH], ALU.mult)\
                    .then_inc(s["q_sin_ok"], 1)

            def ln2(c, t):
                m = small2[:, t, :]
                at = (c * T + t) * 3
                hold(pool, "ln2_stats", c * T + t + 1)
                pool.tensor_scalar(m[:, 0:1], mv2[:, t, 1:2], LN_EPS, 1.0, ALU.add, ALU.mult).then_inc(s["ln2_var"], 1)
                pool.wait_ge(s["ln2_var"], at + 1)
                pool.tensor_tensor(m[:, 1:2], m[:, 0:1], neg_half[:, 0:1], ALU.pow).then_inc(s["ln2_var"], 1)
                hold(pool, "ln2_var", at + 2)
                pool.tensor_scalar(m[:, 2:3], mv2[:, t, 0:1], -1.0, m[:, 1:2], ALU.mult, ALU.mult).then_inc(s["ln2_var"], 1)
                pool.tensor_scalar(m[:, 3:4], m[:, 1:2], t12[:, 1:2], 1.0, ALU.mult, ALU.add).then_inc(s["ln2_scales"], 1)
                hold(pool, "ln2_var", at + 3)
                pool.tensor_scalar(m[:, 4:5], m[:, 2:3], t12[:, 1:2], 1.0, ALU.mult, ALU.mult).then_inc(s["ln2_scales"], 1)

            def affine(c, t):
                hold(pool, "y_ready", c * T + t + 1)
                pool.tensor_scalar(x2[:, t, :], x2[:, t, :], small2[:, t, 3:4], small2[:, t, 4:5],
                                   ALU.mult, ALU.add).then_inc(s["aff_ready"], 1)

            def prologue():
                pool.wait_ge(s["tanh_ok"], 1)
                for half in (0, 1):
                    ln1(0, half)
                    xn(0, 0, half, False)
                pool.wait_ge(s["flags_ok"], 16 * B)

            def start(path):
                ctx_norm(0, path, 0)
                pool.wait_ge(s["tab_in"], 16)
                q_sine(0, 0, 0)
                k_sines(0, path, 0)
                if path.blocks == 2:
                    ctx_norm(0, path, 1)
                    k_sines(0, path, 1)
                q_sine(0, 0, 1)
                normalize(path, 0, 0)
                q_sine(0, 0, 2)
                q_sine(0, 0, 3)

            def attention(path, b, cc, first, last):
                c = b * NC + cc
                if first:
                    pool.wait_ge(s["wo_ok"], NH)
                if path.ahead:
                    normalize(path, c, 1)
                if not last:
                    ln1(c + 1, 0)
                    xn(c + 1, 1 - cc, 0, not first)
                if cc:
                    router_rank(b)
                if not last:
                    ln1(c + 1, 1)
                    xn(c + 1, 1 - cc, 1, not first)
                if not path.ahead:
                    normalize(path, c, 1)
                normalize(path, c, 2)
                if not first:
                    for t in range(1, T):
                        affine(c - 1, t)
                if path.ahead:
                    normalize(path, c, 3)
                if not last:
                    q_sine(c + 1, 1 - cc, 0)
                if not path.ahead:
                    normalize(path, c, 3)
                if not last:
                    q_sine(c + 1, 1 - cc, 1)

            def outputs(path, b, cc, new_keys, first, last):
                c, ncc = b * NC + cc, 1 - cc
                if not last:
                    q_sine(c + 1, ncc, 2)
                if new_keys:
                    ctx_norm(b + 1, path, 0)
                ln2(c, 0)
                if not last:
                    q_sine(c + 1, ncc, 3)
                if new_keys:
                    k_sines(b + 1, path, 0)
                    if path.blocks == 2:
                        ctx_norm(b + 1, path, 1)
                        k_sines(b + 1, path, 1)
                if new_keys or last:
                    ln2(c, 1)
                if not last:
                    normalize(path, c + 1, 0)
                    if not new_keys:
                        ln2(c, 1)
                ln2(c, 2)
                ln2(c, 3)
                affine(c, 0)

            prologue()
            pipeline(pool, start, attention, outputs)
            for t in range(1, T):
                affine(B * NC - 1, t)

        @block.scalar
        def _(act):
            act.wait_ge(s["g_in"], 32)
            act.activation(t12[:, :], gates_in[:, :], ACT.Tanh).then_inc(s["tanh_ok"], 1)

            def hi(dst, src, wait, at, done, inc=1):
                act.wait_ge(s[wait], at)
                act.activation(dst, src, ACT.Copy).then_inc(s[done], inc)

            def tx_hi(n, tiles=range(T)):
                for t in tiles:
                    hi(xT[0][:, :, t * P:(t + 1) * P], tbank[t % 2][:, :].rearrange("p (k n) -> p k n", k=KC),
                       "tx_full", n * T + t + 1, "tx_hi")

            def ty_hi(c, tiles=range(T)):
                for t in tiles:
                    hi(xT[0][:, :, t * P:(t + 1) * P], tbank[t % 2][:, :].rearrange("p (k n) -> p k n", k=KC),
                       "ty_full", c * T + t + 1, "ty_hi")

            def q_swap_halves(n, h):
                act.wait_ge(s["q_full"], n * NH + h + 1)
                proj, swapped, _, _ = rotation(n, h)
                act.activation(swapped[0:64, :], proj[64:128, :], ACT.Copy).then_inc(s["q_swapped"], 1)
                act.activation(swapped[64:128, :], proj[0:64, :], ACT.Copy).then_inc(s["q_swapped"], 1)

            def q_high(n, h):
                act.wait_ge(s["q_sum"], n * NH + h + 1)
                act.activation(qT[0][:, h, :], rotation(n, h)[3], ACT.Copy).then_inc(s["q_hi"], 1)

            def exps(path, c, h, tiles=range(T)):
                w = path.nk * P
                o = (h % 2) * 1024 if path.ahead else 0
                for qt in tiles:
                    i = h * T + qt
                    act.wait_ge(s["lg_min"], c * 16 + i + 1)
                    p = probs[:, o + qt * w:o + (qt + 1) * w]
                    act.activation(p, p, ACT.Exp, bias=lmin[:, i:i + 1], scale=-1.0,
                                   accum_out=lsum[:, i:i + 1]).then_inc(s["ex_done"], 1)

            def tp_high(path, c, h, kt):
                slot = (h % 2) * 2 + kt if path.ahead else kt % 4
                hi(pT[0][:, slot, :], tp[kt % 2][:, :], "tp_full", (c * NH + h) * 8 + (kt + 1) * path.unit, "tp_hi", path.unit)

            def pv_high(c, h):
                hi(eT[0][:, h, :], enc[:, :], "pv_full", c * NH + h + 1, "pv_hi")

            def y(c, t):
                act.wait_ge(s["ln2_scales"], (c * T + t) * 2 + 2)
                act.activation(norm[:, t, :], x2[:, t, :], ACT.Identity, bias=small2[:, t, 2:3],
                               scale=small2[:, t, 1:2]).then_inc(s["y_ready"], 1)

            def ctx_high(b, path, k):
                for j in range(path.bt):
                    kt = k * path.bt + j
                    hi(ctx_part(0, path)[:, :, j * P:(j + 1) * P], tbank[kt % 2][:, :].rearrange("p (k n) -> p k n", k=KC),
                       "tc_full", b * 8 + (kt + 1) * path.unit, "tc_hi", path.unit)

            def k_swap_halves(b, path, k):
                w = 2 // path.blocks
                n = path.bt * P
                act.wait_ge(s["k_full"], b * 2 + (k + 1) * w)
                bank = keys_bank(b)
                act.activation(q_swap[0:64, 0:n], bank[64:128, 0:n], ACT.Copy).then_inc(s["k_swapped"], w)
                act.activation(q_swap[64:128, 0:n], bank[0:64, 0:n], ACT.Copy).then_inc(s["k_swapped"], w)

            def k_high(b, path, k):
                w = 2 // path.blocks
                n = path.bt * P
                at = b * 2 + (k + 1) * w
                act.wait_ge(s["k_sum"], at)
                act.activation(kT[0][:, k * n:(k + 1) * n], q_rot[:, 0:n], ACT.Copy).then_inc(s["k_hi"], w)

            def v_high(b, path, k):
                w = 2 // path.blocks
                n = path.bt * P
                hi(v[0][:, k * path.bt:(k + 1) * path.bt, :], enc[:, 0:n].rearrange("p (t n) -> p t n", n=HD),
                   "v_full", b * 2 + (k + 1) * w, "v_hi", w)

            def prologue():
                act.wait_ge(s["rms_ok"], 1)
                act.wait_ge(s["raw_w"], 16)
                for k in range(KC):
                    act.activation(wq[0][:, k, :].rearrange("p (h n) -> p h n", h=NH), raw_q[:, :, k, :], ACT.Copy,
                                   scale=rms1[:, k:k + 1]).then_inc(s["wq_hi"], 1)
                tx_hi(0)
                act.wait_ge(s["raw_kv_in"], 16)
                for k in range(KC):
                    act.activation(wkv[0][:, :, k, :], raw_kv[:, :, k, :], ACT.Copy,
                                   scale=rms1[:, k:k + 1]).then_inc(s["wkv_hi"], 1)
                act.wait_ge(s["flags_ok"], 16 * B)

            def start(path):
                q_swap_halves(0, 0)
                q_high(0, 0)
                for k in range(path.blocks):
                    ctx_high(0, path, k)
                    k_swap_halves(0, path, k)
                    k_high(0, path, k)
                    if path.blocks == 2:
                        v_high(0, path, k)
                act.wait_ge(s["raw_w"], 32)
                for h in range(NH):
                    act.activation(wo[0][:, h, :], raw_o[:, h, :], ACT.Copy, scale=t12[:, 0:1]).then_inc(s["wo_hi"], 1)
                q_swap_halves(0, 1)
                exps(path, 0, 0)
                q_high(0, 1)
                hi(wdn[0][:, :, :], tbank[0][:, :].rearrange("p (k n) -> p k n", k=KC), "dn_w_full", 1, "dn_w_hi")
                hi(wup[0][:, :], tbank[1][:, :], "up_w_full", 1, "up_w_hi")
                if path.blocks == 1:
                    v_high(0, path, 0)
                for h in (2, 3):
                    q_swap_halves(0, h)
                    q_high(0, h)

            def router_exp(b):
                act.wait_ge(s["rt_neg"], b + 1)
                act.activation(rt[:, 3, :], rt[:, 0, :], ACT.Exp, bias=rt[:, 2, 0:1]).then_inc(s["rt_exp"], 1)

            def down_high(c):
                act.wait_ge(s["dn_full"], c + 1)
                act.activation(dT[0][:, :], qbank[:, :], ACT.Copy, scale=gate[:, 0:1]).then_inc(s["dn_hi"], 1)

            def attention(path, b, cc, first, last):
                c = b * NC + cc
                n = c + 1

                def exps_ahead(h, tiles=range(T)):
                    if path.ahead:
                        exps(path, c, h, tiles)

                def weighted(h):
                    if not path.ahead:
                        for kt in range(path.nk):
                            tp_high(path, c, h, kt)
                    pv_high(c, h)
                    if not path.ahead and h < NH - 1:
                        exps(path, c, h + 1)

                def turned(h):
                    if path.ahead:
                        for kt in range(path.nk):
                            tp_high(path, c, h, kt)

                exps_ahead(1, (0, 1))
                if cc:
                    y(c - 1, 1)
                turned(0)
                exps_ahead(1, (2, 3))
                if not first:
                    ty_hi(c - 1, (0,))
                    y(c - 1, T - 2)
                    ty_hi(c - 1, (1,))
                    y(c - 1, T - 1)
                    ty_hi(c - 1, (2, 3))
                if cc:
                    router_exp(b)
                weighted(0)
                exps_ahead(2)
                turned(1)
                if not last:
                    tx_hi(n)
                if not first:
                    act.wait_ge(s["gate_ok"], b + cc)
                    down_high(c - 1)
                weighted(1)
                exps_ahead(3, (0, 1))
                turned(2)
                exps_ahead(3, (2, 3))
                if path.ahead:
                    if not last:
                        q_swap_halves(n, 0)
                    weighted(2)
                    turned(3)
                    if not last:
                        q_high(n, 0)
                        q_swap_halves(n, 1)
                    weighted(3)
                    if not last:
                        q_high(n, 1)
                else:
                    for h in (0, 1):
                        if not last:
                            q_swap_halves(n, h)
                            q_high(n, h)
                        weighted(2 + h)

            def outputs(path, b, cc, new_keys, first, last):
                c = b * NC + cc
                if not last:
                    q_swap_halves(c + 1, 2)
                    if not new_keys:
                        q_high(c + 1, 2)
                    q_swap_halves(c + 1, 3)
                if new_keys:
                    ctx_high(b + 1, path, 0)
                    q_high(c + 1, 2)
                y(c, 0)
                if not last:
                    q_high(c + 1, 3)
                if new_keys:
                    k_swap_halves(b + 1, path, 0)
                    k_high(b + 1, path, 0)
                    v_high(b + 1, path, 0)
                    if path.blocks == 2:
                        ctx_high(b + 1, path, 1)
                        k_swap_halves(b + 1, path, 1)
                        k_high(b + 1, path, 1)
                        v_high(b + 1, path, 1)
                    y(c, 1)
                if not last:
                    exps(path, c + 1, 0)

            prologue()
            pipeline(act, start, attention, outputs)
            y(B * NC - 1, 1)
            y(B * NC - 1, 2)
            ty_hi(B * NC - 1, (0, 1))
            y(B * NC - 1, 3)
            ty_hi(B * NC - 1, (2, 3))
            down_high(B * NC - 1)

        @block.vector
        def _(dve):
            dve.sem_inc(s["fin_done"], T)

            def lo(dst, src, high, wait, at, done, inc=1):
                dve.wait_ge(s[wait], at)
                dve.tensor_tensor(dst, src, high.bitcast(F32), ALU.subtract).then_inc(s[done], inc)

            def ln1(b, cc, half):
                c = b * NC + cc
                tiles = range(half * T // 2, (half + 1) * T // 2)
                dve.wait_ge(s[f"x_in{cc}{'ab'[half]}"], b * 16 + 16)
                for t in tiles:
                    dve.bn_stats(st6[:, 0, t, :], xb[cc][:, t, :]).then_inc(s["ln1_bn"], 1)
                for t in tiles:
                    hold(dve, "ln1_bn", c * T + t + 1)
                    dve.bn_aggr(mv1[:, t, :], st6[:, 0, t, :]).then_inc(s["ln1_stats"], 1)

            def tx_lo(n, tiles=range(T)):
                for t in tiles:
                    lo(xT[1][:, :, t * P:(t + 1) * P], tbank[t % 2][:, :].rearrange("p (k n) -> p k n", k=KC),
                       xT[0][:, :, t * P:(t + 1) * P], "tx_hi", n * T + t + 1, "tx_done")

            def ty_lo(c, tiles=range(T)):
                for t in tiles:
                    lo(xT[1][:, :, t * P:(t + 1) * P], tbank[t % 2][:, :].rearrange("p (k n) -> p k n", k=KC),
                       xT[0][:, :, t * P:(t + 1) * P], "ty_hi", c * T + t + 1, "ty_done")

            def q_cos(n, ncc, h):
                i = n * NH + h
                if is_start(n) and h == 1:
                    dve.wait_ge(s["k_done"], 2)
                if h == 3 and not is_start(n):
                    dve.wait_ge(s["q_done"], i - 1)
                elif not is_start(i):
                    dve.wait_ge(s["q_done"], i)
                dve.wait_ge(s["q_swapped"], (i + 1) * 2)
                proj, _, _, rotated = rotation(n, h)
                dve.tensor_tensor(rotated, proj, qtab[:, 0, ncc * CH:(ncc + 1) * CH], ALU.mult)\
                    .then_inc(s["q_cos_ok"], 1)

            def q_sum(n, h):
                i = n * NH + h
                dve.wait_ge(s["q_cos_ok"], i + 1)
                dve.wait_ge(s["q_sin_ok"], i + 1)
                _, _, sines, rotated = rotation(n, h)
                dve.tensor_tensor(rotated, rotated, sines, ALU.add).then_inc(s["q_sum"], 1)

            def q_low(n, h):
                i = n * NH + h
                dve.wait_ge(s["q_hi"], i + 1)
                dve.tensor_tensor(qT[1][:, h, :], rotation(n, h)[3], qT[0][:, h, :].bitcast(F32), ALU.subtract)\
                    .then_inc(s["q_done"], 1)

            def minima(path, c, h):
                w = path.nk * P
                o = (h % 2) * 1024 if path.ahead else 0
                for qt in range(T):
                    i = h * T + qt
                    src = lg[:, qt * w:(qt + 1) * w] if path.ahead else lg[:, :]
                    hold(dve, "lg_full", c * 16 + (i | 1 if path.ahead else i) + 1)
                    dve.tensor_tensor_reduce(probs[:, o + qt * w:o + (qt + 1) * w], src, bias[:, 0:w], 1.0, 3.4e38,
                                             ALU.add, ALU.min, lmin[:, i:i + 1]).then_inc(s["lg_min"], 1)

            def inverses(c, h):
                dve.wait_ge(s["ex_done"], c * 16 + (h + 1) * T)
                dve.reciprocal(lrec[:, h * T:(h + 1) * T], lsum[:, h * T:(h + 1) * T]).then_inc(s["rec_done"], 1)

            def tp_low(path, c, h, kt):
                slot = (h % 2) * 2 + kt if path.ahead else kt % 4
                lo(pT[1][:, slot, :], tp[kt % 2][:, :], pT[0][:, slot, :], "tp_hi",
                   (c * NH + h) * 8 + (kt + 1) * path.unit, "tp_done", path.unit)

            def pv_low(c, h):
                lo(eT[1][:, h, :], enc[:, :], eT[0][:, h, :], "pv_hi", c * NH + h + 1, "pv_done")

            def residual(c, cc, t, first):
                if not first:
                    dve.wait_ge(s["stored"], c * 16)
                dve.wait_ge(s["op_full"], c * T + t + 1)
                dve.tensor_tensor(x2[:, t, :], tp[t % 2][:, :], xb[cc][:, t, :], ALU.add)\
                    .then_inc(s["res_done"], 1)

            def ln2_stats(c, t):
                dve.wait_ge(s["res_done"], c * T + t + 1)
                dve.bn_stats(st6[:, 1, t, :], x2[:, t, :]).then_inc(s["ln2_bn"], 1)
                hold(dve, "ln2_bn", c * T + t + 1)
                dve.bn_aggr(mv2[:, t, :], st6[:, 1, t, :]).then_inc(s["ln2_stats"], 1)

            def ctx_stats(b, path, k):
                w = 2 // path.blocks
                dve.wait_ge(s["ctx_in_s"], 16 * (b * 2 + (k + 1) * w))
                for j in range(path.bt):
                    kt = k * path.bt + j
                    dve.bn_stats(st6[:, 2, j, :], ctx_raw[:, j, :]).then_inc(s["ctx_bn"], path.unit)
                    hold(dve, "ctx_bn", b * 8 + (kt + 1) * path.unit)
                    dve.bn_aggr(mvc[:, kt, :], st6[:, 2, j, :]).then_inc(s["ctx_stats"], path.unit)

            def mask_bias(b, path):
                m = path.nk * P
                dve.wait_ge(s["mask_b_in"], (b + 1) * 16)
                dve.tensor_scalar(bias[:, 0:m], mask_u8[:, 0:m], -FILL, FILL, ALU.mult, ALU.add)\
                    .then_inc(s["bias_ok"], 1)

            def ctx_low(b, path, k):
                for j in range(path.bt):
                    kt = k * path.bt + j
                    lo(ctx_part(1, path)[:, :, j * P:(j + 1) * P], tbank[kt % 2][:, :].rearrange("p (k n) -> p k n", k=KC),
                       ctx_part(0, path)[:, :, j * P:(j + 1) * P], "tc_hi", b * 8 + (kt + 1) * path.unit, "tc_done", path.unit)

            def k_cos(b, path, k, rotations):
                w = 2 // path.blocks
                n = path.bt * P
                at = b * 2 + (k + 1) * w
                if k:
                    dve.wait_ge(s["k_done"], at - w)
                dve.wait_ge(s["q_done"], rotations)
                dve.wait_ge(s["k_swapped"], at * 2)
                dve.wait_ge(s["ktab_in"], 16 * at)
                dve.tensor_tensor(q_rot[:, 0:n], keys_bank(b)[:, 0:n], ktab[:, 0, 0:n], ALU.mult).then_inc(s["k_cos"], w)

            def k_low(b, path, k):
                w = 2 // path.blocks
                n = path.bt * P
                at = b * 2 + (k + 1) * w
                dve.wait_ge(s["k_cos"], at)
                dve.wait_ge(s["k_sin"], at)
                dve.tensor_tensor(q_rot[:, 0:n], q_rot[:, 0:n], q_sin[:, 0:n], ALU.add).then_inc(s["k_sum"], w)
                dve.wait_ge(s["k_hi"], at)
                dve.tensor_tensor(kT[1][:, k * n:(k + 1) * n], q_rot[:, 0:n],
                                  kT[0][:, k * n:(k + 1) * n].bitcast(F32), ALU.subtract).then_inc(s["k_done"], w)

            def v_low(b, path, k):
                w = 2 // path.blocks
                n = path.bt * P
                lo(v[1][:, k * path.bt:(k + 1) * path.bt, :], enc[:, 0:n].rearrange("p (t n) -> p t n", n=HD),
                   v[0][:, k * path.bt:(k + 1) * path.bt, :], "v_hi", b * 2 + (k + 1) * w, "v_done", w)

            STEPS = 6

            def router_max(b):
                l = rt[:, 0, :]
                dve.wait_ge(s["rt_full"], b + 1)
                dve.tensor_copy(l, qbank[:, 0:E]).then_inc(s["rt_read"], 1)
                hold(dve, "rt_read", b + 1)
                dve.max(rt[:, 1, :], l).then_inc(s["gate_step"], 1)
                mine = l.rearrange("p (e o) -> p e o", o=1).to_broadcast([P, E, E])
                other = l.rearrange("p (o e) -> p o e", o=1).to_broadcast([P, E, E])
                dve.tensor_tensor(cmp[:, 0], other, mine, ALU.is_gt).then_inc(s["compared"], 1)
                dve.tensor_tensor(cmp[:, 1], other, mine, ALU.is_equal).then_inc(s["compared"], 1)
                hold(dve, "gate_step", b * STEPS + 1)
                dve.tensor_scalar(rt[:, 2, 0:1], rt[:, 1, 0:1], -1.0, None, ALU.mult).then_inc(s["rt_neg"], 1)

            def router_gate(b):
                dve.wait_ge(s["rank_ok"], b + 1)
                dve.wait_ge(s["rt_exp"], b + 1)
                dve.scalar_tensor_tensor(out=rt[:, 6, :], in0=rt[:, 4, :], scalar=TOPK - 0.5, in1=rt[:, 3, :],
                                         op0=ALU.is_lt, op1=ALU.mult).then_inc(s["gate_step"], 1)
                hold(dve, "gate_step", b * STEPS + 2)
                dve.tensor_reduce(rt[:, 7, 0:1], rt[:, 6, :], AX.X, ALU.add).then_inc(s["gate_step"], 1)
                dve.tensor_tensor(rt[:, 8, :], rt[:, 6, :], own[:, :], ALU.mult).then_inc(s["gate_step"], 1)
                hold(dve, "gate_step", b * STEPS + 4)
                dve.tensor_reduce(rt[:, 7, 1:2], rt[:, 8, :], AX.X, ALU.add).then_inc(s["gate_step"], 1)
                dve.reciprocal(rt[:, 7, 2:3], rt[:, 7, 0:1]).then_inc(s["gate_step"], 1)
                hold(dve, "gate_step", b * STEPS + 6)
                dve.scalar_tensor_tensor(out=gate[:, 0:1], in0=rt[:, 7, 1:2], scalar=rt[:, 7, 2:3],
                                         in1=t12[:, 1:2], op0=ALU.mult, op1=ALU.mult).then_inc(s["gate_ok"], 1)

            def down_low(gates, c):
                dve.wait_ge(s["gate_ok"], gates)
                dve.wait_ge(s["dn_hi"], c + 1)
                dve.scalar_tensor_tensor(out=dT[1][:, :], in0=qbank[:, :], scalar=gate[:, 0:1], in1=dT[0][:, :].bitcast(F32),
                                         op0=ALU.mult, op1=ALU.subtract).then_inc(s["dn_done"], 1)

            def final(c, t):
                dve.wait_ge(s["up_full"], c * T + t + 1)
                dve.wait_ge(s["aff_ready"], c * T + t + 1)
                dve.tensor_tensor(x2[:, t, :], tbank[t % 2][:, :], x2[:, t, :], ALU.add)\
                    .then_inc(s["fin_done"], 1)

            def split_scaled(raw, dst, high, scale, wait, at, done):
                dve.wait_ge(s[wait], at)
                dve.scalar_tensor_tensor(out=dst, in0=raw, scalar=scale, in1=high.bitcast(F32),
                                         op0=ALU.mult, op1=ALU.subtract).then_inc(s[done], 1)

            def path_flags():
                attended, number = flag_f[:, 0, :], flag_f[:, 1, :]
                count = [0]

                def link(ins):
                    count[0] += 1
                    ins.then_inc(s["flag_step"], 1)
                    dve.wait_ge(s["flag_step"], count[0])

                dve.wait_ge(s["mask_in"], 16)
                link(dve.tensor_reduce(attended[:, 0:NG], mask_rows.rearrange("b (g k) -> b g k", g=NG), AX.X, ALU.max))
                for g in range(NG):
                    link(dve.tensor_scalar(number[:, g:g + 1], attended[:, g:g + 1], float(g), None, ALU.mult))
                link(dve.tensor_reduce(flag_f[:, :, NG], flag_f[:, :, 0:NG], AX.X, ALU.add))
                link(dve.tensor_scalar(number[:, NG + 1:NG + 2], number[:, NG:NG + 1], float(NG - 1), None, ALU.min))
                link(dve.tensor_scalar(flags_b[:, 0:1], attended[:, NG:NG + 1], 1.0, None, ALU.not_equal))
                link(dve.tensor_copy(flags_b[:, 1:2], number[:, NG + 1:NG + 2]))
                assert count[0] == FLAG_STEPS

            def prologue():
                path_flags()
                dve.wait_ge(s["aux_full"], 1)
                aux = tbank[0][:, 0:KC * E].rearrange("p (k n) -> p k n", k=KC)
                dve.tensor_scalar(rms1[:, :], tbank[1][:, 0:KC], 1.0, None, ALU.add).then_inc(s["rms_ok"], 1)
                ln1(0, 0, 0)
                ln1(0, 0, 1)
                dve.tensor_copy(wrt[0][:, :, :], aux).then_inc(s["rt_ok"], 1)
                dve.wait_ge(s["rt_ok"], 1)
                dve.tensor_tensor(wrt[1][:, :, :], aux, wrt[0][:, :, :].bitcast(F32), ALU.subtract)\
                    .then_inc(s["rt_ok"], 1)
                dve.wait_ge(s["rms_ok"], 1)
                for k in range(KC):
                    split_scaled(raw_q[:, :, k, :], wq[1][:, k, :].rearrange("p (h n) -> p h n", h=NH),
                                 wq[0][:, k, :].rearrange("p (h n) -> p h n", h=NH), rms1[:, k:k + 1], "wq_hi", k + 1, "wq_ok")
                tx_lo(0)
                for k in range(KC):
                    split_scaled(raw_kv[:, :, k, :], wkv[1][:, :, k, :], wkv[0][:, :, k, :], rms1[:, k:k + 1],
                                 "wkv_hi", k + 1, "wkv_ok")
                dve.wait_ge(s["const_ok"], 1)
                dve.wait_ge(s["flags_ok"], 16 * B)

            def first_query(h):
                q_cos(0, 0, h)
                q_sum(0, h)
                q_low(0, h)

            def start(path):
                ctx_stats(0, path, 0)
                mask_bias(0, path)
                dve.wait_ge(s["tab_in"], 16)
                first_query(0)
                for k in range(path.blocks):
                    if k:
                        ctx_stats(0, path, k)
                    ctx_low(0, path, k)
                    k_cos(0, path, k, 1)
                    k_low(0, path, k)
                    if path.blocks == 2:
                        v_low(0, path, k)
                for h in range(NH):
                    split_scaled(raw_o[:, h, :], wo[1][:, h, :], wo[0][:, h, :], t12[:, 0:1], "wo_hi", h + 1, "wo_ok")
                q_cos(0, 0, 1)
                minima(path, 0, 0)
                q_sum(0, 1)
                q_low(0, 1)
                lo(wdn[1][:, :, :], tbank[0][:, :].rearrange("p (k n) -> p k n", k=KC), wdn[0][:, :, :], "dn_w_hi", 1, "dn_w_ok")
                lo(wup[1][:, :], tbank[1][:, :], wup[0][:, :], "up_w_hi", 1, "up_w_ok")
                inverses(0, 0)
                if path.blocks == 1:
                    v_low(0, path, 0)
                first_query(2)
                first_query(3)

            def attention(path, b, cc, first, last):
                c = b * NC + cc
                n = c + 1
                ncc = 1 - cc

                def turned(h):
                    if path.ahead:
                        for kt in range(path.nk):
                            tp_low(path, c, h, kt)

                def minima_ahead(h):
                    if path.ahead:
                        minima(path, c, h)

                def inverses_ahead(h):
                    if path.ahead:
                        inverses(c, h)

                def weighted(h):
                    if not path.ahead:
                        for kt in range(path.nk):
                            tp_low(path, c, h, kt)
                    pv_low(c, h)
                    if not path.ahead and h < NH - 1:
                        minima(path, c, h + 1)
                        inverses(c, h + 1)

                if not first:
                    residual(c - 1, ncc, T - 1, is_start(c - 1))
                minima_ahead(1)
                if not first:
                    ln2_stats(c - 1, T - 1)
                turned(0)
                inverses_ahead(1)
                if not first:
                    ty_lo(c - 1, (0, 1))
                if not last:
                    ln1(b + cc, ncc, 0)
                if not first:
                    ty_lo(c - 1, (2, 3))
                if cc:
                    router_max(b)
                minima_ahead(2)
                weighted(0)
                if not last:
                    ln1(b + cc, ncc, 1)
                turned(1)
                if not last:
                    tx_lo(n, (0, 1))
                inverses_ahead(2)
                if cc:
                    router_gate(b)
                if not last:
                    tx_lo(n, (2, 3))
                if not first:
                    down_low(b + cc, c - 1)
                weighted(1)
                minima_ahead(3)
                if not first:
                    final(c - 1, 0)
                    final(c - 1, 1)
                turned(2)
                inverses_ahead(3)
                if not last:
                    q_cos(n, ncc, 0)
                if not first:
                    final(c - 1, 2)
                    final(c - 1, 3)
                if path.ahead:
                    if not last:
                        q_sum(n, 0)
                    weighted(2)
                    turned(3)
                    if not last:
                        q_low(n, 0)
                        q_cos(n, ncc, 1)
                    weighted(3)
                    if not last:
                        q_sum(n, 1)
                        q_low(n, 1)
                else:
                    for h in (0, 1):
                        if not last:
                            if h:
                                q_cos(n, ncc, 1)
                            q_sum(n, h)
                            q_low(n, h)
                        weighted(2 + h)

            def outputs(path, b, cc, new_keys, first, last):
                c, n = b * NC + cc, b * NC + cc + 1

                def residual_stats(t):
                    residual(c, cc, t, first)
                    ln2_stats(c, t)

                if new_keys:
                    ctx_stats(b + 1, path, 0)
                if not last:
                    q_cos(n, 1 - cc, 2)
                if new_keys:
                    mask_bias(b + 1, path)
                residual_stats(0)
                if not last:
                    q_sum(n, 2)
                    if not new_keys:
                        q_low(n, 2)
                    q_cos(n, 1 - cc, 3)
                if new_keys:
                    ctx_low(b + 1, path, 0)
                    q_low(n, 2)
                if not last:
                    q_sum(n, 3)
                    if not new_keys:
                        minima(path, n, 0)
                    q_low(n, 3)
                if new_keys:
                    residual_stats(1)
                    k_cos(b + 1, path, 0, (n + 1) * NH)
                    k_low(b + 1, path, 0)
                    v_low(b + 1, path, 0)
                    if path.blocks == 2:
                        ctx_stats(b + 1, path, 1)
                        ctx_low(b + 1, path, 1)
                        k_cos(b + 1, path, 1, (n + 1) * NH)
                        k_low(b + 1, path, 1)
                        v_low(b + 1, path, 1)
                    minima(path, n, 0)
                    residual_stats(2)
                else:
                    residual_stats(1)
                if not last:
                    inverses(n, 0)
                if not new_keys:
                    residual_stats(2)
                if last:
                    residual_stats(3)

            prologue()
            pipeline(dve, start, attention, outputs)
            ty_lo(B * NC - 1)
            down_low(B, B * NC - 1)
            for t in range(T):
                final(B * NC - 1, t)

        @block.tensor
        def _(pe):
            def product(dst, a, b, steps):
                last = None
                for i in range(steps):
                    for j, (p, q) in enumerate(((0, 0), (0, 1), (1, 0))):
                        last = pe.matmul(dst, a(p, i), b(q, i), start=(i == 0 and j == 0),
                                         stop=(i == steps - 1 and j == 2), skip_group_check=True)
                return last

            def turn(dst, src, n=P):
                return pe.transpose(dst, src, ident[0:n, 0:n])

            def turn_norm(t, full):
                for k in range(KC):
                    last = turn(tbank[t % 2][:, k * P:(k + 1) * P], norm[:, t, k * P:(k + 1) * P])
                last.then_inc(s[full], 1)

            def tx(n, between=None):
                for t in range(T):
                    if t == 2 and between:
                        between()
                    if t >= 2:
                        pe.wait_ge(s["tx_done"], n * T + t - 1)
                    pe.wait_ge(s["xn_ready"], n * T + t + 1)
                    turn_norm(t, "tx_full")

            def ty(c, between=None, batch=None):
                for t in range(T):
                    if t == 2 and between:
                        between()
                    if t == 2 and batch is not None:
                        router(batch, c)
                    if t < 2:
                        pe.wait_ge(s["fin_done"], c * T + T)
                    else:
                        pe.wait_ge(s["ty_done"], c * T + t - 1)
                    pe.wait_ge(s["y_ready"], c * T + t + 1)
                    turn_norm(t, "ty_full")

            def router(b, c):
                pe.wait_ge(s["ty_done"], c * T + 1)
                product(qbank[:, 0:E], lambda p, k: xT[p][:, k, 0:1].to_broadcast([P, P]),
                        lambda q, k: wrt[q][:, k, :], KC).then_inc(s["rt_full"], 1)

            def down(c, batch=None):
                pe.wait_ge(s["ty_done"], (c + 1) * T)
                if batch is not None:
                    pe.wait_ge(s["rt_read"], batch + 1)
                product(qbank[:, :], lambda p, k: wdn[p][:, k, :], lambda q, k: xT[q][:, k, :], KC)\
                    .then_inc(s["dn_full"], 1)

            def up(c, tiles=range(T)):
                for t in tiles:
                    if t < 2:
                        pe.wait_ge(s["dn_done"], c + 1)
                    else:
                        pe.wait_ge(s["fin_done"], T + c * T + t - 1)
                    product(tbank[t % 2][:, :], lambda p, _: dT[p][:, t * P:(t + 1) * P],
                            lambda q, _: wup[q][:, :], 1).then_inc(s["up_full"], 1)

            def q_proj(n, h):
                pe.wait_ge(s["tx_done"], (n + 1) * T)
                if is_start(n):
                    if h == 3:
                        pe.wait_ge(s["q_swapped"], 2)
                        pe.wait_ge(s["q_cos_ok"], 1)
                elif h < 2:
                    pe.wait_ge(s["q_swapped"], (n * NH + h) * 2)
                    pe.wait_ge(s["q_cos_ok"], n * NH + h)
                else:
                    pe.wait_ge(s["lg_min"], n * 16)
                product(rotation(n, h)[0], lambda p, k: wq[p][:, k, h * HD:(h + 1) * HD],
                        lambda q, k: xT[q][:, k, :], KC).then_inc(s["q_full"], 1)

            def first_logits(path, n):
                if not is_start(n):
                    pe.wait_ge(s["q_swapped"], (n + 1) * NH * 2)
                    pe.wait_ge(s["q_cos_ok"], (n + 1) * NH)
                    pe.wait_ge(s["q_done"], n * NH + 3)
                logits(path, n, 0)

            def logits(path, c, h):
                w = path.nk * P
                pe.wait_ge(s["q_done"], c * NH + h + 1)
                for qt in range(T):
                    i = c * 16 + h * T + qt
                    if h or qt:
                        if path.ahead and h and qt % 2 == 0:
                            pe.wait_ge(s["lg_min"], i - T + 2)
                        elif not path.ahead:
                            pe.wait_ge(s["lg_min"], i)
                    for half in range(max(1, w // 512)):
                        n = min(w, 512)
                        dst = lg[:, qt * w:(qt + 1) * w] if path.ahead else lg[:, half * n:(half + 1) * n]
                        last = product(dst, lambda p, _: qT[p][:, h, qt * P:(qt + 1) * P],
                                       lambda q, _: kT[q][:, half * n:(half + 1) * n], 1)
                    last.then_inc(s["lg_full"], 1)

            def turn_probs(path, c, h, kt, first):
                w = path.nk * P
                o = (h % 2) * 1024 if path.ahead else 0
                at = (c * NH + h) * 8
                if path.ahead and h:
                    pe.wait_ge(s["tp_done"], at - 4 + 4 * kt)
                elif not path.ahead and kt >= 2:
                    pe.wait_ge(s["tp_done"], at + kt - 1)
                elif not path.ahead and h:
                    pe.wait_ge(s["tp_done"], at)
                elif not first:
                    pe.wait_ge(s["res_done"], c * T - 1 + kt)
                else:
                    pe.wait_ge(s["q_swapped"], 3 * 2)
                    pe.wait_ge(s["q_cos_ok"], 3)
                for qt in range(T):
                    pe.wait_ge(s["nrm_done"], c * 16 + h * T + qt + 1)
                    last = turn(tp[kt % 2][:, qt * P:(qt + 1) * P], probs[:, o + qt * w + kt * P:o + qt * w + (kt + 1) * P])
                last.then_inc(s["tp_full"], path.unit)

            def weigh_values(path, c, h, kt):
                slot = (h % 2) * 2 + kt if path.ahead else kt % 4
                pe.wait_ge(s["tp_done"], (c * NH + h) * 8 + (kt + 1) * path.unit)
                if kt == 0:
                    if not is_start(c * NH + h):
                        pe.wait_ge(s["pv_done"], c * NH + h)
                for j, (p, q) in enumerate(((0, 0), (0, 1), (1, 0))):
                    last = pe.matmul(enc[:, :], v[p][:, kt, :], pT[q][:, slot, :], start=(kt == 0 and j == 0),
                                     stop=(kt == path.nk - 1 and j == 2), skip_group_check=True)
                if kt == path.nk - 1:
                    last.then_inc(s["pv_full"], 1)

            def attention(path, b, cc, first, last):
                c = b * NC + cc
                n = c + 1

                def weigh(h):
                    if path.ahead:
                        for kt in range(path.nk):
                            weigh_values(path, c, h, kt)

                def others(h):
                    if h == 0:
                        if first:
                            weigh(0)
                        else:
                            ty(c - 1, lambda: weigh(0), b if cc else None)
                    if h == 1:
                        if not first:
                            down(c - 1, b if cc else None)
                        if last:
                            weigh(1)
                        else:
                            tx(n, lambda: weigh(1))
                    if h == 2:
                        if not first:
                            if not last:
                                pe.wait_ge(s["tx_done"], (n + 1) * T)
                            up(c - 1, (0, 1))
                        if not last:
                            q_proj(n, 0)
                        if not first:
                            up(c - 1, (2, 3))
                        weigh(2)
                    if h == 3:
                        if not last:
                            q_proj(n, 1)
                        weigh(3)

                for h in range(NH):
                    if path.ahead:
                        if h < NH - 1:
                            logits(path, c, h + 1)
                        for kt in range(path.nk):
                            turn_probs(path, c, h, kt, first)
                        others(h)
                    else:
                        others(h)
                        turn_probs(path, c, h, 0, first)
                        for kt in range(1, path.nk):
                            turn_probs(path, c, h, kt, first)
                            weigh_values(path, c, h, kt - 1)
                        weigh_values(path, c, h, path.nk - 1)
                        if h < NH - 1:
                            logits(path, c, h + 1)

            def out_proj(c, t):
                if t < 2:
                    pe.wait_ge(s["wo_ok"], NH)
                    pe.wait_ge(s["tp_done"], (c + 1) * NH * 8)
                    pe.wait_ge(s["pv_done"], (c + 1) * NH)
                else:
                    pe.wait_ge(s["res_done"], c * T + t - 1)
                product(tp[t % 2][:, :], lambda p, h: eT[p][:, h, t * P:(t + 1) * P],
                        lambda q, h: wo[q][:, h, :], NH).then_inc(s["op_full"], 1)

            def turn_ctx(b, path, k):
                for j in range(path.bt):
                    kt = k * path.bt + j
                    pe.wait_ge(s["ctx_normed"], b * 8 + (kt + 1) * path.unit)
                    if kt >= 2:
                        pe.wait_ge(s["tc_done"], b * 8 + (kt - 1) * path.unit)
                    for kk in range(KC):
                        last = turn(tbank[kt % 2][:, kk * P:(kk + 1) * P], ctx_raw[:, j, kk * P:(kk + 1) * P])
                    last.then_inc(s["tc_full"], path.unit)

            def k_proj(b, path, k, rotations):
                w = 2 // path.blocks
                n = path.bt * P
                pe.wait_ge(s["tc_done"], b * 8 + (k + 1) * path.bt * path.unit)
                if k:
                    pe.wait_ge(s["k_cos"], b * 2 + k)
                elif not is_start(b):
                    pe.wait_ge(s["q_cos_ok"], rotations)
                product(keys_bank(b)[:, 0:n], lambda p, kk: wkv[p][:, 0, kk, :], lambda q, kk: ctx_part(q, path)[:, kk, :], KC)\
                    .then_inc(s["k_full"], w)

            def v_proj(b, path, k):
                w = 2 // path.blocks
                if k:
                    pe.wait_ge(s["v_done"], b * 2 + k)
                for j in range(path.bt):
                    last = product(enc[:, j * P:(j + 1) * P], lambda p, kk: ctx_part(p, path)[:, kk, j * P:(j + 1) * P],
                                   lambda q, kk: wkv[q][:, 1, kk, :], KC)
                last.then_inc(s["v_full"], w)

            def keys_there(b):
                pe.wait_ge(s["k_done"], (b + 1) * 2)
                pe.wait_ge(s["v_done"], (b + 1) * 2)
                pe.wait_ge(s["bias_ok"], b + 1)

            def outputs(path, b, cc, new_keys, first, last):
                c, n = b * NC + cc, b * NC + cc + 1
                if not last:
                    q_proj(n, 2)
                out_proj(c, 0)
                if not last:
                    q_proj(n, 3)
                if new_keys:
                    pe.wait_ge(s["fin_done"], n * T)
                    turn_ctx(b + 1, path, 0)
                out_proj(c, 1)
                if new_keys:
                    k_proj(b + 1, path, 0, n * NH + 2)
                    v_proj(b + 1, path, 0)
                    if path.blocks == 2:
                        turn_ctx(b + 1, path, 1)
                        k_proj(b + 1, path, 1, None)
                        v_proj(b + 1, path, 1)
                    out_proj(c, 2)
                    keys_there(b + 1)
                    first_logits(path, n)
                else:
                    if not last:
                        first_logits(path, n)
                    out_proj(c, 2)
                out_proj(c, 3)

            pe.wait_ge(s["ident_ok"], 1)
            pe.wait_ge(s["raw_aux_in"], 32)
            for k in range(KC):
                pe.transpose(tbank[0][:, k * E:(k + 1) * E], raw_router[:, k * P:(k + 1) * P], ident[0:E, 0:E])
            pe.transpose(tbank[1][:, 0:KC], raw_rms, ident[0:KC, 0:KC]).then_inc(s["aux_full"], 1)
            pe.wait_ge(s["rt_ok"], 2)
            pe.wait_ge(s["rms_ok"], 1)
            tx(0)
            pe.wait_ge(s["wq_ok"], KC)
            q_proj(0, 0)
            pe.wait_ge(s["wkv_ok"], KC)
            pe.wait_ge(s["flags_ok"], 16 * B)

            def start(path):
                for k in range(path.blocks):
                    if k:
                        pe.wait_ge(s["k_cos"], 1)
                        pe.wait_ge(s["k_swapped"], 2)
                    turn_ctx(0, path, k)
                    k_proj(0, path, k, None)
                    if path.blocks == 2:
                        v_proj(0, path, k)
                q_proj(0, 1)
                pe.wait_ge(s["k_done"], 2)
                pe.wait_ge(s["bias_ok"], 1)
                first_logits(path, 0)
                pe.wait_ge(s["raw_dn_in"], 16)
                pe.wait_ge(s["raw_up_in"], 16 * KC)
                for k in range(KC):
                    last = turn(tbank[0][:, k * P:(k + 1) * P], raw_dn[:, k * P:(k + 1) * P])
                last.then_inc(s["dn_w_full"], 1)
                for k in range(KC):
                    last = turn(tbank[1][:, k * P:(k + 1) * P], raw_up[:, k, :])
                last.then_inc(s["up_w_full"], 1)
                if path.blocks == 1:
                    v_proj(0, path, 0)
                q_proj(0, 2)
                q_proj(0, 3)
                pe.wait_ge(s["v_done"], 2)
                pe.wait_ge(s["dn_w_ok"], 1)
                pe.wait_ge(s["up_w_ok"], 1)

            pipeline(pe, start, attention, outputs)
            ty(B * NC - 1)
            down(B * NC - 1)
            up(B * NC - 1)


_INS = ["x", "ctx_1024", "mask_BxS2_bk0", "g_xattn", "g_ffn", "L0_xattn_rms_scale", "L0_xattn_q_w",
        "L0_xattn_kv_w", "L0_xattn_out_w", "L0_ffn_router_w", "L0_ffn_lora_down", "L0_ffn_lora_up"]
_OUT = ((B, S, D), "float32")


def kernel(**inputs):
    import numpy as _np
    import concourse.bacc as _bacc
    from concourse import mybir as _mybir
    from concourse.bass_utils import run_bass_kernel_spmd as _run

    nc = _bacc.Bacc("TRN2", target_bir_lowering=False, num_devices=1)
    arrays, args = {}, []

    def give(name, a):
        arrays[name] = a
        args.append(nc.dram_tensor(name, a.shape, _mybir.dt.from_np(a.dtype), kind="ExternalInput").ap())

    for name in _INS:
        a = _np.ascontiguousarray(inputs[name])
        give(f"in_{name}_dram", a)
    for name, a in zip(("q_table", "k_table"), rope_tables()):
        give(f"in_{name}_dram", a)
    shape, dtype = _OUT
    args.append(nc.dram_tensor("out_dram", shape, _mybir.dt.from_np(_np.dtype(dtype)), kind="ExternalOutput").ap())
    gated_block(nc, *args)
    r = _run(nc, [arrays], core_ids=[0])
    return r.results[0]["out_dram"]
```
